# Optimizing a Trainium2 kernel written in Bass

```python
import numpy as np
import jax
import jax.numpy as jnp

def _softmax(x, axis=-1):
    return jax.nn.softmax(x, axis=axis)

def _gelu(x):
    return jax.nn.gelu(x, approximate=True)

def _silu(x):
    return jax.nn.silu(x)

def _sigmoid(x):
    return jax.nn.sigmoid(x)

def _layernorm(x, axis=-1, eps=1e-05):
    m = jnp.mean(x, axis=axis, keepdims=True)
    v = jnp.var(x, axis=axis, keepdims=True)
    return (x - m) / jnp.sqrt(v + eps)

def _scatter_add(tgt, idx, src, axis=0):
    return tgt.at[idx].add(src)

def _segment_sum(src, seg, n):
    return jax.ops.segment_sum(src, seg, n)
kernel_name = 'mk_seq_postln_d2_jaxref_r8_da7a6e'

def setup_inputs(seed: int=0):
    np.random.seed(seed)
    _w = jnp.asarray

    def _L0_attn_setup():
        import jax, jax.numpy as jnp
        import numpy as np

        def _layernorm(x, g, b, eps=1e-05):
            m = x.mean(-1, keepdims=True)
            v = x.var(-1, keepdims=True)
            return (x - m) * jax.lax.rsqrt(v + eps) * g + b

        def _mamba(x, in_w, conv_w, conv_b, xproj_w, dt_w, dt_b, A_log, D, out_w):
            Bsz, L, _ = x.shape
            d_state = A_log.shape[1]
            dt_rank = dt_w.shape[1]
            d_conv = conv_w.shape[1]
            u, z = jnp.split(x @ in_w.T, 2, axis=-1)
            u_pad = jnp.pad(u, ((0, 0), (d_conv - 1, 0), (0, 0)))
            u = sum((u_pad[:, k:k + L, :] * conv_w[:, k] for k in range(d_conv))) + conv_b
            u = jax.nn.silu(u)
            dbc = u @ xproj_w.T
            dt = jax.nn.softplus(dbc[..., :dt_rank] @ dt_w.T + dt_b)
            Bm = dbc[..., dt_rank:dt_rank + d_state]
            Cm = dbc[..., dt_rank + d_state:]
            A = -jnp.exp(A_log)
            dA = jnp.exp(dt[..., None] * A)
            dBu = (dt * u)[..., None] * Bm[:, :, None, :]

            def step(h, inp):
                dA_t, dBu_t, C_t = inp
                h = dA_t * h + dBu_t
                return (h, jnp.einsum('bdn,bn->bd', h, C_t))
            h0 = jnp.zeros((Bsz, u.shape[-1], d_state), x.dtype)
            _, ys = jax.lax.scan(step, h0, (dA.swapaxes(0, 1), dBu.swapaxes(0, 1), Cm.swapaxes(0, 1)))
            y = ys.swapaxes(0, 1) + u * D
            return y * jax.nn.silu(z) @ out_w.T
        key = jax.random.key(seed)
        ks = jax.random.split(key, 3)
        d_model, d_state, d_conv, d_inner, dt_rank = (128, 16, 4, 256, 64)
        B, L = (2, 128)

        def mk(k, shape, s=0.02):
            return jax.random.normal(k, shape, jnp.float32) * s

        def mamba_params(kb):
            k = jax.random.split(kb, 6)
            return {'in_w': mk(k[0], (2 * d_inner, d_model)), 'conv_w': mk(k[1], (d_inner, d_conv), 0.2), 'conv_b': jnp.zeros((d_inner,), jnp.float32), 'xproj_w': mk(k[2], (dt_rank + 2 * d_state, d_inner)), 'dt_w': mk(k[3], (d_inner, dt_rank), 0.1), 'dt_b': jnp.full((d_inner,), -4.0, jnp.float32) + mk(k[4], (d_inner,), 0.5), 'Alog': jnp.log(jnp.tile(jnp.arange(1, d_state + 1, dtype=jnp.float32), (d_inner, 1))), 'D': jnp.ones((d_inner,), jnp.float32), 'out_w': mk(k[5], (d_model, d_inner))}
        pf = mamba_params(ks[0])
        pb = mamba_params(ks[1])
        inp = {'x': jax.random.normal(ks[2], (B, L, d_model), jnp.float32), 'ln_g': jnp.ones((d_model,), jnp.float32), 'ln_b': jnp.zeros((d_model,), jnp.float32)}
        for pre, p in (('f_', pf), ('b_', pb)):
            for nm, v in p.items():
                inp[pre + nm] = v
        return inp
    _L0_attn_in = _L0_attn_setup()

    def _L0_ffn_setup():
        import jax, jax.numpy as jnp
        import numpy as np
        ALPHA = 2.0
        TOP_K = 2
        key = jax.random.key(seed)
        ks = jax.random.split(key, 8)
        B, S, D, H, E = (2, 256, 128, 512, 8)
        Er = E - 1
        s_in = 1.0 / np.sqrt(D)
        s_hid = 1.0 / np.sqrt(H)
        return {'x': jax.random.normal(ks[0], (B, S, D), dtype=jnp.float32), 'router_w': jax.random.normal(ks[1], (D, E), dtype=jnp.float32) * s_in, 'up_w': jax.random.normal(ks[2], (Er, D, H), dtype=jnp.float32) * s_in, 'gate_w': jax.random.normal(ks[3], (Er, D, H), dtype=jnp.float32) * s_in, 'down_w': jax.random.normal(ks[4], (Er, H, D), dtype=jnp.float32) * s_hid * 0.1, 'shared_up_w': jax.random.normal(ks[5], (D, H), dtype=jnp.float32) * s_in, 'shared_gate_w': jax.random.normal(ks[6], (D, H), dtype=jnp.float32) * s_in, 'shared_down_w': jax.random.normal(ks[7], (H, D), dtype=jnp.float32) * s_hid * 0.1}
    _L0_ffn_in = _L0_ffn_setup()

    def _L1_attn_setup():
        import jax, jax.numpy as jnp
        import numpy as np
        NUM_HEADS = 8
        SCALE_BASE = 512.0
        GN_EPS = 1e-05

        def rotate_every_two(x):
            x1 = x[..., ::2]
            x2 = x[..., 1::2]
            return jnp.stack([-x2, x1], axis=-1).reshape(x.shape)

        def xpos_apply(x, downscale):
            L, D = (x.shape[1], x.shape[2])
            half = D // 2
            scale_vec = (jnp.arange(0, D, 2, dtype=jnp.float32) + 0.4 * D) / (1.4 * D)
            pos = jnp.arange(L, dtype=jnp.float32)
            scale = scale_vec[None, :] ** (pos[:, None] / SCALE_BASE)
            inv_freq = 1.0 / 10000.0 ** (jnp.arange(half, dtype=jnp.float32) / half)
            sinusoid = pos[:, None] * inv_freq[None, :]
            sin, cos = (jnp.sin(sinusoid), jnp.cos(sinusoid))
            if downscale:
                scale = 1.0 / scale
            sin_s = jnp.repeat(sin * scale, 2, axis=-1)
            cos_s = jnp.repeat(cos * scale, 2, axis=-1)
            return x * cos_s + rotate_every_two(x) * sin_s

        def decay_mask_fn(T, num_heads):
            s, e = (np.log(1.0 / 32.0), np.log(1.0 / 512.0))
            gamma = 1.0 - jnp.exp(jnp.linspace(s, e, num_heads).astype(jnp.float32))
            log_decay = jnp.log(gamma)
            idx = jnp.arange(T)
            expo = (idx[:, None] - idx[None, :]).astype(jnp.float32)
            tri = idx[:, None] >= idx[None, :]
            expo_safe = jnp.where(tri, expo, 0.0)
            mask = jnp.exp(log_decay[:, None, None] * expo_safe) * tri
            scale = jnp.sqrt(mask.sum(axis=-1, keepdims=True))
            return mask / scale

        def _reference_tuple_inner(hidden_states, w_qkv, b_qkv, w_g, b_g, w_p, b_p):
            B, T, E = hidden_states.shape
            H = NUM_HEADS
            V = 2 * E
            dk, dv = (E // H, V // H)
            qkv = hidden_states @ w_qkv + b_qkv
            q, k, v = (qkv[..., :E], qkv[..., E:2 * E], qkv[..., 2 * E:])
            q = xpos_apply(q, downscale=False)
            k = xpos_apply(k, downscale=True)
            q = q.reshape(B, T, H, dk).transpose(0, 2, 1, 3)
            k = k.reshape(B, T, H, dk).transpose(0, 2, 1, 3)
            v = v.reshape(B, T, H, dv).transpose(0, 2, 1, 3)
            mask = decay_mask_fn(T, H)
            retention = jnp.einsum('bhid,bhjd->bhij', q, k) * dk ** (-0.5)
            retention = retention * mask[None]
            out = jnp.einsum('bhij,bhjv->bhiv', retention, v)
            curr_kv = jnp.einsum('hj,bhjk,bhjv->bhkv', mask[:, -1, :], k, v)
            retention_out = out.transpose(0, 2, 1, 3).reshape(B, T, V)
            g = retention_out.reshape(B * T, H, dv)
            mu = g.mean(axis=-1, keepdims=True)
            var = ((g - mu) ** 2).mean(axis=-1, keepdims=True)
            normed = ((g - mu) / jnp.sqrt(var + GN_EPS)).reshape(B, T, V)
            gated = jax.nn.silu(hidden_states @ w_g + b_g) * normed
            proj = gated @ w_p + b_p
            return (proj, curr_kv)
        key = jax.random.key(seed)
        ks = jax.random.split(key, 4)
        B, T, E = (2, 256, 128)
        V = 2 * E
        return {'hidden_states': jax.random.normal(ks[0], (B, T, E), dtype=jnp.float32), 'w_qkv': jax.random.normal(ks[1], (E, 2 * E + V), dtype=jnp.float32) * 0.02, 'b_qkv': jnp.zeros((2 * E + V,), dtype=jnp.float32), 'w_g': jax.random.normal(ks[2], (E, V), dtype=jnp.float32) * 0.02, 'b_g': jnp.zeros((V,), dtype=jnp.float32), 'w_p': jax.random.normal(ks[3], (V, E), dtype=jnp.float32) * 0.02, 'b_p': jnp.zeros((E,), dtype=jnp.float32)}
    _L1_attn_in = _L1_attn_setup()

    def _L1_ffn_setup():
        import jax, jax.numpy as jnp
        import numpy as np
        D_MODEL, D_FF, N_EXP = (128, 512, 8)
        key = jax.random.key(seed)
        ks = jax.random.split(key, 8)
        s = lambda fan_in: 1.0 / np.sqrt(fan_in)
        x = jax.random.normal(ks[0], (4, 256, D_MODEL), dtype=jnp.float32)
        Wr = jax.random.uniform(ks[1], (N_EXP, D_MODEL), jnp.float32, -s(D_MODEL), s(D_MODEL))
        br = jax.random.uniform(ks[2], (N_EXP,), jnp.float32, -s(D_MODEL), s(D_MODEL))
        W1 = jax.random.uniform(ks[3], (N_EXP, D_FF, D_MODEL), jnp.float32, -s(D_MODEL), s(D_MODEL))
        b1 = jax.random.uniform(ks[4], (N_EXP, D_FF), jnp.float32, -s(D_MODEL), s(D_MODEL))
        W2 = jax.random.uniform(ks[5], (N_EXP, D_MODEL, D_FF), jnp.float32, -s(D_FF), s(D_FF))
        b2 = jax.random.uniform(ks[6], (N_EXP, D_MODEL), jnp.float32, -s(D_FF), s(D_FF))
        return {'x': x, 'Wr': Wr, 'br': br, 'W1': W1, 'b1': b1, 'W2': W2, 'b2': b2}
    _L1_ffn_in = _L1_ffn_setup()
    _d = {'L0_attn_x': _L0_attn_in['x'], 'L0_attn_ln_g': _L0_attn_in['ln_g'], 'L0_attn_ln_b': _L0_attn_in['ln_b'], 'L0_attn_f_in_w': _L0_attn_in['f_in_w'], 'L0_attn_f_conv_w': _L0_attn_in['f_conv_w'], 'L0_attn_f_conv_b': _L0_attn_in['f_conv_b'], 'L0_attn_f_xproj_w': _L0_attn_in['f_xproj_w'], 'L0_attn_f_dt_w': _L0_attn_in['f_dt_w'], 'L0_attn_f_dt_b': _L0_attn_in['f_dt_b'], 'L0_attn_f_Alog': _L0_attn_in['f_Alog'], 'L0_attn_f_D': _L0_attn_in['f_D'], 'L0_attn_f_out_w': _L0_attn_in['f_out_w'], 'L0_attn_b_in_w': _L0_attn_in['b_in_w'], 'L0_attn_b_conv_w': _L0_attn_in['b_conv_w'], 'L0_attn_b_conv_b': _L0_attn_in['b_conv_b'], 'L0_attn_b_xproj_w': _L0_attn_in['b_xproj_w'], 'L0_attn_b_dt_w': _L0_attn_in['b_dt_w'], 'L0_attn_b_dt_b': _L0_attn_in['b_dt_b'], 'L0_attn_b_Alog': _L0_attn_in['b_Alog'], 'L0_attn_b_D': _L0_attn_in['b_D'], 'L0_attn_b_out_w': _L0_attn_in['b_out_w'], 'L0_ffn_router_w': _L0_ffn_in['router_w'], 'L0_ffn_up_w': _L0_ffn_in['up_w'], 'L0_ffn_gate_w': _L0_ffn_in['gate_w'], 'L0_ffn_down_w': _L0_ffn_in['down_w'], 'L0_ffn_shared_up_w': _L0_ffn_in['shared_up_w'], 'L0_ffn_shared_gate_w': _L0_ffn_in['shared_gate_w'], 'L0_ffn_shared_down_w': _L0_ffn_in['shared_down_w'], 'L1_attn_w_qkv': _L1_attn_in['w_qkv'], 'L1_attn_b_qkv': _L1_attn_in['b_qkv'], 'L1_attn_w_g': _L1_attn_in['w_g'], 'L1_attn_b_g': _L1_attn_in['b_g'], 'L1_attn_w_p': _L1_attn_in['w_p'], 'L1_attn_b_p': _L1_attn_in['b_p'], 'L1_ffn_Wr': _L1_ffn_in['Wr'], 'L1_ffn_br': _L1_ffn_in['br'], 'L1_ffn_W1': _L1_ffn_in['W1'], 'L1_ffn_b1': _L1_ffn_in['b1'], 'L1_ffn_W2': _L1_ffn_in['W2'], 'L1_ffn_b2': _L1_ffn_in['b2']}
    _x0 = _d['L0_attn_x']
    _d['L0_attn_x'] = jax.random.normal(jax.random.fold_in(jax.random.key(seed), 1), (2, 2048, 128), dtype=_x0.dtype)
    del _x0
    return _d

def reference(L0_attn_x, L0_attn_ln_g, L0_attn_ln_b, L0_attn_f_in_w, L0_attn_f_conv_w, L0_attn_f_conv_b, L0_attn_f_xproj_w, L0_attn_f_dt_w, L0_attn_f_dt_b, L0_attn_f_Alog, L0_attn_f_D, L0_attn_f_out_w, L0_attn_b_in_w, L0_attn_b_conv_w, L0_attn_b_conv_b, L0_attn_b_xproj_w, L0_attn_b_dt_w, L0_attn_b_dt_b, L0_attn_b_Alog, L0_attn_b_D, L0_attn_b_out_w, L0_ffn_router_w, L0_ffn_up_w, L0_ffn_gate_w, L0_ffn_down_w, L0_ffn_shared_up_w, L0_ffn_shared_gate_w, L0_ffn_shared_down_w, L1_attn_w_qkv, L1_attn_b_qkv, L1_attn_w_g, L1_attn_b_g, L1_attn_w_p, L1_attn_b_p, L1_ffn_Wr, L1_ffn_br, L1_ffn_W1, L1_ffn_b1, L1_ffn_W2, L1_ffn_b2):

    def _L0_attn_ref(x, ln_g, ln_b, f_in_w, f_conv_w, f_conv_b, f_xproj_w, f_dt_w, f_dt_b, f_Alog, f_D, f_out_w, b_in_w, b_conv_w, b_conv_b, b_xproj_w, b_dt_w, b_dt_b, b_Alog, b_D, b_out_w):
        import jax, jax.numpy as jnp
        import numpy as np

        def _layernorm(x, g, b, eps=1e-05):
            m = x.mean(-1, keepdims=True)
            v = x.var(-1, keepdims=True)
            return (x - m) * jax.lax.rsqrt(v + eps) * g + b

        def _mamba(x, in_w, conv_w, conv_b, xproj_w, dt_w, dt_b, A_log, D, out_w):
            Bsz, L, _ = x.shape
            d_state = A_log.shape[1]
            dt_rank = dt_w.shape[1]
            d_conv = conv_w.shape[1]
            u, z = jnp.split(x @ in_w.T, 2, axis=-1)
            u_pad = jnp.pad(u, ((0, 0), (d_conv - 1, 0), (0, 0)))
            u = sum((u_pad[:, k:k + L, :] * conv_w[:, k] for k in range(d_conv))) + conv_b
            u = jax.nn.silu(u)
            dbc = u @ xproj_w.T
            dt = jax.nn.softplus(dbc[..., :dt_rank] @ dt_w.T + dt_b)
            Bm = dbc[..., dt_rank:dt_rank + d_state]
            Cm = dbc[..., dt_rank + d_state:]
            A = -jnp.exp(A_log)
            dA = jnp.exp(dt[..., None] * A)
            dBu = (dt * u)[..., None] * Bm[:, :, None, :]

            def step(h, inp):
                dA_t, dBu_t, C_t = inp
                h = dA_t * h + dBu_t
                return (h, jnp.einsum('bdn,bn->bd', h, C_t))
            h0 = jnp.zeros((Bsz, u.shape[-1], d_state), x.dtype)
            _, ys = jax.lax.scan(step, h0, (dA.swapaxes(0, 1), dBu.swapaxes(0, 1), Cm.swapaxes(0, 1)))
            y = ys.swapaxes(0, 1) + u * D
            return y * jax.nn.silu(z) @ out_w.T
        res = x
        xn = _layernorm(x, ln_g, ln_b)
        out_f = _mamba(xn, f_in_w, f_conv_w, f_conv_b, f_xproj_w, f_dt_w, f_dt_b, f_Alog, f_D, f_out_w)
        out_b = _mamba(xn[:, ::-1, :], b_in_w, b_conv_w, b_conv_b, b_xproj_w, b_dt_w, b_dt_b, b_Alog, b_D, b_out_w)[:, ::-1, :]
        return res + out_f + out_b

    def _L0_ffn_ref(x, router_w, up_w, gate_w, down_w, shared_up_w, shared_gate_w, shared_down_w):
        import jax, jax.numpy as jnp
        import numpy as np
        ALPHA = 2.0
        TOP_K = 2
        logits = jnp.einsum('bsd,de->bse', x, router_w)
        probs = jax.nn.softmax(logits, axis=-1)
        topk_vals, topk_idx = jax.lax.top_k(probs, TOP_K)
        top1_val = topk_vals[..., 0]
        top1_idx = topk_idx[..., 0]
        hid = jnp.einsum('bsd,edh->ebsh', x, up_w) * jax.nn.silu(jnp.einsum('bsd,edh->ebsh', x, gate_w))
        Er = up_w.shape[0]
        mask = (top1_idx[None, :, :] == jnp.arange(Er)[:, None, None]).astype(x.dtype)
        routed = jnp.einsum('ebsh,ehd,ebs->bsd', hid, down_w, mask)
        shid = jnp.einsum('bsd,dh->bsh', x, shared_up_w) * jax.nn.silu(jnp.einsum('bsd,dh->bsh', x, shared_gate_w))
        shared = jnp.einsum('bsh,hd->bsd', shid, shared_down_w)
        return ALPHA * top1_val[..., None] * routed + shared

    def _L1_attn_ref(hidden_states, w_qkv, b_qkv, w_g, b_g, w_p, b_p):
        import jax, jax.numpy as jnp
        import numpy as np
        NUM_HEADS = 8
        SCALE_BASE = 512.0
        GN_EPS = 1e-05

        def rotate_every_two(x):
            x1 = x[..., ::2]
            x2 = x[..., 1::2]
            return jnp.stack([-x2, x1], axis=-1).reshape(x.shape)

        def xpos_apply(x, downscale):
            L, D = (x.shape[1], x.shape[2])
            half = D // 2
            scale_vec = (jnp.arange(0, D, 2, dtype=jnp.float32) + 0.4 * D) / (1.4 * D)
            pos = jnp.arange(L, dtype=jnp.float32)
            scale = scale_vec[None, :] ** (pos[:, None] / SCALE_BASE)
            inv_freq = 1.0 / 10000.0 ** (jnp.arange(half, dtype=jnp.float32) / half)
            sinusoid = pos[:, None] * inv_freq[None, :]
            sin, cos = (jnp.sin(sinusoid), jnp.cos(sinusoid))
            if downscale:
                scale = 1.0 / scale
            sin_s = jnp.repeat(sin * scale, 2, axis=-1)
            cos_s = jnp.repeat(cos * scale, 2, axis=-1)
            return x * cos_s + rotate_every_two(x) * sin_s

        def decay_mask_fn(T, num_heads):
            s, e = (np.log(1.0 / 32.0), np.log(1.0 / 512.0))
            gamma = 1.0 - jnp.exp(jnp.linspace(s, e, num_heads).astype(jnp.float32))
            log_decay = jnp.log(gamma)
            idx = jnp.arange(T)
            expo = (idx[:, None] - idx[None, :]).astype(jnp.float32)
            tri = idx[:, None] >= idx[None, :]
            expo_safe = jnp.where(tri, expo, 0.0)
            mask = jnp.exp(log_decay[:, None, None] * expo_safe) * tri
            scale = jnp.sqrt(mask.sum(axis=-1, keepdims=True))
            return mask / scale

        def _reference_tuple_inner(hidden_states, w_qkv, b_qkv, w_g, b_g, w_p, b_p):
            B, T, E = hidden_states.shape
            H = NUM_HEADS
            V = 2 * E
            dk, dv = (E // H, V // H)
            qkv = hidden_states @ w_qkv + b_qkv
            q, k, v = (qkv[..., :E], qkv[..., E:2 * E], qkv[..., 2 * E:])
            q = xpos_apply(q, downscale=False)
            k = xpos_apply(k, downscale=True)
            q = q.reshape(B, T, H, dk).transpose(0, 2, 1, 3)
            k = k.reshape(B, T, H, dk).transpose(0, 2, 1, 3)
            v = v.reshape(B, T, H, dv).transpose(0, 2, 1, 3)
            mask = decay_mask_fn(T, H)
            retention = jnp.einsum('bhid,bhjd->bhij', q, k) * dk ** (-0.5)
            retention = retention * mask[None]
            out = jnp.einsum('bhij,bhjv->bhiv', retention, v)
            curr_kv = jnp.einsum('hj,bhjk,bhjv->bhkv', mask[:, -1, :], k, v)
            retention_out = out.transpose(0, 2, 1, 3).reshape(B, T, V)
            g = retention_out.reshape(B * T, H, dv)
            mu = g.mean(axis=-1, keepdims=True)
            var = ((g - mu) ** 2).mean(axis=-1, keepdims=True)
            normed = ((g - mu) / jnp.sqrt(var + GN_EPS)).reshape(B, T, V)
            gated = jax.nn.silu(hidden_states @ w_g + b_g) * normed
            proj = gated @ w_p + b_p
            return (proj, curr_kv)
        return _reference_tuple_inner(hidden_states, w_qkv, b_qkv, w_g, b_g, w_p, b_p)[0]

    def _L1_ffn_ref(x, Wr, br, W1, b1, W2, b2):
        import jax, jax.numpy as jnp
        import numpy as np
        D_MODEL, D_FF, N_EXP = (128, 512, 8)
        B, S, D = x.shape
        xf = x.reshape(-1, D)
        logits = xf @ Wr.T + br
        expert_idx = jnp.argmax(logits, axis=-1)
        h = jax.nn.relu(jnp.einsum('td,efd->etf', xf, W1) + b1[:, None, :])
        y = jnp.einsum('etf,edf->etd', h, W2) + b2[:, None, :]
        out = y[expert_idx, jnp.arange(xf.shape[0])]
        return out.reshape(B, S, D)
    x = L0_attn_x
    x = _layernorm(x + _L0_attn_ref(x, L0_attn_ln_g, L0_attn_ln_b, L0_attn_f_in_w, L0_attn_f_conv_w, L0_attn_f_conv_b, L0_attn_f_xproj_w, L0_attn_f_dt_w, L0_attn_f_dt_b, L0_attn_f_Alog, L0_attn_f_D, L0_attn_f_out_w, L0_attn_b_in_w, L0_attn_b_conv_w, L0_attn_b_conv_b, L0_attn_b_xproj_w, L0_attn_b_dt_w, L0_attn_b_dt_b, L0_attn_b_Alog, L0_attn_b_D, L0_attn_b_out_w), axis=-1)
    x = _layernorm(x + _L0_ffn_ref(x, L0_ffn_router_w, L0_ffn_up_w, L0_ffn_gate_w, L0_ffn_down_w, L0_ffn_shared_up_w, L0_ffn_shared_gate_w, L0_ffn_shared_down_w), axis=-1)
    x = _layernorm(x + _L1_attn_ref(x, L1_attn_w_qkv, L1_attn_b_qkv, L1_attn_w_g, L1_attn_b_g, L1_attn_w_p, L1_attn_b_p), axis=-1)
    x = _layernorm(x + _L1_ffn_ref(x, L1_ffn_Wr, L1_ffn_br, L1_ffn_W1, L1_ffn_b1, L1_ffn_W2, L1_ffn_b2), axis=-1)
    return x

_drawn_inputs = setup_inputs


def setup_inputs(seed=0):
    import zlib

    import numpy as np

    out = dict(_drawn_inputs(seed))
    spreads = {'L0_attn_ln_g': (1.0, 0.6),
     'L0_attn_ln_b': (0.0, 0.8),
     'L0_attn_f_conv_b': (0.0, 0.8),
     'L0_attn_f_D': (1.0, 0.6),
     'L0_attn_b_conv_b': (0.0, 0.8),
     'L0_attn_b_D': (1.0, 0.6),
     'L1_attn_b_qkv': (0.0, 0.1),
     'L1_attn_b_g': (0.0, 0.1),
     'L1_attn_b_p': (0.0, 0.1)}
    factors = {'L0_attn_f_in_w': 5.885,
     'L0_attn_f_conv_w': 5.5,
     'L0_attn_f_xproj_w': 8.0,
     'L0_attn_f_dt_w': 8.0,
     'L0_attn_f_dt_b': 8.0,
     'L0_attn_f_Alog': 8.0,
     'L0_attn_f_out_w': 6.29,
     'L0_attn_b_in_w': 5.896,
     'L0_attn_b_conv_w': 5.785,
     'L0_attn_b_xproj_w': 8.0,
     'L0_attn_b_dt_w': 8.0,
     'L0_attn_b_dt_b': 8.0,
     'L0_attn_b_Alog': 8.0,
     'L0_attn_b_out_w': 6.799,
     'L1_ffn_b1': 2.85}
    for name, (base, spread) in spreads.items():
        noise = np.random.default_rng([zlib.crc32(name.encode()), seed]).standard_normal(out[name].shape)
        drawn = base * np.exp(spread * noise) if base else spread * noise
        out[name] = jnp.asarray(drawn.astype(out[name].dtype))
    for name, factor in factors.items():
        out[name] = (out[name] * factor).astype(out[name].dtype)
    return out
```

```python
import concourse.bass as bass
from concourse import mybir
from contextlib import ExitStack, contextmanager
import numpy as np

F32, BF16, U32, I32 = mybir.dt.float32, mybir.dt.bfloat16, mybir.dt.uint32, mybir.dt.int32
ALU, ACT, AX = mybir.AluOpType, mybir.ActivationFunctionType, mybir.AxisListType
ds = bass.ds

P = 128
B, T, D = 2, 2048, 128
NT = B * T // P
TB = T // P
DI, NS, RK, TAPS = 256, 16, 64, 4
CH = 512
NCH = B * T // CH
HF = DI // P
FF, NE = 512, 8
FK = FF // P
ST = NT + NE
NH, DK, DV = 8, 16, 32
EV = NH * DV
EPS = 1e-5
SPREAD = 0.5186097621917725
FACTORS = ((0.5234627723693848, 0.29748213291168213), (-0.04265656694769859, 0.8761158585548401),
           (-0.7388817667961121, 0.7267470359802246), (-1.2040492296218872, 0.11629842966794968))

W_U = 0
W_Z = W_U + TAPS * DI
W_XD = W_Z + DI
W_XB = W_XD + HF * RK
W_DT = W_XB + HF * 96
W_O = W_DT + DI
W_CB = W_O + HF * D
W_DB = W_CB + HF
W_D = W_DB + HF
W_A = W_D + HF
W_N = W_A + HF * NS

RC_REV = 0
RC_RUN = RC_REV + NE
RC_MULT = RC_RUN + NE * NT
RC_ONE = RC_MULT + NT
RC_J = RC_ONE + NE
RC_N = RC_J + ST + 2


class Mark:
    def __init__(self, lane, at, loops):
        self.lane, self.at, self.loops = lane, at, loops


class Counts:
    START = 1 << 13

    def __init__(self, nc, known):
        self.nc, self.known, self.per, self.later = nc, known, {}, {}
        self.lanes, self.loops, self.n_loops, self.scopes = [], [], 0, [(None, {})]

    @contextmanager
    def loop(self, n):
        key = self.n_loops
        self.n_loops += 1
        before = [(l, l.at) for l in self.lanes]
        for l in self.lanes:
            l.waited = {}
        with self.nc.Fori(0, n, 1) as i:
            self.loops.append((key, i, n))
            self.scopes.append((key, {}))
            yield i
            self.loops.pop()
            _, names = self.scopes.pop()
        self.later.update({(key, name): mark for name, mark in names.items()})
        self.scopes[-1][1].update(names)
        for l, at in before:
            self.per[key, l.name] = l.at - at
            l.at = at + n * (l.at - at)
            l.waited = {}

    def named(self, name):
        found = []
        for key, names in reversed(self.scopes):
            if name in names:
                return found + [(names[name], None)]
            if (key, name) in self.known[1]:
                found.append((self.known[1][key, name], key))
        return found

    def value(self, mark, back):
        per = self.known[0]
        active = {key: i for key, i, _ in self.loops}
        value, terms = mark.at, []
        for key, n in mark.loops:
            m = per.get((key, mark.lane.name), 0)
            if key in active:
                terms += [(active[key], m)] if m else []
            else:
                value += (n - 1) * m
        if back is not None:
            value -= per.get((back, mark.lane.name), 0)
        return value, terms


class Lane:
    def __init__(self, c, name, engine, sem, step=1, start=Counts.START):
        self.c, self.name, self.e, self.sem, self.step = c, name, engine, sem, step
        self.at = self.start = start
        self.waited = {}
        c.lanes.append(self)

    def __call__(self, ins, name=None):
        ins.then_inc(self.sem, self.step)
        self.at += self.step
        m = Mark(self, self.at, [(k, n) for k, _, n in self.c.loops])
        if name:
            self.c.scopes[-1][1][name] = m
        return m

    def wait(self, *marks):
        for m in marks:
            for mark, back in (self.c.named(m) if isinstance(m, str) else [(m, None)]):
                value, terms = self.c.value(mark, back)
                key = (mark.lane.name, tuple(per for _, per in terms))
                if self.waited.get(key, -1) >= value:
                    continue
                self.waited[key] = value
                for i, per in terms:
                    value = value + i * per
                self.e.wait_ge(next(l.sem for l in self.c.lanes if l.name == mark.lane.name), value)


def build(nc, known, a, out):
    c = Counts(nc, known)
    ctx = ExitStack()

    def lane(name, engine, step=1, start=Counts.START):
        l = Lane(c, name, engine, ctx.enter_context(nc.semaphore("s_" + name)), step, start)
        if start:
            engine.sem_inc(l.sem, start)
        return l

    with ctx:
        V = lane("vector", nc.vector)
        S = lane("scalar", nc.scalar)
        G = lane("gpsimd", nc.gpsimd)
        M = lane("tensor", nc.tensor)
        L = {k: lane("load_" + k, nc.sync, 16) for k in ("x", "zero", "mamba", "w", "const")}
        L["out"] = lane("store_out", nc.sync, 16)
        SY = Lane(c, "sync", nc.sync, None)

        def name(new, old):
            c.scopes[-1][1][new] = c.scopes[-1][1][old]

        s_carry = ctx.enter_context(nc.semaphore("s_carry"))

        def barrier():
            now = [Mark(l, l.at, []) for l in c.lanes if l.at > l.start]
            for w in (V, S, G, M, SY):
                w.wait(*now)

        used = {}

        def unused(name):
            used[name] = used.get(name, 0) + 1
            return name if used[name] == 1 else f"{name}_{used[name]}"

        def sb(scope, name, shape, dt=F32):
            return scope.enter_context(nc.sbuf_tensor(unused(name), shape, dt))

        def bank(scope, name, n=1):
            return scope.enter_context(nc.psum_tensor(unused(name), [P, n * 512], F32))

        def flat(t):
            return t.rearrange("p a c -> p (a c)")

        def view(t, n, w, off=0):
            return t[:, off:off + n * w].rearrange("p (n w) -> p n w", n=n)

        def mm(out, lhsT, rhs, start=True, stop=True, name=None, inc=True):
            i = nc.tensor.matmul(out, lhsT, rhs, start=start, stop=stop)
            return M(i, name) if inc else None

        def tr(out, in_, name=None, inc=True):
            i = nc.tensor.transpose(out, in_, ident[:, :])
            return M(i, name) if inc else None

        bx = sb(ctx, "residual", [P, NT, D])
        ident = sb(ctx, "ident", [P, P])
        mirror = sb(ctx, "mirror", [P, P])
        eps = sb(ctx, "eps", [P, 1])
        zeros = sb(ctx, "zeros", [P, D])
        mean = sb(ctx, "mean", [P, NT])
        rstd = sb(ctx, "rstd", [P, NT])
        xsorted = nc.dram_tensor("xsorted", (ST * P, D), F32, kind="Internal").ap()
        ysorted = nc.dram_tensor("ysorted", (ST * P, D), F32, kind="Internal").ap()

        for k in range(4):
            n = NT // 4
            in_x = L["x"](nc.sync.dma_start(bx[:, k * n:(k + 1) * n, :], a["x"][:, k * n:(k + 1) * n, :]))
        L["const"](nc.sync.dma_start(ident[:, :], a["ident"]))
        in_c = L["const"](nc.sync.dma_start(mirror[:, :], a["mirror"]))
        h_eps = V(nc.vector.memset(eps[:, :], EPS))

        SY.wait(V(nc.vector.memset(zeros[:, :], 0.0)))
        for s in range(4):
            t = slice(s * ST // 4, (s + 1) * ST // 4)
            L["zero"](nc.sync.dma_start(xsorted.rearrange("(t p) d -> p t d", p=P)[:, t, :],
                                        zeros[:, :].unsqueeze(1).broadcast_to([P, ST // 4, D])), "zeroed")

        def normalise_stats(cen, sq, ready):
            V.wait(ready)
            h = V(nc.vector.tensor_reduce(mean[:, :], bx[:, :, :], AX.X, ALU.add))
            V.wait(h)
            h = V(nc.vector.tensor_scalar(mean[:, :], mean[:, :], 1.0 / D, None, ALU.mult))
            V.wait(h)
            n = NT // 4
            for k in range(4):
                t = slice(k * n, (k + 1) * n)
                h = V(nc.vector.tensor_tensor(cen[:, t, :], bx[:, t, :],
                                              mean[:, t].unsqueeze(2).broadcast_to([P, n, D]), ALU.subtract))
                S.wait(h, ready)
                hs = S(nc.scalar.activation(sq[:, t, :], cen[:, t, :], ACT.Square))
                V.wait(hs)
                h = V(nc.vector.tensor_reduce(rstd[:, t], sq[:, t, :], AX.X, ALU.add))
            S.wait(h, h_eps)
            h = S(nc.scalar.activation(rstd[:, :], rstd[:, :], ACT.Sqrt, bias=eps[:, 0:1], scale=1.0 / D))
            V.wait(h)
            return V(nc.vector.reciprocal(rstd[:, :], rstd[:, :]), "rstd")

        def layer0_mamba():
            with ExitStack() as k:
                xt = sb(k, "xt", [P, 2 * NCH + 2, TAPS - 1 + CH])
                om = sb(k, "om", [P, 2 * (NCH + 1), CH])
                w = sb(k, "w", [P, W_N])
                lnp = sb(k, "lnp", [P, 2])
                keep = sb(k, "keep", [P, 4 + len(FACTORS)])
                sel = sb(k, "sel", [P, 2 * NS, P], BF16)
                with ExitStack() as k0:
                    xs = sb(k0, "xs", [P, B, D])
                    pt = [bank(k0, f"pt{u}") for u in range(B)]
                    cen = om[:, 0:8, :].rearrange("p a (b d) -> p (a b) d", d=D)
                    sq = om[:, 8:16, :].rearrange("p a (b d) -> p (a b) d", d=D)
                    L["mamba"](nc.sync.dma_start(lnp[:, :], a["lnp"]))
                    L["mamba"](nc.sync.dma_start(keep[:, :], a["keep"]))
                    in_w = L["mamba"](nc.sync.dma_start(sel[0:96, :, :], a["sel"]))
                    normalise_stats(cen, sq, in_x)
                    G(nc.gpsimd.memset(xt[:, 2 * NCH:2 * NCH + 2, :], 0.0), "xt_end")
                    M.wait(in_c)
                    S.wait(in_w)
                    V.wait("rstd")
                    with c.loop(TB // 4) as ci:
                        for kt in range(4):
                            for u in range(B):
                                tile = ci * 4 + (u * TB + kt)
                                V.wait(f"mirrored{u}")
                                V(nc.vector.tensor_scalar(xs[:, u, :], flat(cen[:, ds(tile, 1), :]),
                                                          rstd[:, ds(tile, 1)], None, ALU.mult), f"xs{u}")
                                M.wait(f"xs{u}", f"xt{u}")
                                nc.tensor.matmul(pt[u][:, 0:P], xs[:, u, :], ident[:, :], start=True, stop=True)
                                mm(pt[u][:, P:2 * P], xs[:, u, :], mirror[:, :], name=f"mirrored{u}")
                                S.wait(f"mirrored{u}")
                                col = TAPS - 1 + kt * P
                                S(nc.scalar.activation(flat(xt[:, ds(ci + u * 4, 1), col:col + P]), pt[u][:, 0:P],
                                                       ACT.Identity, bias=lnp[:, 1:2], scale=lnp[:, 0:1]))
                                col = TAPS - 1 + (3 - kt) * P
                                S(nc.scalar.activation(flat(xt[:, ds((NCH + u * 4 + 3) - ci, 1), col:col + P]), pt[u][:, P:2 * P],
                                                       ACT.Identity, bias=lnp[:, 1:2], scale=lnp[:, 0:1]), f"xt{u}")
                    V.wait("xt0", "xt1", "xt_end")
                    V.wait(V(nc.vector.tensor_copy(xt[:, 1:2 * NCH + 1, 0:3], xt[:, 0:2 * NCH, CH:CH + 3])))
                    V(nc.vector.memset(xt[:, 0:2 * NCH + 1:4, 0:3], 0.0))
                    barrier()

                pre = sb(k, "pre", [P, 4, CH])
                uz = [sb(k, f"uz{i}", [P, 4, CH]) for i in range(2)]
                dtr = sb(k, "dtr", [RK, CH])
                mid = sb(k, "mid", [P, CH], BF16)
                bc = [sb(k, f"bc{i}", [P, CH], BF16) for i in range(2)]
                ab = sb(k, "ab", [P, HF, CH])
                rx = sb(k, "rx", [P, HF, CH])
                rest = sb(k, "rest", [P, CH])
                dt = [sb(k, f"dt{i}", [P, HF, CH]) for i in range(2)]
                dtu = [sb(k, f"dtu{i}", [P, HF, CH]) for i in range(2)]
                db = [sb(k, f"db{i}", [P, HF, CH]) for i in range(2)]
                hh = [sb(k, f"hh{i}", [P, HF, CH]) for i in range(3)]
                hc = [sb(k, f"hc{i}", [P, HF, CH]) for i in range(3)]
                cs = [sb(k, f"cs{i}", [P, CH]) for i in range(3)]
                sq = [sb(k, f"sq{i}", [P, HF, CH]) for i in range(2)]
                st = sb(k, "st", [P, NS, HF])
                yz = bx[:, 0:8, :].rearrange("p (h a) d -> p h (a d)", h=HF)
                py = bank(k, "py", 2)
                pb = [bank(k, f"pb{i}") for i in range(2)]
                pc = bank(k, "pc")
                pd = [bank(k, f"pd{i}") for i in range(2)]
                pq = bank(k, "pq")

                def prep(i, slot, before=[], only_u=False):
                    def project(j, col, taps=(TAPS - 1,), last=True):
                        M.wait("w", "pq_empty")
                        at = slot + 1 if j < HF else slot
                        for t in taps:
                            m = nc.tensor.matmul(pq[:, :], w[:, col:col + P] if j >= HF else w[:, col + t * DI:col + t * DI + P],
                                                 flat(xt[:, ds(at, 1), t:t + CH]), start=t == taps[0] and (j >= HF or t == 0),
                                                 stop=t == TAPS - 1)
                        M(m, "pq")

                    def keep_pre(j):
                        S.wait("pq", "w", "uz0", "uz1")
                        bias = w[:, W_CB + j:W_CB + j + 1] if j < HF else 0.0
                        S(nc.scalar.activation(pre[:, j, :], pq[:, :], ACT.Identity, bias=bias), "pq_empty")
                        name(f"pre{j}", "pq_empty")

                    def silu():
                        S.wait("pre0", "pre1", "pre3", f"gated{i}", f"dtu{i}")
                        S(nc.scalar.activation(uz[i][:, :, :], pre[:, :, :], ACT.Silu), f"uz{i}")

                    def rank():
                        M.wait(f"uz{i}", "pq_empty")
                        for h in range(HF):
                            mm(pq[0:RK, :], w[:, W_XD + h * RK:W_XD + (h + 1) * RK], uz[i][:, h, :],
                               start=h == 0, stop=h == HF - 1, name="pq")

                    def keep_rank():
                        S.wait("pq", "dt_in1")
                        S(nc.scalar.activation(dtr[:, :], pq[0:RK, :], ACT.Identity), "pq_empty")
                        name("dtr", "pq_empty")

                    def b_c():
                        M.wait(f"uz{i}", "pq_empty")
                        for h in range(HF):
                            mm(pq[0:96, :], w[:, W_XB + h * 96:W_XB + (h + 1) * 96], uz[i][:, h, :],
                               start=h == 0, stop=h == HF - 1, name="pq")

                    def high_part():
                        V.wait("pq", f"c_read{i}", f"b_read{i}")
                        V.wait(V(nc.vector.tensor_copy(bc[i][0:96, :], pq[0:96, :])), "mid_low")
                        V.wait(V(nc.vector.tensor_tensor(rest[0:96, :], pq[0:96, :], bc[i][0:96, :], ALU.subtract), "pq_empty"))
                        V(nc.vector.tensor_copy(mid[0:96, :], rest[0:96, :]), "mid")

                    def mid_low_parts():
                        V.wait("mid")
                        V(nc.vector.tensor_tensor(bc[i][64:96, :], rest[64:96, :], mid[64:96, :], ALU.subtract))
                        V(nc.vector.tensor_copy(bc[i][32:64, :], mid[32:64, :]), f"bc{i}")
                        name("mid_low", f"bc{i}")

                    def dt_in(h):
                        M.wait("dtr", "pq_empty")
                        mm(pq[:, :], w[0:RK, W_DT + h * P:W_DT + (h + 1) * P], dtr[:, :], name=f"dt_in{h}")

                    def relu_abs(h):
                        bias = w[:, W_DB + h:W_DB + h + 1]
                        S.wait(f"dt_in{h}", "softplus", "factor")
                        S(nc.scalar.activation(rx[:, h, :], pq[:, :], ACT.Relu, bias=bias), "rx")
                        S(nc.scalar.activation(ab[:, h, :], pq[:, :], ACT.Abs, bias=bias), "pq_empty")

                    def exponent():
                        S.wait("pq_empty")
                        S(nc.scalar.activation(ab[:, :, :], ab[:, :, :], ACT.Exp, scale=-1.0), "e")

                    def square(f):
                        S.wait("e", f"factor{f % 2}")
                        S(nc.scalar.activation(sq[f % 2][:, :, :], ab[:, :, :], ACT.Square, scale=SPREAD,
                                               bias=keep[:, 4 + f:5 + f]), f"square{f % 2}")

                    def factor(f):
                        V.wait(f"square{f % 2}", "factor", f"da{i}")
                        V(nc.vector.scalar_tensor_tensor(dt[i][:, :, :], sq[f % 2][:, :, :], FACTORS[f][1],
                                                         ab[:, :, :] if f == 0 else dt[i][:, :, :], ALU.add, ALU.mult), "factor")
                        name(f"factor{f % 2}", "factor")

                    def finish():
                        V.wait("factor", "rx")
                        V(nc.vector.tensor_tensor(dt[i][:, :, :], rx[:, :, :], dt[i][:, :, :], ALU.add), f"dt{i}")
                        name("softplus", f"dt{i}")
                        G.wait(f"dt{i}", f"uz{i}", f"dtu_read{i}")
                        G(nc.gpsimd.tensor_tensor(dtu[i][:, :, :], dt[i][:, :, :], uz[i][:, 0:HF, :], ALU.mult), f"dtu{i}")

                    def of(stage, *args):
                        return lambda: stage(*args)

                    next_u = [[]] * 11 + [
                        [of(project, 0, W_U, (0, 1))], [of(project, 0, W_U, (2, 3))],
                        [of(keep_pre, 0), of(project, 1, W_U + P, (0, 1))], [of(project, 1, W_U + P, (2, 3))],
                        [of(keep_pre, 1)]]
                    if only_u:
                        return next_u
                    rest_ = [[of(project, 2, W_Z)],
                            [of(keep_pre, 2), of(project, 3, W_Z + P)],
                            [of(keep_pre, 3)],
                            [silu, rank],
                            [keep_rank, of(dt_in, 0)],
                            [of(relu_abs, 0), of(dt_in, 1)],
                            [of(relu_abs, 1), exponent, of(square, 0), b_c],
                            [high_part, mid_low_parts, of(square, 1)],
                            [of(factor, 0), of(square, 2)] + before[0:1],
                            [of(factor, 1), of(square, 3)] + before[1:2],
                            [of(factor, 2)] + before[2:3],
                            [of(factor, 3)], [finish]] + [[]] * 3
                    return [x + y for x, y in zip(rest_, next_u)]

                def gate(j):
                    V.wait("summed", "projected", "w")
                    for h in range(HF):
                        V(nc.vector.scalar_tensor_tensor(yz[:, h, :], uz[j][:, h, :], w[:, W_D + h:W_D + h + 1],
                                                         py[:, h * CH:(h + 1) * CH], ALU.mult, ALU.add), "py_empty")
                    G.wait("py_empty")
                    G(nc.gpsimd.tensor_tensor(yz[:, :, :], yz[:, :, :], uz[j][:, HF:2 * HF, :], ALU.mult), f"gated{j}")

                def out_project(j, slot):
                    def tiles(of):
                        M.wait(f"gated{j}", "pq_empty")
                        for kt in of:
                            for h in range(HF):
                                mm(pq[:, kt * P:(kt + 1) * P], yz[:, h, kt * P:(kt + 1) * P], w[:, W_O + h * D:W_O + (h + 1) * D],
                                   start=h == 0, stop=h == HF - 1, name="projected")

                    def store():
                        S.wait("projected")
                        S(nc.scalar.activation(flat(om[:, ds(slot, 1), :]), pq[:, :], ACT.Identity), "pq_empty")
                    return [lambda: tiles((0, 1)), lambda: tiles((2, 3)), store]

                def add_up(n, b):
                    M.wait(f"hc{b}", "py_empty")
                    for h in range(HF):
                        mm(py[:, h * CH:(h + 1) * CH], ident[:, :], hc[b][:, h, :], start=n == 0, stop=n == NS - 1, name=f"summed{b}")
                    if n == NS - 1:
                        name("summed", f"summed{b}")

                def spread_b(n, i):
                    M.wait(f"bc{i}", f"db{n % 2}")
                    mm(pb[n % 2][:, :], sel[0:96, n, :], bc[i][0:96, :], name=f"b{n % 2}")
                    name(f"b_read{i}", f"b{n % 2}")

                def spread_c(n, i):
                    M.wait(f"bc{i}", "cs")
                    mm(pc[:, :], sel[0:96, NS + n, :], bc[i][0:96, :], name=f"c_read{i}")
                    name("c", f"c_read{i}")

                def inflow(n, i):
                    b = n % 2
                    V.wait(f"b{b}", f"dtu{i}", f"scans{b}")
                    V(nc.vector.tensor_tensor(db[b][:, :, :], dtu[i][:, :, :], pb[b][:, :].unsqueeze(1).broadcast_to([P, HF, CH]),
                                              ALU.mult), f"db{b}")
                    name(f"dtu_read{i}", f"db{b}")

                def scan_step(n, i, meanwhile):
                    b, r = n % 2, (i * NS + n) % 3
                    ahead = lambda k: ((n + k) % NS, i if n + k < NS else i ^ 1)
                    S.wait(f"dt{i}", "w")
                    for h in range(HF):
                        S.wait(f"scan{h}")
                        S(nc.scalar.activation(pd[h][:, :], dt[i][:, h, :], ACT.Exp,
                                               scale=w[:, W_A + h * NS + n:W_A + h * NS + n + 1]), f"da{i}")
                        name(f"pd{h}", f"da{i}")
                    S.wait("c", f"hc{r}")
                    S(nc.scalar.activation(cs[r][:, :], pc[:, :], ACT.Identity), "cs")
                    name(f"cs{r}", "cs")
                    inflow(*ahead(1))
                    spread_c(*ahead(1))
                    spread_b(*ahead(2))
                    V.wait(f"db{b}", f"hc{r}", f"state{r}")
                    for h in range(HF):
                        V.wait(f"pd{h}")
                        V(nc.vector.tensor_tensor_scan(hh[r][:, h, :], pd[h][:, :], db[b][:, h, :], st[:, n, h:h + 1],
                                                       ALU.mult, ALU.add), f"scan{h}")
                    name(f"scans{b}", "scan1")
                    if n == 2:
                        gate(i ^ 1)
                    if n == 3:
                        add_up(0, (i * NS) % 3)
                    if n != 2:
                        add_up((n - 2) % NS, (i * NS + n - 2) % (2 * NS) % 3)
                    G.wait("scan1", f"cs{r}", f"summed{r}")
                    G(nc.gpsimd.tensor_tensor(hc[r][:, :, :], hh[r][:, :, :], cs[r][:, :].unsqueeze(1).broadcast_to([P, HF, CH]),
                                              ALU.mult), f"hc{r}")
                    G(nc.gpsimd.tensor_copy(st[:, n, :], hh[r][:, :, CH - 1]), f"state{r}")
                    for work in meanwhile:
                        work()

                with c.loop(2) as di:
                    V.wait("projected", "cs", "pq_empty", "summed1", "state0", "state1", "state2", "c_read0", "b_read1", "dt_in1", "dtu0", "db1", "pre1")
                    V(nc.vector.memset(uz[1][:, :, :], 0.0), "uz1")
                    V(nc.vector.memset(st[:, :, :], 0.0), "st")
                    SY.wait("st")
                    nc.sync.sem_inc(s_carry, 1)
                    L["w"](nc.sync.dma_start(pre[:, 0:2, :], a["conv_w"][:, ds(di, 1), :]))
                    L["w"](nc.sync.dma_start(pre[:, 2, 0:DI], flat(a["in_u"][:, ds(di, 1), :])))
                    in_w = L["w"](nc.sync.dma_start(w[:, W_Z:W_N], flat(a["mamba_w"][:, ds(di, 1), :])))
                    V.wait(in_w)
                    V(nc.vector.tensor_tensor(view(w, TAPS, DI), pre[:, 0:2, :].rearrange("p a (t d) -> p (a t) d", d=DI),
                                              pre[:, 2, 0:DI].unsqueeze(1).broadcast_to([P, TAPS, DI]), ALU.mult))
                    S.wait(in_w)
                    V.wait(S(nc.scalar.activation(w[:, W_A:W_N], w[:, W_A:W_N], ACT.Exp)))
                    V(nc.vector.tensor_scalar(w[:, W_A:W_N], w[:, W_A:W_N], -1.0, None, ALU.mult), "w")
                    V.wait("projected", "summed0", "summed1")
                    V.wait("w", "uz1", "st")
                    M.wait("w")
                    for works in prep(0, di * NCH - 1, only_u=True) + prep(0, di * NCH):
                        for work in works:
                            work()
                    for step in (2 * NS - 2, 2 * NS - 1):
                        b = step % 3
                        V(nc.vector.memset(hc[b][:, :, :], 0.0), f"hc{b}")
                    add_up(0, (2 * NS - 2) % 3)
                    spread_b(0, 0)
                    spread_c(0, 0)
                    inflow(0, 0)
                    spread_b(1, 0)
                    with c.loop(NCH // 2) as qi:
                        V.wait("state0", "state1", "state2")
                        V.wait(V(nc.vector.tensor_scalar(st[:, :, :], st[:, :, :], keep[:, ds(qi, 1)], None, ALU.mult)))
                        for i in range(2):
                            steps = prep(i ^ 1, di * NCH + qi * 2 + (i + 1), out_project(i ^ 1, di * (NCH + 1) + qi * 2 + i))
                            for n in range(NS):
                                scan_step(n, i, steps[n])
                    add_up(NS - 2, (2 * NS - 2) % 3)
                    add_up(NS - 1, (2 * NS - 1) % 3)
                    gate(1)
                    for work in out_project(1, di * (NCH + 1) + NCH):
                        work()

                barrier()
                again = L["x"](nc.sync.dma_start(bx[:, 0:8, :], a["x"][:, 0:8, :]))
                for g in (0, 1, 6, 7, 4, 5, 2, 3):
                    bnk = (pb[0], pb[1], pc, pq)[g % 4]
                    M.wait(f"turned{g % 4}")
                    mm(bnk[:, :], mirror[:, :], om[:, NCH + 2 + g, :], name="turned")
                    if g == 2:
                        V.wait(again)
                    t = (g // 4) * TB + (3 - g % 4) * 4
                    V.wait(V(nc.vector.scalar_tensor_tensor(bx[:, t:t + 4, :], bx[:, t:t + 4, :], 2.0,
                                                            view(om[:, 1 + t // 4, :], 4, D), ALU.mult, ALU.add)), "turned")
                    for kt in range(4):
                        V(nc.vector.tensor_tensor(bx[:, t + 3 - kt, :], bx[:, t + 3 - kt, :], bnk[:, kt * P:(kt + 1) * P], ALU.add),
                          f"turned{g % 4}")
                barrier()

        def final():
            with ExitStack() as k:
                cen = sb(k, "cen", [P, NT, D])
                sq = sb(k, "sq_last", [P, NT, D])
                normalise_stats(cen, sq, in_x)
                V.wait("rstd")
                n = NT // 4
                for s in range(4):
                    t = slice(s * n, (s + 1) * n)
                    V(nc.vector.tensor_tensor(cen[:, t, :], cen[:, t, :], rstd[:, t].unsqueeze(2).broadcast_to([P, n, D]),
                                              ALU.mult), "x_out")
                    SY.wait("x_out")
                    L["out"](nc.sync.dma_start(out[:, t, :], cen[:, t, :]))
                SY.wait(Mark(L["out"], L["out"].at, []))

        def experts(glu, layer):
            with ExitStack() as k:
                small, shared, weights, sorted_x = [lane(f"load{layer}_{s}", nc.sync, 16) for s in ("small", "shared", "weights", "sorted_x")]
                scatter = lane(f"scatter{layer}", nc.gpsimd, 16, 0)
                store_y = lane(f"store{layer}_sorted_y", nc.sync, 16)
                gather = [lane(f"gather{layer}_{s}", nc.gpsimd, 16, 0) for s in range(4)]
                q = (2 if glu else 1) * FF
                x1 = sb(k, "x1", [P, NT, D])
                xsort = sb(k, "xsort", [P, ST + 2, D])
                ysort = sb(k, "ysort", [P, ST, D])
                back = ysort[:, 0:NT, :]
                wx = sb(k, "wx", [P, NE, q + FF])
                rc = sb(k, "rc", [P, RC_N])
                before = sb(k, "before", [P, P], BF16)
                every = sb(k, "every", [P, P], BF16)
                rw = sb(k, "rw", [P, NE])
                lg = sb(k, "lg", [P, NT, NE])
                hot = sb(k, "hot", [P, NT, NE])
                hot_b = sb(k, "hot_b", [P, NT, NE], BF16)
                work_ = sb(k, "work", [P, NT, NE])
                incl = sb(k, "incl", [P, NE, NT])
                tot = sb(k, "tot", [P, NE, NT])
                top = sb(k, "top", [P, NT])
                factor2 = sb(k, "factor2", [P, NT])
                tiles_of = sb(k, "tiles_of", [P, NE])
                ends = sb(k, "ends", [P, NE])
                cmp_ = sb(k, "cmp", [P, ST + 2, NE])
                exf = sb(k, "exf", [P, ST + 2])
                expert = sb(k, "expert", [P, ST + 2], I32)
                pos = sb(k, "pos", [P, NT], U32)
                xs4 = [sb(k, f"xs4{u}", [P, 4, D]) for u in range(2)]
                xt4 = [sb(k, f"xt4{u}", [P, 4 * P]) for u in range(2)]
                sg = [sb(k, f"sg{u}", [P, FF]) for u in range(2)]
                hid = [sb(k, f"hid{u}", [P, FF]) for u in range(2)]
                ht = [sb(k, f"ht{u}", [P, FF]) for u in range(2)]
                pbk = [bank(k, f"bank{u}") for u in range(8)]
                pt, pl, pu, pg, pw = pbk[0:2], pbk[2], pbk[3:5], pbk[5:7], pbk[7]
                if glu:
                    xall = sb(k, "xall", [P, NT * P])
                    ws = sb(k, "ws", [P, 3 * FF])
                    ht4 = [sb(k, f"ht4{u}", [P, 4 * P]) for u in range(2)]
                else:
                    brb = sb(k, "brb", [P, NE])
                    b1 = sb(k, "b1", [P, NE * FK])
                    b2 = sb(k, "b2", [P, NE, D])

                small(nc.sync.dma_start(rw[:, :], a[f"rw{layer}"]))
                small(nc.sync.dma_start(before[:, :], a["before"]))
                small(nc.sync.dma_start(every[:, :], a["every"]))
                if not glu:
                    small(nc.sync.dma_start(brb[:, :], a["br"].partition_broadcast(P)))
                    small(nc.sync.dma_start(b1[:, :], a["b1"]))
                    small(nc.sync.dma_start(b2[:, :, :], a["b2"].partition_broadcast(P)))
                in_r = small(nc.sync.dma_start(rc[:, :], a["rc"]))
                if glu:
                    in_s = shared(nc.sync.dma_start(ws[:, :], a["shared_w"]))
                    no_expert = V(nc.vector.memset(wx[:, NE - 1:NE, :], 0.0))
                else:
                    no_expert = in_r
                last = NE - 1 if glu else NE
                weights(nc.sync.dma_start(wx[:, 0:4, :], a[f"l{layer}_w"][:, 0:4, :]))
                in_e = weights(nc.sync.dma_start(wx[:, 4:last, :], a[f"l{layer}_w"][:, 4:last, :]))
                V(nc.vector.memset(xsort[:, ST:ST + 2, :], 0.0), "xsort_end")

                normalise_stats(x1, back, in_r)
                V.wait("rstd")
                for s in range(4):
                    t = slice(s * NT // 4, (s + 1) * NT // 4)
                    V(nc.vector.tensor_tensor(x1[:, t, :], x1[:, t, :], rstd[:, t].unsqueeze(2).broadcast_to([P, NT // 4, D]),
                                              ALU.mult), "x1")

                def transpose_x(g, u):
                    V.wait("x1", f"xs4_read{u}")
                    V(nc.vector.tensor_copy(xs4[u][:, :, :], x1[:, ds(g * 4, 4), :]), f"xs4{u}")
                    M.wait(f"xs4{u}", f"xt4{u}")
                    for kt in range(4):
                        tr(pt[u][:, kt * P:(kt + 1) * P], xs4[u][:, kt, :], f"xs4_read{u}")
                    S.wait(f"xs4_read{u}", f"logits{u}")
                    S(nc.scalar.activation(xt4[u][:, :], pt[u][:, :], ACT.Identity), f"xt4{u}")
                    if glu:
                        S.wait(f"xt4{u}")
                        S(nc.scalar.activation(xall[:, ds(g * (4 * P), 4 * P)], xt4[u][:, :], ACT.Identity), "xall")

                def logits(g, u):
                    M.wait(f"xt4{u}", f"lg{u}", in_r)
                    for kt in range(4):
                        mm(pg[u][:, kt * NE:(kt + 1) * NE], xt4[u][:, kt * P:(kt + 1) * P], rw[:, :], name=f"logits{u}")
                    V.wait(f"logits{u}")
                    if glu:
                        V(nc.vector.tensor_copy(lg[:, ds(g * 4, 4), :], view(pg[u], 4, NE)), f"lg{u}")
                    else:
                        V(nc.vector.tensor_tensor(lg[:, ds(g * 4, 4), :], view(pg[u], 4, NE),
                                                  brb[:, :].unsqueeze(1).broadcast_to([P, 4, NE]), ALU.add), f"lg{u}")

                M.wait(in_c)
                with c.loop(NT // 8) as gi:
                    transpose_x(gi * 2, 0)
                    transpose_x(gi * 2 + 1, 1)
                    logits(gi * 2, 0)
                    logits(gi * 2 + 1, 1)

                def step(ins, name=None):
                    V.wait(V(ins, name))
                over_e = lambda v: v.unsqueeze(2).broadcast_to([P, NT, NE])
                V.wait("lg0", "lg1", in_r)
                step(nc.vector.tensor_reduce(top[:, :], lg[:, :, :], AX.X, ALU.max))
                step(nc.vector.tensor_tensor(lg[:, :, :], lg[:, :, :], over_e(top[:, :]), ALU.subtract), "shifted")
                if glu:
                    S.wait("shifted")
                    S(nc.scalar.activation(work_[:, :, :], lg[:, :, :], ACT.Exp), "exps")
                step(nc.vector.tensor_scalar(hot[:, :, :], lg[:, :, :], 0.0, None, ALU.is_ge))
                step(nc.vector.tensor_tensor(hot[:, :, :], hot[:, :, :], rc[:, RC_REV:RC_REV + NE].unsqueeze(1).broadcast_to([P, NT, NE]),
                                             ALU.mult))
                step(nc.vector.tensor_reduce(top[:, :], hot[:, :, :], AX.X, ALU.max))
                step(nc.vector.tensor_tensor(hot[:, :, :], hot[:, :, :], over_e(top[:, :]), ALU.is_equal))
                step(nc.vector.tensor_copy(hot_b[:, :, :], hot[:, :, :]), "hot_b")
                M.wait("hot_b")
                mm(pg[0][:, 0:NT * NE], before[:, :], flat(hot_b[:, :, :]))
                mm(pg[1][:, 0:NT * NE], every[:, :], flat(hot_b[:, :, :]), name="ranks")
                if glu:
                    V.wait("exps")
                    step(nc.vector.tensor_reduce(factor2[:, :], work_[:, :, :], AX.X, ALU.add))
                    step(nc.vector.reciprocal(factor2[:, :], factor2[:, :]))
                    step(nc.vector.tensor_scalar(factor2[:, :], factor2[:, :], 2.0, None, ALU.mult), "factor2")
                V.wait("ranks")
                step(nc.vector.tensor_copy(tot[:, :, :], view(pg[1], NT, NE).rearrange("p t e -> p e t")))
                step(nc.vector.tensor_tensor_scan(flat(incl[:, :, :]), rc[:, RC_RUN:RC_RUN + NE * NT], flat(tot[:, :, :]), 0.0,
                                                  ALU.mult, ALU.add))
                step(nc.vector.tensor_tensor(tot[:, :, :], incl[:, :, :], tot[:, :, :], ALU.subtract))
                step(nc.vector.tensor_tensor(work_[:, :, :].rearrange("p t e -> p (t e)").rearrange("p (e m) -> p e m", e=NE),
                                             incl[:, :, NT - 1:NT].broadcast_to([P, NE, NT]),
                                             rc[:, RC_MULT:RC_MULT + NT].unsqueeze(1).broadcast_to([P, NE, NT]), ALU.is_gt))
                step(nc.vector.tensor_reduce(tiles_of[:, :], work_[:, :, :].rearrange("p t e -> p (t e)").rearrange("p (e m) -> p e m", e=NE),
                                             AX.X, ALU.add))
                step(nc.vector.tensor_tensor_scan(ends[:, :], rc[:, RC_ONE:RC_ONE + NE], tiles_of[:, :], 0.0, ALU.mult, ALU.add))
                step(nc.vector.tensor_tensor(tiles_of[:, :], ends[:, :], tiles_of[:, :], ALU.subtract))
                step(nc.vector.scalar_tensor_tensor(tot[:, :, :], tiles_of[:, :].unsqueeze(2).broadcast_to([P, NE, NT]), float(P),
                                                    tot[:, :, :], ALU.mult, ALU.add))
                step(nc.vector.tensor_tensor(work_[:, :, :], view(pg[0], NT, NE), tot[:, :, :].rearrange("p e t -> p t e"), ALU.add))
                step(nc.vector.tensor_tensor(work_[:, :, :], work_[:, :, :], hot[:, :, :], ALU.mult))
                step(nc.vector.tensor_reduce(top[:, :], work_[:, :, :], AX.X, ALU.add))
                step(nc.vector.tensor_copy(pos[:, :], top[:, :]), "pos")
                step(nc.vector.tensor_tensor(cmp_[:, :, :], rc[:, RC_J:RC_J + ST + 2].unsqueeze(2).broadcast_to([P, ST + 2, NE]),
                                             ends[:, :].unsqueeze(1).broadcast_to([P, ST + 2, NE]), ALU.is_ge))
                step(nc.vector.tensor_reduce(exf[:, :], cmp_[:, :, :], AX.X, ALU.add))
                step(nc.vector.tensor_scalar(exf[:, :], exf[:, :], float(NE - 1), None, ALU.min))
                step(nc.vector.tensor_copy(expert[:, :], exf[:, :]), "expert")

                G.wait("pos", "x1", "zeroed")
                for t in range(NT):
                    sent = scatter(nc.gpsimd.indirect_dma_start(
                        out=xsorted, out_offset=bass.IndirectOffsetOnAxis(ap=pos[:, t:t + 1], axis=0),
                        in_=x1[:, t, :], in_offset=None))
                SY.wait(sent)
                for s in range(4):
                    t = slice(s * ST // 4, (s + 1) * ST // 4)
                    in_xs = sorted_x(nc.sync.dma_start(xsort[:, t, :], xsorted.rearrange("(t p) d -> p t d", p=P)[:, t, :]))

                if glu:
                    M.wait(in_s, "xall", "lg1")
                    with c.loop(NT // 4) as g:
                        def hidden(f):
                            u = f % 2
                            M.wait(f"ht4{u}")
                            mm(pu[u][:, :], ws[:, f * P:(f + 1) * P], xall[:, ds(g * (4 * P), 4 * P)])
                            mm(pg[u][:, :], ws[:, FF + f * P:FF + (f + 1) * P], xall[:, ds(g * (4 * P), 4 * P)], name=f"ug{u}")
                            S.wait(f"ug{u}", f"ht4{u}")
                            S(nc.scalar.activation(sg[u][:, :], pg[u][:, :], ACT.Silu), f"sg{u}")
                            V.wait(f"sg{u}", f"down{u}")
                            V(nc.vector.tensor_tensor(ht4[u][:, :], pu[u][:, :], sg[u][:, :], ALU.mult), f"ht4{u}")

                        def down(f):
                            u = f % 2
                            M.wait(f"ht4{u}", "yt_read")
                            mm(pw[:, :], ws[:, 2 * FF + f * P:2 * FF + (f + 1) * P], ht4[u][:, :], start=f == 0, stop=f == FK - 1,
                               name=f"down{u}")

                        hidden(0)
                        for f in range(1, FK):
                            hidden(f)
                            down(f - 1)
                        down(FK - 1)
                        S.wait("down1", "yt4_read")
                        S(nc.scalar.activation(ht[0][:, :], pw[:, :], ACT.Identity), "yt_read")
                        M.wait("yt_read", "added")
                        for kt in range(4):
                            tr(pt[0][:, kt * P:(kt + 1) * P], ht[0][:, kt * P:(kt + 1) * P], "yt4_read")
                        V.wait("yt4_read")
                        V(nc.vector.tensor_tensor(bx[:, ds(g * 4, 4), :], x1[:, ds(g * 4, 4), :], view(pt[0], 4, P), ALU.add), "added")
                    V.wait("added")
                    S.wait("added")

                def get_x(j, u):
                    V.wait(f"xs_read{u}", "xsort_end", in_xs)
                    V(nc.vector.tensor_copy(xs4[u][:, 0, :], flat(xsort[:, ds(j, 1), :])), f"xs{u}")
                    M.wait(f"xs{u}", f"xt{u}")
                    tr(pt[u][:, 0:P], xs4[u][:, 0, :], f"xs_read{u}")
                    S.wait(f"xs_read{u}", f"ug{u}")
                    S(nc.scalar.activation(xt4[u][:, 0:P], pt[u][:, 0:P], ACT.Identity), f"xt{u}")

                def products_in(j, u):
                    e = nc.tensor.value_load(expert[0:1, ds(j, 1)], min_val=0, max_val=NE - 1)
                    M.wait(f"xt{u}", f"hid{u}")
                    if glu:
                        mm(pu[u][:, :], xt4[u][:, 0:P], flat(wx[:, ds(e, 1), 0:FF]))
                        mm(pg[u][:, :], xt4[u][:, 0:P], flat(wx[:, ds(e, 1), FF:2 * FF]), name=f"ug{u}")
                        S.wait(f"ug{u}", f"hid{u}")
                        S(nc.scalar.activation(sg[u][:, :], pg[u][:, :], ACT.Silu), f"sg{u}")
                        V.wait(f"sg{u}", f"hid_read{u}")
                        V(nc.vector.tensor_tensor(hid[u][:, :], pu[u][:, :], sg[u][:, :], ALU.mult), f"hid{u}")
                    else:
                        mm(pu[u][:, :], xt4[u][:, 0:P], flat(wx[:, ds(e, 1), 0:FF]), name=f"ug{u}")
                        S.wait(f"ug{u}", f"hid_read{u}")
                        S(nc.scalar.activation(hid[u][:, :], pu[u][:, :], ACT.Identity), f"hid{u}")

                def turn_hidden(j, u):
                    M.wait(f"hid{u}", "ht")
                    for f in range(FK):
                        tr(pl[:, f * P:(f + 1) * P], hid[u][:, f * P:(f + 1) * P], f"hid_read{u}")
                    V.wait(f"hid_read{u}", f"y{u}")
                    if glu:
                        V(nc.vector.tensor_copy(ht[u][:, :], pl[:, :]), "ht")
                    else:
                        e = nc.vector.value_load(expert[0:1, ds(j, 1)], min_val=0, max_val=NE - 1)
                        for f in range(FK):
                            V(nc.vector.tensor_scalar(ht[u][:, f * P:(f + 1) * P], pl[:, f * P:(f + 1) * P],
                                                      b1[:, ds(e * FK + f, 1)], 0.0, ALU.add, ALU.max), "ht")
                    name(f"ht{u}", "ht")

                def products_out(j, u):
                    e = nc.tensor.value_load(expert[0:1, ds(j, 1)], min_val=0, max_val=NE - 1)
                    M.wait(f"ht{u}", f"ysort{u ^ 1}")
                    for f in range(FK):
                        mm(pw[:, 0:P], ht[u][:, f * P:(f + 1) * P], flat(wx[:, ds(e, 1), q + f * P:q + (f + 1) * P]),
                           start=f == 0, stop=f == FK - 1, name=f"y{u}")
                    if glu:
                        S.wait(f"y{u}")
                        S(nc.scalar.activation(flat(ysort[:, ds(j, 1), :]), pw[:, 0:P], ACT.Identity), f"ysort{u}")
                    else:
                        e = nc.vector.value_load(expert[0:1, ds(j, 1)], min_val=0, max_val=NE - 1)
                        V.wait(f"y{u}")
                        V(nc.vector.tensor_tensor(flat(ysort[:, ds(j, 1), :]), pw[:, 0:P], flat(b2[:, ds(e, 1), :]),
                                                  ALU.add), f"ysort{u}")

                M.wait(in_e, no_expert, "expert")
                V.wait(in_e, "expert")
                get_x(0, 0)
                get_x(1, 1)
                products_in(0, 0)
                with c.loop(ST // 2) as ji:
                    for u in range(2):
                        turn_hidden(ji * 2 + u, u)
                        products_in(ji * 2 + (u + 1), u ^ 1)
                        products_out(ji * 2 + u, u)
                        get_x(ji * 2 + (u + 2), u)

                SY.wait("ysort0", "ysort1")
                for s in range(4):
                    t = slice(s * ST // 4, (s + 1) * ST // 4)
                    out_y = store_y(nc.sync.dma_start(ysorted.rearrange("(t p) d -> p t d", p=P)[:, t, :], ysort[:, t, :]))
                G.wait(out_y)
                V.wait(out_y)
                per = NT // 4
                for s in range(4):
                    for t in range(s * per, (s + 1) * per):
                        got = gather[s](nc.gpsimd.indirect_dma_start(
                            out=back[:, t, :], out_offset=None, in_=ysorted,
                            in_offset=bass.IndirectOffsetOnAxis(ap=pos[:, t:t + 1], axis=0)))
                    t = slice(s * per, (s + 1) * per)
                    V.wait(got)
                    if glu:
                        step(nc.vector.tensor_tensor(back[:, t, :], back[:, t, :],
                                                     factor2[:, t].unsqueeze(2).broadcast_to([P, per, D]), ALU.mult))
                    V(nc.vector.tensor_tensor(bx[:, t, :], (bx if glu else x1)[:, t, :], back[:, t, :], ALU.add), "bx")
                barrier()


        def layer1_retention():
            with ExitStack() as k:
                small, tables = [lane(f"load_ret_{s}", nc.sync, 16) for s in ("small", "tables")]
                C = P
                x1 = sb(k, "x2", [P, NT, D])
                sq = sb(k, "sq2", [P, NT, D])
                wqk = sb(k, "wqk", [P, 4 * D])
                wvg = sb(k, "wvg", [P, 2 * EV])
                wp = sb(k, "wp", [P, 2, D])
                bqk = sb(k, "bqk", [P, 4])
                bvg = sb(k, "bvg", [P, 2 * EV])
                bp = sb(k, "bp", [P, D])
                rot = sb(k, "rot", [P, 4, T])
                decay = sb(k, "decay", [P, NH, C])
                edge = sb(k, "edge", [P, 2, C])
                heads4 = sb(k, "heads4", [P, 4])
                block = sb(k, "block", [P, EV])
                gam = sb(k, "gam", [P, 1])
                state = sb(k, "state", [P, B, EV])
                inflow_ = sb(k, "kv_in", [P, B, EV])
                two = lambda n, shape: [sb(k, f"{n}{u}", shape) for u in range(2)]
                xs, xt_ = two("xs_r", [P, B, D]), two("xt_r", [P, B * P])
                ra, rb = two("ra", [P, B, C]), two("rb", [P, B, C])
                qr, kr = two("qr", [P, B, C]), two("kr", [P, B, C])
                q2, k2 = two("q2_", [P, B, C]), two("k2_", [P, B, C])
                k2t = two("k2t", [P, B, C])
                qx = two("qx", [P, B, 4, C])
                vg = two("vg", [P, B, 2 * EV])
                gt = two("gt", [P, B, EV])
                sm = two("sm", [P, NH, C])
                og = two("og", [P, B * NH, DV])
                og2 = sb(k, "og2", [P, B * NH, DV])
                mu = sb(k, "mu", [P, B * NH])
                rs = sb(k, "rs", [P, B * NH])
                gy = sb(k, "gy", [P, B * EV])
                gyt = sb(k, "gyt", [P, B * EV])
                p_turn, p_q, p_k, p_vg, p_s0, p_s1, p_out, p_kv = [bank(k, f"pr{u}") for u in range(8)]
                p_s = (p_s0, p_s1)

                for dst, src in ((wqk[:, :], "wqk"), (wvg[:, :], "wvg"), (bqk[:, :], "bqk"), (edge[:, :, :], "edge"), (heads4[:, :], "heads4"), (block[:, :], "block"),
                                 (gam[:, :], "gam"), (wp[:, :, :], "wp"), (decay[:, :, :], "decay")):
                    small(nc.sync.dma_start(dst, a[src]))
                small(nc.sync.dma_start(bvg[:, :], a["bvg"].partition_broadcast(P)))
                in_s = small(nc.sync.dma_start(bp[:, :], a["bp"].partition_broadcast(P)))
                for r in range(4):
                    in_t = tables(nc.sync.dma_start(rot[:, r, :], a["rot"][:, r, :]))
                V(nc.vector.memset(state[:, :, :], 0.0), "state_r")

                normalise_stats(x1, sq, in_c)
                V.wait("rstd")
                for s in range(4):
                    t = slice(s * NT // 4, (s + 1) * NT // 4)
                    V(nc.vector.tensor_tensor(x1[:, t, :], x1[:, t, :], rstd[:, t].unsqueeze(2).broadcast_to([P, NT // 4, D]),
                                              ALU.mult), "x1")
                V.wait("x1", in_s, in_t)
                G.wait("x1", in_s)
                for s in range(4):
                    t = slice(s * NT // 4, (s + 1) * NT // 4)
                    G(nc.gpsimd.tensor_tensor(bx[:, t, :], x1[:, t, :], bp[:, :].unsqueeze(1).broadcast_to([P, NT // 4, D]),
                                              ALU.add), "x1_bp")
                M.wait(in_s, in_t)
                S.wait(in_s)
                by_batch = lambda v: v.rearrange("p (b c) d -> p b c d", b=B)
                over_b = lambda v: v.unsqueeze(1).broadcast_to([P, B, C])

                def turn_x(c_, u):
                    V.wait("x_turned")
                    V(nc.vector.tensor_copy(xs[u][:, :, :].unsqueeze(2), by_batch(x1[:, :, :])[:, :, ds(c_, 1), :]), "xs_r")
                    M.wait("xs_r", "xt_r", "k2t")
                    for b in range(B):
                        tr(p_turn[:, b * P:(b + 1) * P], xs[u][:, b, :], "x_turned")
                    S.wait("x_turned", f"vg_made{u}", "k_made")
                    S(nc.scalar.activation(xt_[u][:, :], p_turn[:, 0:B * P], ACT.Identity), "xt_r")

                def project_qk(c_, u):
                    M.wait("xt_r", "rot_q", "rot_k")
                    for j, (bnk, nm) in enumerate(((p_q, "q_made"), (p_q, "q_made"), (p_k, "k_made"), (p_k, "k_made"))):
                        mm(bnk[:, (j % 2) * B * C:(j % 2 + 1) * B * C], wqk[:, j * D:(j + 1) * D], xt_[u][:, :], name=nm)

                def rotate(c_, u):
                    for j, (bnk, dst, nm, far) in enumerate(((p_q, qr, "q", q2), (p_k, kr, "k", k2))):
                        V.wait(f"{nm}_made", f"{nm}_summed")
                        for r, part in enumerate((ra[j], rb[j])):
                            V(nc.vector.scalar_tensor_tensor(part[:, :, :], view(bnk, B, C, r * B * C), bqk[:, 2 * j + r:2 * j + r + 1],
                                                             rot[:, 2 * j + r, ds(c_ * C, C)].unsqueeze(1).broadcast_to([P, B, C]),
                                                             ALU.add, ALU.mult), f"rot_{nm}")
                        G.wait(f"rot_{nm}", "scores", "qx", "k2_turned", "from_state")
                        G(nc.gpsimd.tensor_tensor(dst[u][:, :, :], ra[j][:, :, :], rb[j][:, :, :], ALU.add), f"{nm}_summed")
                        G.wait(f"{nm}_summed")
                        G(nc.gpsimd.tensor_tensor(far[u][:, :, :], dst[u][:, :, :], over_b(edge[:, j, :]), ALU.mult), f"{nm}2_{u}")

                def spread_q(u):
                    V.wait("q_summed", "scores")
                    V(nc.vector.tensor_tensor(qx[u][:, :, :, :], qr[u][:, :, :].unsqueeze(2).broadcast_to([P, B, 4, C]),
                                              heads4[:, :].unsqueeze(1).unsqueeze(3).broadcast_to([P, B, 4, C]), ALU.mult), "qx")
                    name(f"qx{u}", "qx")

                def project_vg(b, u):
                    M.wait("vg", "gyt")
                    mm(p_vg[:, :], xt_[u][:, b * P:(b + 1) * P], wvg[:, :], name=f"vg_made{u}")
                    V.wait(f"vg_made{u}", f"kv{u}", f"within{u}", f"gt{u}")
                    V(nc.vector.tensor_tensor(vg[u][:, b, :], p_vg[:, :], bvg[:, :], ALU.add), "vg")
                    name(f"vg{u}", "vg")

                def gates(u):
                    S.wait(f"vg{u}", f"gy{u}")
                    S(nc.scalar.activation(gt[u][:, :, :], vg[u][:, :, EV:2 * EV], ACT.Silu), f"gt{u}")

                def scores(b, u):
                    for s in range(2):
                        M.wait(f"qx{u}", "k_summed", f"decayed{s}")
                        mm(p_s[s][:, :], kr[u][s * 64:(s + 1) * 64, b, :], qx[u][s * 64:(s + 1) * 64, b, :, :].rearrange("p m c -> p (m c)"),
                           name="scores")
                        V.wait("scores", f"within_b{b}")
                        V(nc.vector.tensor_tensor(sm[b][:, 4 * s:4 * s + 4, :], view(p_s[s], 4, C), decay[:, 4 * s:4 * s + 4, :],
                                                  ALU.mult), f"decayed{s}")
                    name(f"sm{b}", "decayed1")

                def outputs(b, u):
                    M.wait(f"q2_{u}", "state_r", "og", f"sm{b}", f"vg{u}")
                    mm(p_out[:, b * EV:(b + 1) * EV], q2[u][:, b, :], state[:, b, :], stop=False, name="from_state")
                    for h in range(NH):
                        mm(p_out[:, b * EV + h * DV:b * EV + (h + 1) * DV], sm[b][:, h, :], vg[u][:, b, h * DV:(h + 1) * DV],
                           start=False, stop=h == NH - 1, name=f"within{u}")
                    name(f"within_b{b}", f"within{u}")

                def take_out(u):
                    S.wait(f"within{u}", f"gy{u}")
                    S(nc.scalar.activation(og[u][:, :, :].rearrange("p g v -> p (g v)"), p_out[:, :], ACT.Identity), "og")
                    name(f"og{u}", "og")

                def turn_k(u):
                    M.wait(f"k2_{u}", "xt_r", "k2t")
                    for b in range(B):
                        tr(p_turn[:, 256 + b * P:256 + (b + 1) * P], k2[u][:, b, :], "k2_turned")
                    S.wait("k2_turned", f"kv{u}")
                    S(nc.scalar.activation(k2t[u][:, :, :], view(p_turn, B, P, 256), ACT.Identity), "k2t")

                def update_state(u):
                    M.wait("k2t", f"vg{u}", "kv_in", "out_r")
                    for b in range(B):
                        mm(p_kv[:, b * EV:(b + 1) * EV], k2t[u][:, b, :], vg[u][:, b, 0:EV], name=f"kv{u}")
                    V.wait(f"kv{u}", "state_r")
                    V(nc.vector.tensor_tensor(inflow_[:, :, :], view(p_kv, B, EV), block[:, :].unsqueeze(1).broadcast_to([P, B, EV]),
                                              ALU.mult), "kv_in")
                    V.wait("kv_in", "from_state")
                    V(nc.vector.scalar_tensor_tensor(state[:, :, :], state[:, :, :], gam[:, 0:1], inflow_[:, :, :],
                                                     ALU.mult, ALU.add), "state_r")

                over_v = lambda v: v[:, :].unsqueeze(2).broadcast_to([P, B * NH, DV])
                def centre(u):
                    V.wait(f"og{u}")
                    V.wait(V(nc.vector.tensor_reduce(mu[:, :], og[u][:, :, :], AX.X, ALU.add)))
                    V.wait(V(nc.vector.tensor_scalar(mu[:, :], mu[:, :], 1.0 / DV, None, ALU.mult)))
                    V(nc.vector.tensor_tensor(og[u][:, :, :], og[u][:, :, :], over_v(mu), ALU.subtract), f"centred{u}")
                    S.wait(f"centred{u}", "rs_sum")
                    S(nc.scalar.activation(og2[:, :, :], og[u][:, :, :], ACT.Square), "og2")

                def spread_of(u):
                    V.wait("og2", "rs")
                    V(nc.vector.tensor_reduce(rs[:, :], og2[:, :, :], AX.X, ALU.add), "rs_sum")
                    S.wait("rs_sum")
                    S(nc.scalar.activation(rs[:, :], rs[:, :], ACT.Sqrt, bias=eps[:, 0:1], scale=1.0 / DV), "rs_root")

                def normed(u):
                    V.wait("rs_root")
                    V(nc.vector.reciprocal(rs[:, :], rs[:, :]), "rs")
                    V.wait("rs")
                    V(nc.vector.tensor_tensor(og[u][:, :, :], og[u][:, :, :], over_v(rs), ALU.mult), f"normed{u}")
                    G.wait(f"normed{u}", f"gt{u}", "gy_turned")
                    G(nc.gpsimd.tensor_tensor(gy[:, :], og[u][:, :, :].rearrange("p g v -> p (g v)"), gt[u][:, :, :].rearrange("p b v -> p (b v)"),
                                              ALU.mult), f"gy{u}")

                def turn_y(u):
                    M.wait(f"gy{u}", "vg", "gyt")
                    for j in range(4):
                        tr(p_vg[:, j * P:(j + 1) * P], gy[:, j * P:(j + 1) * P], "gy_turned")
                    S.wait("gy_turned", "out_made")
                    S(nc.scalar.activation(gyt[:, :], p_vg[:, :], ACT.Identity), "gyt")

                def project_out(c_, u):
                    M.wait("gyt", "kv_in", "out_r")
                    for b in range(B):
                        for j in range(2):
                            mm(p_kv[:, b * P:(b + 1) * P], gyt[:, (2 * b + j) * P:(2 * b + j + 1) * P], wp[:, j, :],
                               start=j == 0, stop=j == 1, name="out_made")
                    V.wait("out_made", "x1_bp")
                    res = by_batch(bx[:, :, :])[:, :, ds(c_, 1), :]
                    V(nc.vector.tensor_tensor(res, res, view(p_kv, B, P).unsqueeze(2), ALU.add), "out_r")

                def turn_of(c_, u, before_=True, after=True):
                    w_ = u ^ 1
                    scores(0, u)
                    if after:
                        turn_x(c_ + 1, w_)
                    if before_:
                        centre(w_)
                    scores(1, u)
                    if after:
                        project_qk(c_ + 1, w_)
                        rotate(c_ + 1, w_)
                    outputs(0, u)
                    if before_:
                        spread_of(w_)
                    turn_k(u)
                    if after:
                        project_vg(0, w_)
                    if before_:
                        normed(w_)
                    outputs(1, u)
                    take_out(u)
                    if after:
                        project_vg(1, w_)
                        gates(w_)
                        spread_q(w_)
                    update_state(u)
                    if before_:
                        turn_y(w_)
                        project_out(c_ - 1, w_)

                turn_x(0, 0)
                project_qk(0, 0)
                rotate(0, 0)
                project_vg(0, 0)
                project_vg(1, 0)
                gates(0)
                spread_q(0)
                turn_of(0, 0, before_=False)
                turn_of(1, 1)
                with c.loop(TB // 2 - 2) as ci:
                    turn_of(ci * 2 + 2, 0)
                    turn_of(ci * 2 + 3, 1)
                turn_of(TB - 2, 0)
                turn_of(TB - 1, 1, after=False)
                centre(1)
                spread_of(1)
                normed(1)
                turn_y(1)
                project_out(TB - 1, 1)
                barrier()

        layer0_mamba()
        experts(True, 0)
        layer1_retention()
        experts(False, 1)
        final()
        return c.per, c.later


def constants():
    k = {"ident": np.eye(P, dtype=np.float32), "mirror": np.eye(P, dtype=np.float32)[::-1]}
    k["keep"] = np.broadcast_to(np.array([0, 1, 0, 1] + [f[0] for f in FACTORS], np.float32), (P, 4 + len(FACTORS)))
    sel = np.zeros((96, 2 * NS, P), np.float32)
    for r in range(96):
        sel[r, r % 32, :] = 1.0
    k["sel"] = sel.astype(mybir.dt.np(BF16))
    k["before"] = np.triu(np.ones((P, P), np.float32), 1).astype(mybir.dt.np(BF16))
    k["every"] = np.ones((P, P), mybir.dt.np(BF16))
    run = np.ones((NE, NT), np.float32)
    run[:, 0] = 0.0
    row = np.concatenate([NE - np.arange(NE), run.reshape(-1), P * np.arange(NT), np.ones(NE), np.arange(ST + 2)])
    f32 = np.float32
    pos = np.arange(T, dtype=f32)
    scale = ((np.arange(0, D, 2, dtype=f32) + f32(0.4 * D)) / f32(1.4 * D))[:, None] ** (pos[None, :] / f32(512.0))
    angle = (f32(1.0) / f32(10000.0) ** (np.arange(D // 2, dtype=f32) / f32(D // 2)))[:, None] * pos[None, :]
    sin, cos, sign = np.sin(angle), np.cos(angle), np.tile(np.array([[-1], [1]], f32), (D // 2, 1))
    pairs = lambda v: np.repeat(v, 2, axis=0)
    gamma = 1.0 - np.exp(np.linspace(np.log(1 / 32), np.log(1 / 512), NH))
    log = np.log(gamma.astype(f32).astype(np.float64))
    decays = lambda n: np.exp(log[:, None] * n)
    norm = 1.0 / np.sqrt(np.cumsum(decays(np.arange(T)), axis=1)) * DK ** -0.5
    by_head = lambda v: np.repeat(v, DK, axis=0)
    k["rot"] = np.stack([pairs(cos * scale) * by_head(norm), pairs(sin * scale) * sign * by_head(norm),
                         pairs(cos / scale), pairs(sin / scale) * sign], 1).astype(f32)
    k["edge"] = np.stack([by_head(decays(np.arange(P) + 1)), by_head(decays(P - 1 - np.arange(P)))], 1).astype(f32)
    gap = np.arange(P)[None, :] - np.arange(P)[:, None]
    k["decay"] = (np.exp(log[None, :, None] * np.maximum(gap, 0)[:, None, :]) * (gap >= 0)[:, None, :]).astype(f32)
    k["heads4"] = (np.arange(P)[:, None] // DK % 4 == np.arange(4)).astype(f32)
    k["block"] = (np.arange(P)[:, None] // DK == np.arange(EV)[None, :] // DV).astype(f32)
    k["gam"] = by_head(decays(np.array([P]))).astype(f32)
    k["rc"] = np.broadcast_to(row.astype(np.float32), (P, RC_N))
    return k


def layout(x):
    x = {key: np.asarray(v) for key, v in x.items()}
    r = {"x": x["L0_attn_x"].reshape(NT, P, D).transpose(1, 0, 2)}
    r["lnp"] = np.stack([x["L0_attn_ln_g"], x["L0_attn_ln_b"]], 1)
    halves = lambda v: v.reshape(HF, P, -1).transpose(1, 0, 2).reshape(P, -1)
    in_u, conv, packed = [], [], []
    for d in "fb":
        g = lambda name: x[f"L0_attn_{d}_{name}"]
        in_u.append(g("in_w")[:DI].T)
        conv.append(np.broadcast_to(g("conv_w").T.reshape(TAPS * DI), (P, TAPS * DI)))
        bc = g("xproj_w")[RK:].T
        packed.append(np.concatenate([
            g("in_w")[DI:].T, halves(g("xproj_w")[:RK].T), halves(np.concatenate([bc, bc, bc], 1)),
            np.concatenate([g("dt_w").T, g("dt_w").T]), halves(g("out_w").T), halves(g("conv_b")),
            halves(g("dt_b")), halves(g("D")), halves(g("Alog"))], 1))
    r["in_u"], r["conv_w"], r["mamba_w"] = (np.stack(v, 1) for v in (in_u, conv, packed))
    rows = lambda v: v.reshape(*v.shape[:-2], FK, P, D).swapaxes(-3, -2).reshape(*v.shape[:-2], P, FK * D)
    f = lambda name: x["L0_ffn_" + name]
    r["rw0"] = f("router_w")
    r["shared_w"] = np.concatenate([f("shared_up_w"), f("shared_gate_w"), rows(f("shared_down_w"))], 1)
    r["l0_w"] = np.concatenate([f("up_w"), f("gate_w"), rows(f("down_w"))], 2).swapaxes(0, 1)
    f = lambda name: x["L1_attn_" + name]
    w_q, w_k, w_v = np.split(f("w_qkv"), (D, 2 * D), axis=1)
    b_q, b_k, b_v = np.split(f("b_qkv"), (D, 2 * D))
    pair = np.arange(D) ^ 1
    r["wqk"] = np.concatenate([w_q, w_q[:, pair], w_k, w_k[:, pair]], 1)
    r["bqk"] = np.stack([b_q, b_q[pair], b_k, b_k[pair]], 1)
    r["wvg"], r["bvg"] = np.concatenate([w_v, f("w_g")], 1), np.concatenate([b_v, f("b_g")])
    r["wp"], r["bp"] = f("w_p").reshape(2, P, D).swapaxes(0, 1), f("b_p")
    f = lambda name: x["L1_ffn_" + name]
    r["rw1"], r["br"], r["b2"] = f("Wr").T, f("br"), f("b2")
    r["l1_w"] = np.concatenate([f("W1").swapaxes(1, 2), rows(f("W2").swapaxes(1, 2))], 2).swapaxes(0, 1)
    r["b1"] = f("b1").reshape(NE, FK, P).transpose(2, 0, 1).reshape(P, NE * FK)
    return r


def kernel(**inputs):
    import concourse.bacc as bacc
    from concourse.bass_utils import run_bass_kernel_spmd

    arrays = {name: np.ascontiguousarray(v) for name, v in {**constants(), **layout(inputs)}.items()}
    known = ({}, {})
    for _ in range(2):
        nc = bacc.Bacc("TRN2", target_bir_lowering=False, num_devices=1)
        aps = {name: nc.dram_tensor("in_" + name, v.shape, mybir.dt.from_np(v.dtype), kind="ExternalInput").ap()
               for name, v in arrays.items()}
        out = nc.dram_tensor("out", (P, NT, D), F32, kind="ExternalOutput").ap()
        known = build(nc, known, aps, out)
    r = run_bass_kernel_spmd(nc, [{"in_" + name: v for name, v in arrays.items()}], core_ids=[0])
    return r.results[0]["out"].transpose(1, 0, 2).reshape(B, T, D)
```

```python
import concourse.bass as bass
from concourse import mybir
from contextlib import ExitStack, contextmanager
import numpy as np

F32, BF16, U32, I32 = mybir.dt.float32, mybir.dt.bfloat16, mybir.dt.uint32, mybir.dt.int32
ALU, ACT, AX = mybir.AluOpType, mybir.ActivationFunctionType, mybir.AxisListType
ds = bass.ds

P = 128
B, T, D = 2, 2048, 128
NT = B * T // P
TB = T // P
DI, NS, RK, TAPS = 256, 16, 64, 4
CH = 512
NCH = B * T // CH
HF = DI // P
FF, NE = 512, 8
FK = FF // P
ST = NT + NE
NH, DK, DV = 8, 16, 32
EV = NH * DV
EPS = 1e-5
SPREAD = 0.5186097621917725
FACTORS = ((0.5234627723693848, 0.29748213291168213), (-0.04265656694769859, 0.8761158585548401),
           (-0.7388817667961121, 0.7267470359802246), (-1.2040492296218872, 0.11629842966794968))

W_U = 0
W_Z = W_U + TAPS * DI
W_XD = W_Z + DI
W_XB = W_XD + HF * RK
W_DT = W_XB + HF * 96
W_O = W_DT + DI
W_CB = W_O + HF * D
W_DB = W_CB + HF
W_D = W_DB + HF
W_A = W_D + HF
W_N = W_A + HF * NS

RC_REV = 0
RC_RUN = RC_REV + NE
RC_MULT = RC_RUN + NE * NT
RC_ONE = RC_MULT + NT
RC_J = RC_ONE + NE
RC_N = RC_J + ST + 3


class Mark:
    def __init__(self, lane, at, loops):
        self.lane, self.at, self.loops = lane, at, loops


class Counts:
    START = 1 << 13

    def __init__(self, nc, known):
        self.nc, self.known, self.per, self.later = nc, known, {}, {}
        self.lanes, self.loops, self.n_loops, self.scopes = [], [], 0, [(None, {})]

    @contextmanager
    def loop(self, n):
        key = self.n_loops
        self.n_loops += 1
        before = [(l, l.at) for l in self.lanes]
        for l in self.lanes:
            l.waited = {}
        with self.nc.Fori(0, n, 1) as i:
            self.loops.append((key, i, n))
            self.scopes.append((key, {}))
            yield i
            self.loops.pop()
            _, names = self.scopes.pop()
        self.later.update({(key, name): mark for name, mark in names.items()})
        self.scopes[-1][1].update(names)
        for l, at in before:
            self.per[key, l.name] = l.at - at
            l.at = at + n * (l.at - at)
            l.waited = {}

    def named(self, name):
        found = []
        for key, names in reversed(self.scopes):
            if name in names:
                return found + [(names[name], None)]
            if (key, name) in self.known[1]:
                found.append((self.known[1][key, name], key))
        return found

    def value(self, mark, back):
        per = self.known[0]
        active = {key: i for key, i, _ in self.loops}
        value, terms = mark.at, []
        for key, n in mark.loops:
            m = per.get((key, mark.lane.name), 0)
            if key in active:
                terms += [(active[key], m)] if m else []
            else:
                value += (n - 1) * m
        if back is not None:
            value -= per.get((back, mark.lane.name), 0)
        return value, terms


class Lane:
    def __init__(self, c, name, engine, sem, step=1, start=Counts.START):
        self.c, self.name, self.e, self.sem, self.step = c, name, engine, sem, step
        self.at = self.start = start
        self.waited = {}
        c.lanes.append(self)

    def __call__(self, ins, name=None):
        ins.then_inc(self.sem, self.step)
        self.at += self.step
        m = Mark(self, self.at, [(k, n) for k, _, n in self.c.loops])
        if name:
            self.c.scopes[-1][1][name] = m
        return m

    def wait(self, *marks):
        for m in marks:
            for mark, back in (self.c.named(m) if isinstance(m, str) else [(m, None)]):
                value, terms = self.c.value(mark, back)
                key = (mark.lane.name, tuple(per for _, per in terms))
                if self.waited.get(key, -1) >= value:
                    continue
                self.waited[key] = value
                for i, per in terms:
                    value = value + i * per
                self.e.wait_ge(next(l.sem for l in self.c.lanes if l.name == mark.lane.name), value)


def build(nc, known, a, out):
    c = Counts(nc, known)
    ctx = ExitStack()

    def lane(name, engine, step=1, start=Counts.START):
        l = Lane(c, name, engine, ctx.enter_context(nc.semaphore("s_" + name)), step, start)
        if start:
            engine.sem_inc(l.sem, start)
        return l

    with ctx:
        V = lane("vector", nc.vector)
        S = lane("scalar", nc.scalar)
        G = lane("gpsimd", nc.gpsimd)
        M = lane("tensor", nc.tensor)
        L = {k: lane("load_" + k, nc.sync, 16) for k in ("x", "zero", "mamba", "w", "const")}
        L["out"] = lane("store_out", nc.sync, 16)
        SY = Lane(c, "sync", nc.sync, None)

        def name(new, old):
            c.scopes[-1][1][new] = c.scopes[-1][1][old]

        def barrier():
            now = [Mark(l, l.at, []) for l in c.lanes if l.at > l.start]
            for w in (V, S, G, M, SY):
                w.wait(*now)

        used = {}

        def unused(name):
            used[name] = used.get(name, 0) + 1
            return name if used[name] == 1 else f"{name}_{used[name]}"

        def sb(scope, name, shape, dt=F32):
            return scope.enter_context(nc.sbuf_tensor(unused(name), shape, dt))

        def bank(scope, name, n=1):
            return scope.enter_context(nc.psum_tensor(unused(name), [P, n * 512], F32))

        def flat(t):
            return t.rearrange("p a c -> p (a c)")

        def view(t, n, w, off=0):
            return t[:, off:off + n * w].rearrange("p (n w) -> p n w", n=n)

        def mm(out, lhsT, rhs, start=True, stop=True, name=None, inc=True):
            i = nc.tensor.matmul(out, lhsT, rhs, start=start, stop=stop)
            return M(i, name) if inc else None

        def tr(out, in_, name=None, inc=True):
            i = nc.tensor.transpose(out, in_, ident[:, :])
            return M(i, name) if inc else None

        bx = sb(ctx, "residual", [P, NT, D])
        ident = sb(ctx, "ident", [P, P])
        mirror = sb(ctx, "mirror", [P, P])
        eps = sb(ctx, "eps", [P, 1])
        zeros = sb(ctx, "zeros", [P, D])
        mean = sb(ctx, "mean", [P, NT])
        rstd = sb(ctx, "rstd", [P, NT])
        xsorted = nc.dram_tensor("xsorted", (ST * P, D), F32, kind="Internal").ap()
        ysorted = nc.dram_tensor("ysorted", (ST * P, D), F32, kind="Internal").ap()

        for k in range(4):
            n = NT // 4
            in_x = L["x"](nc.sync.dma_start(bx[:, k * n:(k + 1) * n, :], a["x"][:, k * n:(k + 1) * n, :]))
        L["const"](nc.sync.dma_start(ident[:, :], a["ident"]))
        in_c = L["const"](nc.sync.dma_start(mirror[:, :], a["mirror"]))
        h_eps = V(nc.vector.memset(eps[:, :], EPS))

        SY.wait(V(nc.vector.memset(zeros[:, :], 0.0)))
        for s in range(4):
            t = slice(s * ST // 4, (s + 1) * ST // 4)
            L["zero"](nc.sync.dma_start(xsorted.rearrange("(t p) d -> p t d", p=P)[:, t, :],
                                        zeros[:, :].unsqueeze(1).broadcast_to([P, ST // 4, D])), "zeroed")

        def normalise_stats(cen, sq, ready):
            V.wait(ready)
            h = V(nc.vector.tensor_reduce(mean[:, :], bx[:, :, :], AX.X, ALU.add))
            V.wait(h)
            h = V(nc.vector.tensor_scalar(mean[:, :], mean[:, :], 1.0 / D, None, ALU.mult))
            V.wait(h)
            n = NT // 4
            for k in range(4):
                t = slice(k * n, (k + 1) * n)
                h = V(nc.vector.tensor_tensor(cen[:, t, :], bx[:, t, :],
                                              mean[:, t].unsqueeze(2).broadcast_to([P, n, D]), ALU.subtract))
                S.wait(h, ready)
                hs = S(nc.scalar.activation(sq[:, t, :], cen[:, t, :], ACT.Square))
                V.wait(hs)
                h = V(nc.vector.tensor_reduce(rstd[:, t], sq[:, t, :], AX.X, ALU.add))
            S.wait(h, h_eps)
            h = S(nc.scalar.activation(rstd[:, :], rstd[:, :], ACT.Sqrt, bias=eps[:, 0:1], scale=1.0 / D))
            V.wait(h)
            return V(nc.vector.reciprocal(rstd[:, :], rstd[:, :]), "rstd")

        def layer0_mamba():
            with ExitStack() as k:
                xt = sb(k, "xt", [P, 2 * NCH + 2, TAPS - 1 + CH])
                om = sb(k, "om", [P, 2 * (NCH + 1), CH])
                wd = [sb(k, f"w{i}", [P, W_N]) for i in range(2)]
                lnp = sb(k, "lnp", [P, 2])
                keep = sb(k, "keep", [P, NCH + len(FACTORS)])
                sel = sb(k, "sel", [P, 2 * NS], BF16)
                with ExitStack() as k0:
                    xs = sb(k0, "xs", [P, B, D])
                    pt = [bank(k0, f"pt{u}") for u in range(B)]
                    cen = om[:, 0:8, :].rearrange("p a (b d) -> p (a b) d", d=D)
                    sq = om[:, 8:16, :].rearrange("p a (b d) -> p (a b) d", d=D)
                    L["mamba"](nc.sync.dma_start(lnp[:, :], a["lnp"]))
                    L["mamba"](nc.sync.dma_start(keep[:, :], a["keep"]))
                    in_w = L["mamba"](nc.sync.dma_start(sel[0:96, :], a["sel"]))
                    normalise_stats(cen, sq, in_x)
                    G(nc.gpsimd.memset(xt[:, 2 * NCH:2 * NCH + 2, :], 0.0), "xt_end")
                    M.wait(in_c)
                    S.wait(in_w)
                    V.wait("rstd")
                    with c.loop(TB // 4) as ci:
                        for kt in range(4):
                            for u in range(B):
                                tile = ci * 4 + (u * TB + kt)
                                V.wait(f"mirrored{u}")
                                V(nc.vector.tensor_scalar(xs[:, u, :], flat(cen[:, ds(tile, 1), :]),
                                                          rstd[:, ds(tile, 1)], None, ALU.mult), f"xs{u}")
                                M.wait(f"xs{u}", f"xt{u}")
                                nc.tensor.matmul(pt[u][:, 0:P], xs[:, u, :], ident[:, :], start=True, stop=True)
                                mm(pt[u][:, P:2 * P], xs[:, u, :], mirror[:, :], name=f"mirrored{u}")
                                S.wait(f"mirrored{u}")
                                col = TAPS - 1 + kt * P
                                S(nc.scalar.activation(flat(xt[:, ds(ci + u * 4, 1), col:col + P]), pt[u][:, 0:P],
                                                       ACT.Identity, bias=lnp[:, 1:2], scale=lnp[:, 0:1]))
                                col = TAPS - 1 + (3 - kt) * P
                                S(nc.scalar.activation(flat(xt[:, ds((NCH + u * 4 + 3) - ci, 1), col:col + P]), pt[u][:, P:2 * P],
                                                       ACT.Identity, bias=lnp[:, 1:2], scale=lnp[:, 0:1]), f"xt{u}")
                    V.wait("xt0", "xt1", "xt_end")
                    V.wait(V(nc.vector.tensor_copy(xt[:, 1:2 * NCH + 1, 0:3], xt[:, 0:2 * NCH, CH:CH + 3])))
                    V(nc.vector.memset(xt[:, 0:2 * NCH + 1:4, 0:3], 0.0))
                    barrier()

                pre = sb(k, "pre", [P, 4, CH])
                uz = [sb(k, f"uz{i}", [P, 4, CH]) for i in range(2)]
                dtr = sb(k, "dtr", [RK, CH])
                mid = sb(k, "mid", [P, CH], BF16)
                bc = [sb(k, f"bc{i}", [P, CH], BF16) for i in range(2)]
                ab = sb(k, "ab", [P, HF, CH])
                rx = sb(k, "rx", [P, HF, CH])
                rest = sb(k, "rest", [P, CH])
                dt = [sb(k, f"dt{i}", [P, HF, CH]) for i in range(2)]
                dtu = [sb(k, f"dtu{i}", [P, HF, CH]) for i in range(2)]
                db = [sb(k, f"db{i}", [P, HF, CH]) for i in range(2)]
                yz, sq0, sq1, hh4 = [bx[:, s * 8:s * 8 + 8, :].rearrange("p (h a) d -> p h (a d)", h=HF) for s in range(4)]
                sq = (sq0, sq1)
                hh = [sb(k, f"hh{i}", [P, HF, CH]) for i in range(4)] + [hh4]
                hc = [sb(k, f"hc{i}", [P, HF, CH]) for i in range(3)]
                cs = [sb(k, f"cs{i}", [P, CH]) for i in range(3)]
                st = sb(k, "st", [P, 2, NS, HF])
                py = bank(k, "py", 2)
                pb = [bank(k, f"pb{i}") for i in range(2)]
                pc = [bank(k, f"pc{i}") for i in range(2)]
                pq = [bank(k, f"pq{i}") for i in range(2)]

                def prep(i, slot, next_slot, before=[], only_u=False):
                    def project(j, col, taps=(TAPS - 1,), last=True):
                        M.wait("w", f"pq{j % 2}_empty")
                        at, w = (next_slot, wd[i ^ 1]) if j < HF else (slot, wd[i])
                        for t in taps:
                            m = nc.tensor.matmul(pq[j % 2][:, :], w[:, col:col + P] if j >= HF else w[:, col + t * DI:col + t * DI + P],
                                                 flat(xt[:, ds(at, 1), t:t + CH]), start=t == taps[0] and (j >= HF or t == 0),
                                                 stop=t == TAPS - 1)
                        M(m, f"pq{j % 2}")

                    def keep_pre(j):
                        S.wait(f"pq{j % 2}", "w", "uz0", "uz1")
                        bias = wd[i ^ 1][:, W_CB + j:W_CB + j + 1] if j < HF else 0.0
                        S(nc.scalar.activation(pre[:, j, :], pq[j % 2][:, :], ACT.Identity, bias=bias), f"pre{j}")
                        name(f"pq{j % 2}_empty", f"pre{j}")

                    def silu():
                        S.wait("pre0", "pre1", "pre3", f"gated{i}", f"dtu{i}")
                        S(nc.scalar.activation(uz[i][:, :, :], pre[:, :, :], ACT.Silu), f"uz{i}")

                    def rank():
                        M.wait(f"uz{i}", "pq0_empty")
                        for h in range(HF):
                            mm(pq[0][0:RK, :], wd[i][:, W_XD + h * RK:W_XD + (h + 1) * RK], uz[i][:, h, :],
                               start=h == 0, stop=h == HF - 1, name="pq0")

                    def keep_rank():
                        S.wait("pq0", "dt_in1")
                        S(nc.scalar.activation(dtr[:, :], pq[0][0:RK, :], ACT.Identity), "dtr")
                        name("pq0_empty", "dtr")

                    def b_c():
                        M.wait(f"uz{i}", "pq1_empty")
                        for h in range(HF):
                            mm(pq[1][0:96, :], wd[i][:, W_XB + h * 96:W_XB + (h + 1) * 96], uz[i][:, h, :],
                               start=h == 0, stop=h == HF - 1, name="pq1")

                    def high_part():
                        V.wait("pq1", f"c_read{i}", f"b_read{i}")
                        V.wait(V(nc.vector.tensor_copy(bc[i][0:96, :], pq[1][0:96, :])), "mid_low")
                        V.wait(V(nc.vector.tensor_tensor(rest[0:96, :], pq[1][0:96, :], bc[i][0:96, :], ALU.subtract), "pq1_empty"))
                        V(nc.vector.tensor_copy(mid[0:96, :], rest[0:96, :]), "mid")

                    def mid_low_parts():
                        V.wait("mid")
                        V(nc.vector.tensor_tensor(bc[i][64:96, :], rest[64:96, :], mid[64:96, :], ALU.subtract))
                        V(nc.vector.tensor_copy(bc[i][32:64, :], mid[32:64, :]), f"bc{i}")
                        name("mid_low", f"bc{i}")

                    def dt_in(h):
                        M.wait("dtr", f"pq{1 - h}_empty")
                        mm(pq[1 - h][:, :], wd[i][0:RK, W_DT + h * P:W_DT + (h + 1) * P], dtr[:, :], name=f"dt_in{h}")

                    def relu_abs(h):
                        bias = wd[i][:, W_DB + h:W_DB + h + 1]
                        S.wait(f"dt_in{h}", "softplus", "factor")
                        S(nc.scalar.activation(rx[:, h, :], pq[1 - h][:, :], ACT.Relu, bias=bias), "rx")
                        S(nc.scalar.activation(ab[:, h, :], pq[1 - h][:, :], ACT.Abs, bias=bias), "abs")
                        name(f"pq{1 - h}_empty", "abs")

                    def exponent():
                        S.wait("abs")
                        S(nc.scalar.activation(ab[:, :, :], ab[:, :, :], ACT.Exp, scale=-1.0), "e")

                    def square(f):
                        S.wait("e", f"factor{f % 2}")
                        S(nc.scalar.activation(sq[f % 2][:, :, :], ab[:, :, :], ACT.Square, scale=SPREAD,
                                               bias=keep[:, NCH + f:NCH + f + 1]), f"square{f % 2}")

                    def factor(f):
                        V.wait(f"square{f % 2}", "factor", f"da{i}")
                        V(nc.vector.scalar_tensor_tensor(dt[i][:, :, :], sq[f % 2][:, :, :], FACTORS[f][1],
                                                         ab[:, :, :] if f == 0 else dt[i][:, :, :], ALU.add, ALU.mult), "factor")
                        name(f"factor{f % 2}", "factor")

                    def finish():
                        V.wait("factor", "rx")
                        V(nc.vector.tensor_tensor(dt[i][:, :, :], rx[:, :, :], dt[i][:, :, :], ALU.add), f"dt{i}")
                        name("softplus", f"dt{i}")
                        G.wait(f"dt{i}", f"uz{i}", f"dtu_read{i}")
                        G(nc.gpsimd.tensor_tensor(dtu[i][:, :, :], dt[i][:, :, :], uz[i][:, 0:HF, :], ALU.mult), f"dtu{i}")

                    def of(stage, *args):
                        return lambda: stage(*args)

                    next_u = [[]] * 11 + [
                        [of(project, 0, W_U, (0, 1))], [of(project, 0, W_U, (2, 3))],
                        [of(keep_pre, 0), of(project, 1, W_U + P, (0, 1))], [of(project, 1, W_U + P, (2, 3))],
                        [of(keep_pre, 1)]]
                    if only_u:
                        return next_u
                    rest_ = [[of(project, 2, W_Z)],
                            [of(keep_pre, 2), of(project, 3, W_Z + P)],
                            [of(keep_pre, 3)],
                            [silu, rank],
                            [keep_rank, of(dt_in, 0)],
                            [of(relu_abs, 0), of(dt_in, 1)],
                            [of(relu_abs, 1), exponent, of(square, 0), b_c],
                            [high_part, mid_low_parts, of(square, 1)],
                            [of(factor, 0)] + before[0:1],
                            [of(square, 2), of(factor, 1)] + before[1:2],
                            [of(square, 3), of(factor, 2)] + before[2:3],
                            [of(factor, 3)], [finish]] + [[]] * 3
                    return [x + y for x, y in zip(rest_, next_u)]

                def gate(j):
                    V.wait("summed", "projected", "w")
                    for h in range(HF):
                        V(nc.vector.scalar_tensor_tensor(yz[:, h, :], uz[j][:, h, :], wd[j][:, W_D + h:W_D + h + 1],
                                                         py[:, h * CH:(h + 1) * CH], ALU.mult, ALU.add), "py_empty")
                    G.wait("py_empty")
                    G(nc.gpsimd.tensor_tensor(yz[:, :, :], yz[:, :, :], uz[j][:, HF:2 * HF, :], ALU.mult), f"gated{j}")

                def out_project(j, slot):
                    def tiles(of):
                        M.wait(f"gated{j}", "pq0_empty")
                        for kt in of:
                            for h in range(HF):
                                mm(pq[0][:, kt * P:(kt + 1) * P], yz[:, h, kt * P:(kt + 1) * P], wd[j][:, W_O + h * D:W_O + (h + 1) * D],
                                   start=h == 0, stop=h == HF - 1, name="projected")

                    def store():
                        S.wait("projected")
                        S(nc.scalar.activation(flat(om[:, ds(slot, 1), :]), pq[0][:, :], ACT.Identity), "pq0_empty")
                    return [lambda: tiles((0, 1)), lambda: tiles((2, 3)), store]

                def add_up(n, b):
                    M.wait(f"hc{b}", "py_empty")
                    for h in range(HF):
                        mm(py[:, h * CH:(h + 1) * CH], ident[:, :], hc[b][:, h, :], start=n == 0, stop=n == NS - 1, name=f"summed{b}")
                    if n == NS - 1:
                        name("summed", f"summed{b}")

                def spread_b(n, i):
                    M.wait(f"bc{i}", f"db{n % 2}")
                    mm(pb[n % 2][:, :], sel[0:96, n:n + 1].broadcast_to([96, P]), bc[i][0:96, :], name=f"b{n % 2}")
                    name(f"b_read{i}", f"b{n % 2}")

                def spread_c(n, i):
                    M.wait(f"bc{i}", f"c_copied{n % 2}")
                    mm(pc[n % 2][:, :], sel[0:96, NS + n:NS + n + 1].broadcast_to([96, P]), bc[i][0:96, :], name=f"c_read{i}")
                    name(f"c{n % 2}", f"c_read{i}")

                def inflow(n, i):
                    b = n % 2
                    V.wait(f"b{b}", f"dtu{i}", f"scans{b}")
                    V(nc.vector.tensor_tensor(db[b][:, :, :], dtu[i][:, :, :], pb[b][:, :].unsqueeze(1).broadcast_to([P, HF, CH]),
                                              ALU.mult), f"db{b}")
                    name(f"dtu_read{i}", f"db{b}")

                def decays(n, i):
                    r = (i * NS + n) % 5
                    S.wait(f"dt{i}", "w", f"state{r}")
                    for h in range(HF):
                        S(nc.scalar.activation(hh[r][:, h, :], dt[i][:, h, :], ACT.Exp,
                                               scale=wd[i][:, W_A + h * NS + n:W_A + h * NS + n + 1]), f"da{i}")
                        name(f"a{r}{h}", f"da{i}")

                def copy_c(n, i):
                    r = (i * NS + n) % 3
                    S.wait(f"c{n % 2}", f"hc{r}")
                    S(nc.scalar.activation(cs[r][:, :], pc[n % 2][:, :], ACT.Identity), "cs")
                    name(f"cs{r}", "cs")
                    name(f"c_copied{n % 2}", "cs")

                def scan_step(n, i, meanwhile):
                    b, r, m = n % 2, (i * NS + n) % 5, (i * NS + n) % 3
                    ahead = lambda k: ((n + k) % NS, i if n + k < NS else i ^ 1)
                    decays(*ahead(1))
                    copy_c(*ahead(1))
                    inflow(*ahead(1))
                    spread_c(*ahead(2))
                    spread_b(*ahead(2))
                    V.wait(f"db{b}")
                    for h in range(HF):
                        V.wait(f"a{r}{h}")
                        V(nc.vector.tensor_tensor_scan(hh[r][:, h, :], hh[r][:, h, :], db[b][:, h, :], st[:, i, n, h:h + 1],
                                                       ALU.mult, ALU.add), f"scan{r}")
                    name(f"scans{b}", f"scan{r}")
                    if n == 2:
                        gate(i ^ 1)
                    if n == 3:
                        add_up(0, (i * NS) % 3)
                    if n != 2:
                        add_up((n - 2) % NS, (i * NS + n - 2) % (2 * NS) % 3)
                    G.wait(f"scan{r}", f"cs{m}", f"summed{m}")
                    G(nc.gpsimd.tensor_tensor(hc[m][:, :, :], hh[r][:, :, :], cs[m][:, :].unsqueeze(1).broadcast_to([P, HF, CH]),
                                              ALU.mult), f"hc{m}")
                    G(nc.gpsimd.tensor_copy(st[:, i, n, :], hh[r][:, :, CH - 1]), f"state{r}")
                    for work in meanwhile:
                        work()

                V(nc.vector.memset(uz[1][:, :, :], 0.0), "uz1")
                V(nc.vector.memset(st[:, :, :, :], 0.0), "st")
                V.wait("uz1", "st")
                for i, w in enumerate(wd):
                    conv = (pre, uz[0])[i]
                    load = lane(f"load_w{i}", nc.sync, 16)
                    load(nc.sync.dma_start(conv[:, 0:2, :], a["conv_w"][:, i, :]))
                    load(nc.sync.dma_start(conv[:, 2, 0:DI], a["in_u"][:, i, :]))
                    in_w = load(nc.sync.dma_start(w[:, W_Z:W_N], a["mamba_w"][:, i, :]))
                    V.wait(in_w)
                    V(nc.vector.tensor_tensor(view(w, TAPS, DI), conv[:, 0:2, :].rearrange("p a (t d) -> p (a t) d", d=DI),
                                              conv[:, 2, 0:DI].unsqueeze(1).broadcast_to([P, TAPS, DI]), ALU.mult))
                    S.wait(in_w)
                    V.wait(S(nc.scalar.activation(w[:, W_A:W_N], w[:, W_A:W_N], ACT.Exp)))
                    V(nc.vector.tensor_scalar(w[:, W_A:W_N], w[:, W_A:W_N], -1.0, None, ALU.mult), "w")
                M.wait("w")
                S.wait("w")
                for works in prep(1, 0, 0, only_u=True) + prep(0, 0, NCH):
                    for work in works:
                        work()
                for step in (2 * NS - 2, 2 * NS - 1):
                    b = step % 3
                    V(nc.vector.memset(hc[b][:, :, :], 0.0), f"hc{b}")
                add_up(0, (2 * NS - 2) % 3)
                spread_b(0, 0)
                spread_c(0, 0)
                decays(0, 0)
                copy_c(0, 0)
                inflow(0, 0)
                spread_b(1, 0)
                spread_c(1, 0)
                with c.loop(NCH) as q:
                    V.wait("state0", "state1", "state2", "state3", "state4")
                    V.wait(V(nc.vector.tensor_scalar(st[:, :, :, :], st[:, :, :, :], keep[:, ds(q, 1)], None, ALU.mult)))
                    first = prep(1, q + NCH, q + 1, out_project(1, q + (NCH + 1)))
                    second = prep(0, q + 1, q + (NCH + 1), out_project(0, q + 1))
                    for i, steps in enumerate((first, second)):
                        for n in range(NS):
                            scan_step(n, i, steps[n])
                add_up(NS - 2, (2 * NS - 2) % 3)
                add_up(NS - 1, (2 * NS - 1) % 3)
                gate(1)
                for work in out_project(1, 2 * NCH + 1):
                    work()

                barrier()
                again = [lane(f"load_x_again{s}", nc.sync, 16)(nc.sync.dma_start(bx[:, s * 8:s * 8 + 8, :], a["x"][:, s * 8:s * 8 + 8, :]))
                         for s in range(4)]
                for g in (2, 3, 0, 1, 6, 7, 4, 5):
                    bnk = (pb[0], pb[1], pc[0], pq[0])[g % 4]
                    M.wait(f"turned{g % 4}")
                    mm(bnk[:, :], mirror[:, :], om[:, NCH + 2 + g, :], name="turned")
                    t = (g // 4) * TB + (3 - g % 4) * 4
                    V.wait(again[t // 8])
                    V.wait(V(nc.vector.scalar_tensor_tensor(bx[:, t:t + 4, :], bx[:, t:t + 4, :], 2.0,
                                                            view(om[:, 1 + t // 4, :], 4, D), ALU.mult, ALU.add)), "turned")
                    for kt in range(4):
                        V(nc.vector.tensor_tensor(bx[:, t + 3 - kt, :], bx[:, t + 3 - kt, :], bnk[:, kt * P:(kt + 1) * P], ALU.add),
                          f"turned{g % 4}")
                barrier()

        def final():
            with ExitStack() as k:
                cen = sb(k, "cen", [P, NT, D])
                sq = sb(k, "sq_last", [P, NT, D])
                normalise_stats(cen, sq, in_x)
                V.wait("rstd")
                n = NT // 4
                for s in range(4):
                    t = slice(s * n, (s + 1) * n)
                    V(nc.vector.tensor_tensor(cen[:, t, :], cen[:, t, :], rstd[:, t].unsqueeze(2).broadcast_to([P, n, D]),
                                              ALU.mult), "x_out")
                    SY.wait("x_out")
                    L["out"](nc.sync.dma_start(out[:, t, :], cen[:, t, :]))
                SY.wait(Mark(L["out"], L["out"].at, []))

        def experts(glu, layer):
            with ExitStack() as k:
                small, shared, weights, sorted_x = [lane(f"load{layer}_{s}", nc.sync, 16) for s in ("small", "shared", "weights", "sorted_x")]
                scatter = lane(f"scatter{layer}", nc.gpsimd, 16, 0)
                store_y = lane(f"store{layer}_sorted_y", nc.sync, 16)
                gather = [lane(f"gather{layer}_{s}", nc.gpsimd, 16, 0) for s in range(4)]
                q = (2 if glu else 1) * FF
                x1 = sb(k, "x1", [P, NT, D])
                xsort = sb(k, "xsort", [P, ST + 3, D])
                ysort = sb(k, "ysort", [P, ST, D])
                back = ysort[:, 0:NT, :]
                wx = sb(k, "wx", [P, NE, q + FF])
                rc = sb(k, "rc", [P, RC_N])
                before = sb(k, "before", [P, P], BF16)
                every = sb(k, "every", [P, P], BF16)
                rw = sb(k, "rw", [P, NE])
                lg = sb(k, "lg", [P, NT, NE])
                hot = sb(k, "hot", [P, NT, NE])
                hot_b = sb(k, "hot_b", [P, NT, NE], BF16)
                work_ = sb(k, "work", [P, NT, NE])
                incl = sb(k, "incl", [P, NE, NT])
                tot = sb(k, "tot", [P, NE, NT])
                top = sb(k, "top", [P, NT])
                factor2 = sb(k, "factor2", [P, NT])
                tiles_of = sb(k, "tiles_of", [P, NE])
                ends = sb(k, "ends", [P, NE])
                cmp_ = sb(k, "cmp", [P, ST + 3, NE])
                exf = sb(k, "exf", [P, ST + 3])
                expert = sb(k, "expert", [P, ST + 3], I32)
                pos = sb(k, "pos", [P, NT], U32)
                xs4 = [sb(k, f"xs4{u}", [P, 4, D]) for u in range(2)]
                xt4 = [sb(k, f"xt4{u}", [P, 4 * P]) for u in range(2)]
                sg = [sb(k, f"sg{u}", [P, FF]) for u in range(2)]
                hid = [sb(k, f"hid{u}", [P, FF]) for u in range(2)]
                ht = [sb(k, f"ht{u}", [P, FF]) for u in range(2)]
                pbk = [bank(k, f"bank{u}") for u in range(8)]
                pt, pl, pu, pg, pw = pbk[0:2], pbk[2], pbk[3:5], pbk[5:7], pbk[7]
                if glu:
                    xall = sb(k, "xall", [P, NT * P])
                    ws = sb(k, "ws", [P, 3 * FF])
                    ht4 = [sb(k, f"ht4{u}", [P, 4 * P]) for u in range(2)]
                else:
                    brb = sb(k, "brb", [P, NE])
                    b1 = sb(k, "b1", [P, NE * FK])
                    b2 = sb(k, "b2", [P, NE, D])

                small(nc.sync.dma_start(rw[:, :], a[f"rw{layer}"]))
                small(nc.sync.dma_start(before[:, :], a["before"]))
                small(nc.sync.dma_start(every[:, :], a["every"]))
                if not glu:
                    small(nc.sync.dma_start(brb[:, :], a["br"].partition_broadcast(P)))
                    small(nc.sync.dma_start(b1[:, :], a["b1"]))
                    small(nc.sync.dma_start(b2[:, :, :], a["b2"].partition_broadcast(P)))
                in_r = small(nc.sync.dma_start(rc[:, :], a["rc"]))
                if glu:
                    in_s = shared(nc.sync.dma_start(ws[:, :], a["shared_w"]))
                    no_expert = V(nc.vector.memset(wx[:, NE - 1:NE, :], 0.0))
                else:
                    no_expert = in_r
                last = NE - 1 if glu else NE
                weights(nc.sync.dma_start(wx[:, 0:4, :], a[f"l{layer}_w"][:, 0:4, :]))
                in_e = weights(nc.sync.dma_start(wx[:, 4:last, :], a[f"l{layer}_w"][:, 4:last, :]))
                V(nc.vector.memset(xsort[:, ST:ST + 3, :], 0.0), "xsort_end")

                normalise_stats(x1, back, in_r)
                V.wait("rstd")
                for s in range(4):
                    t = slice(s * NT // 4, (s + 1) * NT // 4)
                    V(nc.vector.tensor_tensor(x1[:, t, :], x1[:, t, :], rstd[:, t].unsqueeze(2).broadcast_to([P, NT // 4, D]),
                                              ALU.mult), "x1")

                def transpose_x(g, u):
                    V.wait("x1", f"xs4_read{u}")
                    V(nc.vector.tensor_copy(xs4[u][:, :, :], x1[:, ds(g * 4, 4), :]), f"xs4{u}")
                    M.wait(f"xs4{u}", f"xt4{u}")
                    for kt in range(4):
                        tr(pt[u][:, kt * P:(kt + 1) * P], xs4[u][:, kt, :], f"xs4_read{u}")
                    S.wait(f"xs4_read{u}", f"logits{u}")
                    S(nc.scalar.activation(xt4[u][:, :], pt[u][:, :], ACT.Identity), f"xt4{u}")
                    if glu:
                        S.wait(f"xt4{u}")
                        S(nc.scalar.activation(xall[:, ds(g * (4 * P), 4 * P)], xt4[u][:, :], ACT.Identity), "xall")

                def logits(g, u):
                    M.wait(f"xt4{u}", f"lg{u}", in_r)
                    for kt in range(4):
                        mm(pg[u][:, kt * NE:(kt + 1) * NE], xt4[u][:, kt * P:(kt + 1) * P], rw[:, :], name=f"logits{u}")
                    V.wait(f"logits{u}")
                    if glu:
                        V(nc.vector.tensor_copy(lg[:, ds(g * 4, 4), :], view(pg[u], 4, NE)), f"lg{u}")
                    else:
                        V(nc.vector.tensor_tensor(lg[:, ds(g * 4, 4), :], view(pg[u], 4, NE),
                                                  brb[:, :].unsqueeze(1).broadcast_to([P, 4, NE]), ALU.add), f"lg{u}")

                M.wait(in_c)
                with c.loop(NT // 8) as gi:
                    transpose_x(gi * 2, 0)
                    transpose_x(gi * 2 + 1, 1)
                    logits(gi * 2, 0)
                    logits(gi * 2 + 1, 1)

                def step(ins, name=None):
                    V.wait(V(ins, name))
                over_e = lambda v: v.unsqueeze(2).broadcast_to([P, NT, NE])
                V.wait("lg0", "lg1", in_r)
                step(nc.vector.tensor_reduce(top[:, :], lg[:, :, :], AX.X, ALU.max))
                step(nc.vector.tensor_tensor(lg[:, :, :], lg[:, :, :], over_e(top[:, :]), ALU.subtract), "shifted")
                if glu:
                    S.wait("shifted")
                    S(nc.scalar.activation(work_[:, :, :], lg[:, :, :], ACT.Exp), "exps")
                step(nc.vector.tensor_scalar(hot[:, :, :], lg[:, :, :], 0.0, None, ALU.is_ge))
                step(nc.vector.tensor_tensor(hot[:, :, :], hot[:, :, :], rc[:, RC_REV:RC_REV + NE].unsqueeze(1).broadcast_to([P, NT, NE]),
                                             ALU.mult))
                step(nc.vector.tensor_reduce(top[:, :], hot[:, :, :], AX.X, ALU.max))
                step(nc.vector.tensor_tensor(hot[:, :, :], hot[:, :, :], over_e(top[:, :]), ALU.is_equal))
                step(nc.vector.tensor_copy(hot_b[:, :, :], hot[:, :, :]), "hot_b")
                M.wait("hot_b")
                mm(pg[0][:, 0:NT * NE], before[:, :], flat(hot_b[:, :, :]))
                mm(pg[1][:, 0:NT * NE], every[:, :], flat(hot_b[:, :, :]), name="ranks")
                if glu:
                    V.wait("exps")
                    step(nc.vector.tensor_reduce(factor2[:, :], work_[:, :, :], AX.X, ALU.add))
                    step(nc.vector.reciprocal(factor2[:, :], factor2[:, :]))
                    step(nc.vector.tensor_scalar(factor2[:, :], factor2[:, :], 2.0, None, ALU.mult), "factor2")
                V.wait("ranks")
                step(nc.vector.tensor_copy(tot[:, :, :], view(pg[1], NT, NE).rearrange("p t e -> p e t")))
                step(nc.vector.tensor_tensor_scan(flat(incl[:, :, :]), rc[:, RC_RUN:RC_RUN + NE * NT], flat(tot[:, :, :]), 0.0,
                                                  ALU.mult, ALU.add))
                step(nc.vector.tensor_tensor(tot[:, :, :], incl[:, :, :], tot[:, :, :], ALU.subtract))
                step(nc.vector.tensor_tensor(work_[:, :, :].rearrange("p t e -> p (t e)").rearrange("p (e m) -> p e m", e=NE),
                                             incl[:, :, NT - 1:NT].broadcast_to([P, NE, NT]),
                                             rc[:, RC_MULT:RC_MULT + NT].unsqueeze(1).broadcast_to([P, NE, NT]), ALU.is_gt))
                step(nc.vector.tensor_reduce(tiles_of[:, :], work_[:, :, :].rearrange("p t e -> p (t e)").rearrange("p (e m) -> p e m", e=NE),
                                             AX.X, ALU.add))
                step(nc.vector.tensor_tensor_scan(ends[:, :], rc[:, RC_ONE:RC_ONE + NE], tiles_of[:, :], 0.0, ALU.mult, ALU.add))
                step(nc.vector.tensor_tensor(tiles_of[:, :], ends[:, :], tiles_of[:, :], ALU.subtract))
                step(nc.vector.scalar_tensor_tensor(tot[:, :, :], tiles_of[:, :].unsqueeze(2).broadcast_to([P, NE, NT]), float(P),
                                                    tot[:, :, :], ALU.mult, ALU.add))
                step(nc.vector.tensor_tensor(work_[:, :, :], view(pg[0], NT, NE), tot[:, :, :].rearrange("p e t -> p t e"), ALU.add))
                step(nc.vector.tensor_tensor(work_[:, :, :], work_[:, :, :], hot[:, :, :], ALU.mult))
                step(nc.vector.tensor_reduce(top[:, :], work_[:, :, :], AX.X, ALU.add))
                step(nc.vector.tensor_copy(pos[:, :], top[:, :]), "pos")
                step(nc.vector.tensor_tensor(cmp_[:, :, :], rc[:, RC_J:RC_J + ST + 3].unsqueeze(2).broadcast_to([P, ST + 3, NE]),
                                             ends[:, :].unsqueeze(1).broadcast_to([P, ST + 3, NE]), ALU.is_ge))
                step(nc.vector.tensor_reduce(exf[:, :], cmp_[:, :, :], AX.X, ALU.add))
                step(nc.vector.tensor_scalar(exf[:, :], exf[:, :], float(NE - 1), None, ALU.min))
                step(nc.vector.tensor_copy(expert[:, :], exf[:, :]), "expert")

                G.wait("pos", "x1", "zeroed")
                for t in range(NT):
                    sent = scatter(nc.gpsimd.indirect_dma_start(
                        out=xsorted, out_offset=bass.IndirectOffsetOnAxis(ap=pos[:, t:t + 1], axis=0),
                        in_=x1[:, t, :], in_offset=None))
                SY.wait(sent)
                for s in range(4):
                    t = slice(s * ST // 4, (s + 1) * ST // 4)
                    in_xs = sorted_x(nc.sync.dma_start(xsort[:, t, :], xsorted.rearrange("(t p) d -> p t d", p=P)[:, t, :]))

                if glu:
                    M.wait(in_s, "xall", "lg1")
                    with c.loop(NT // 4) as g:
                        def hidden(f):
                            u = f % 2
                            M.wait(f"ht4{u}")
                            mm(pu[u][:, :], ws[:, f * P:(f + 1) * P], xall[:, ds(g * (4 * P), 4 * P)])
                            mm(pg[u][:, :], ws[:, FF + f * P:FF + (f + 1) * P], xall[:, ds(g * (4 * P), 4 * P)], name=f"ug{u}")
                            S.wait(f"ug{u}", f"ht4{u}")
                            S(nc.scalar.activation(sg[u][:, :], pg[u][:, :], ACT.Silu), f"sg{u}")
                            V.wait(f"sg{u}", f"down{u}")
                            V(nc.vector.tensor_tensor(ht4[u][:, :], pu[u][:, :], sg[u][:, :], ALU.mult), f"ht4{u}")

                        def down(f):
                            u = f % 2
                            M.wait(f"ht4{u}", "yt_read")
                            mm(pw[:, :], ws[:, 2 * FF + f * P:2 * FF + (f + 1) * P], ht4[u][:, :], start=f == 0, stop=f == FK - 1,
                               name=f"down{u}")

                        hidden(0)
                        for f in range(1, FK):
                            hidden(f)
                            down(f - 1)
                        down(FK - 1)
                        S.wait("down1", "yt4_read")
                        S(nc.scalar.activation(ht[0][:, :], pw[:, :], ACT.Identity), "yt_read")
                        M.wait("yt_read", "added")
                        for kt in range(4):
                            tr(pt[0][:, kt * P:(kt + 1) * P], ht[0][:, kt * P:(kt + 1) * P], "yt4_read")
                        V.wait("yt4_read")
                        V(nc.vector.tensor_tensor(bx[:, ds(g * 4, 4), :], x1[:, ds(g * 4, 4), :], view(pt[0], 4, P), ALU.add), "added")
                    V.wait("added")
                    S.wait("added")

                def get_x(j, u):
                    V.wait(f"xs_read{u}", "xsort_end", in_xs)
                    V(nc.vector.tensor_copy(xs4[u][:, 0, :], flat(xsort[:, ds(j, 1), :])), f"xs{u}")
                    M.wait(f"xs{u}", f"xt{u}")
                    tr(pt[u][:, 0:P], xs4[u][:, 0, :], f"xs_read{u}")
                    S.wait(f"xs_read{u}", f"ug{u}")
                    S(nc.scalar.activation(xt4[u][:, 0:P], pt[u][:, 0:P], ACT.Identity), f"xt{u}")

                e_pe = [nc.tensor.alloc_register(unused(f"expert_pe{r}")) for r in range(4)]
                e_v = [nc.vector.alloc_register(unused(f"expert_v{r}")) for r in range(3)]

                def held(engine, reg):
                    return engine.snap(reg, min_val=0, max_val=NE - 1)

                def load_pe(j):
                    nc.tensor.reg_load(e_pe, expert[0:1, ds(j, 4)])

                def load_v(j):
                    if not glu:
                        nc.vector.reg_load(e_v, expert[0:1, ds(j, 3)])

                def products_in(u, e):
                    M.wait(f"xt{u}", f"hid{u}")
                    if glu:
                        mm(pu[u][:, :], xt4[u][:, 0:P], flat(wx[:, ds(e, 1), 0:FF]))
                        mm(pg[u][:, :], xt4[u][:, 0:P], flat(wx[:, ds(e, 1), FF:2 * FF]), name=f"ug{u}")
                        S.wait(f"ug{u}", f"hid{u}")
                        S(nc.scalar.activation(sg[u][:, :], pg[u][:, :], ACT.Silu), f"sg{u}")
                    else:
                        mm(pu[u][:, :], xt4[u][:, 0:P], flat(wx[:, ds(e, 1), 0:FF]), name=f"ug{u}")
                        S.wait(f"ug{u}", f"hid_read{u}")
                        S(nc.scalar.activation(hid[u][:, :], pu[u][:, :], ACT.Identity), f"hid{u}")

                def gate_hidden(u):
                    if glu:
                        V.wait(f"sg{u}", f"hid_read{u}")
                        V(nc.vector.tensor_tensor(hid[u][:, :], pu[u][:, :], sg[u][:, :], ALU.mult), f"hid{u}")

                def turn_hidden(u, bias_of):
                    M.wait(f"hid{u}", "ht")
                    for f in range(FK):
                        tr(pl[:, f * P:(f + 1) * P], hid[u][:, f * P:(f + 1) * P], f"hid_read{u}")
                    V.wait(f"hid_read{u}", f"y{u}")
                    if glu:
                        V(nc.vector.tensor_copy(ht[u][:, :], pl[:, :]), "ht")
                    else:
                        e = held(nc.vector, bias_of)
                        for f in range(FK):
                            V(nc.vector.tensor_scalar(ht[u][:, f * P:(f + 1) * P], pl[:, f * P:(f + 1) * P],
                                                      b1[:, ds(e * FK + f, 1)], 0.0, ALU.add, ALU.max), "ht")
                    name(f"ht{u}", "ht")

                def products_out(j, u, e, bias_of):
                    M.wait(f"ht{u}", f"ysort{u ^ 1}")
                    for f in range(FK):
                        mm(pw[:, 0:P], ht[u][:, f * P:(f + 1) * P], flat(wx[:, ds(e, 1), q + f * P:q + (f + 1) * P]),
                           start=f == 0, stop=f == FK - 1, name=f"y{u}")
                    if glu:
                        S.wait(f"y{u}")
                        S(nc.scalar.activation(flat(ysort[:, ds(j, 1), :]), pw[:, 0:P], ACT.Identity), f"ysort{u}")
                    else:
                        e = held(nc.vector, bias_of)
                        V.wait(f"y{u}")
                        V(nc.vector.tensor_tensor(flat(ysort[:, ds(j, 1), :]), pw[:, 0:P], flat(b2[:, ds(e, 1), :]),
                                                  ALU.add), f"ysort{u}")

                M.wait(in_e, no_expert, "expert")
                V.wait(in_e, "expert")
                load_pe(0)
                load_v(0)
                for j in range(2):
                    get_x(j, j)
                    products_in(j, held(nc.tensor, e_pe[j]))
                    gate_hidden(j)
                get_x(2, 0)
                get_x(3, 1)
                turn_hidden(0, e_v[0])
                with c.loop(ST // 2 - 1) as ji:
                    first = ji * 2
                    products_in(0, held(nc.tensor, e_pe[2]))
                    get_x(first + 4, 0)
                    turn_hidden(1, e_v[1])
                    gate_hidden(0)
                    products_out(first, 0, held(nc.tensor, e_pe[0]), e_v[0])
                    products_in(1, held(nc.tensor, e_pe[3]))
                    last_pe = held(nc.tensor, e_pe[1])
                    load_pe(first + 2)
                    get_x(first + 5, 1)
                    turn_hidden(0, e_v[2])
                    gate_hidden(1)
                    last_v = None if glu else held(nc.vector, e_v[1])
                    load_v(first + 2)
                    products_out(first + 1, 1, last_pe, last_v)
                products_out(ST - 2, 0, held(nc.tensor, e_pe[0]), e_v[0])
                turn_hidden(1, e_v[1])
                products_out(ST - 1, 1, held(nc.tensor, e_pe[1]), e_v[1])

                SY.wait("ysort0", "ysort1")
                for s in range(4):
                    t = slice(s * ST // 4, (s + 1) * ST // 4)
                    out_y = store_y(nc.sync.dma_start(ysorted.rearrange("(t p) d -> p t d", p=P)[:, t, :], ysort[:, t, :]))
                G.wait(out_y)
                V.wait(out_y)
                per = NT // 4
                for s in range(4):
                    for t in range(s * per, (s + 1) * per):
                        got = gather[s](nc.gpsimd.indirect_dma_start(
                            out=back[:, t, :], out_offset=None, in_=ysorted,
                            in_offset=bass.IndirectOffsetOnAxis(ap=pos[:, t:t + 1], axis=0)))
                    t = slice(s * per, (s + 1) * per)
                    V.wait(got)
                    if glu:
                        step(nc.vector.tensor_tensor(back[:, t, :], back[:, t, :],
                                                     factor2[:, t].unsqueeze(2).broadcast_to([P, per, D]), ALU.mult))
                    V(nc.vector.tensor_tensor(bx[:, t, :], (bx if glu else x1)[:, t, :], back[:, t, :], ALU.add), "bx")
                barrier()


        def layer1_retention():
            with ExitStack() as k:
                small, tables = [lane(f"load_ret_{s}", nc.sync, 16) for s in ("small", "tables")]
                C = P
                x1 = sb(k, "x2", [P, NT, D])
                sq = sb(k, "sq2", [P, NT, D])
                wqk = sb(k, "wqk", [P, 4 * D])
                wvg = sb(k, "wvg", [P, 2 * EV])
                wp = sb(k, "wp", [P, 2, D])
                bqk = sb(k, "bqk", [P, 4])
                bvg = sb(k, "bvg", [P, 2 * EV])
                bp = sb(k, "bp", [P, D])
                rot = sb(k, "rot", [P, 4, T])
                decay = sb(k, "decay", [P, NH, C])
                edge = sb(k, "edge", [P, 2, C])
                heads4 = sb(k, "heads4", [P, 4])
                block = sb(k, "block", [P, EV])
                gam = sb(k, "gam", [P, 1])
                state = sb(k, "state", [P, B, EV])
                inflow_ = sb(k, "kv_in", [P, B, EV])
                two = lambda n, shape: [sb(k, f"{n}{u}", shape) for u in range(2)]
                xs, xt_ = two("xs_r", [P, B, D]), two("xt_r", [P, B * P])
                ra, rb = two("ra", [P, B, C]), two("rb", [P, B, C])
                qr, kr = two("qr", [P, B, C]), two("kr", [P, B, C])
                q2, k2 = two("q2_", [P, B, C]), two("k2_", [P, B, C])
                k2t = two("k2t", [P, B, C])
                qx = two("qx", [P, B, 4, C])
                vg = two("vg", [P, B, 2 * EV])
                gt = two("gt", [P, B, EV])
                sm = two("sm", [P, NH, C])
                og = two("og", [P, B * NH, DV])
                og2 = sb(k, "og2", [P, B * NH, DV])
                mu = sb(k, "mu", [P, B * NH])
                rs = sb(k, "rs", [P, B * NH])
                gy = sb(k, "gy", [P, B * EV])
                gyt = sb(k, "gyt", [P, B * EV])
                p_turn, p_q, p_k, p_vg, p_s0, p_s1, p_out, p_kv = [bank(k, f"pr{u}") for u in range(8)]
                p_s = (p_s0, p_s1)

                for dst, src in ((wqk[:, :], "wqk"), (wvg[:, :], "wvg"), (bqk[:, :], "bqk"), (edge[:, :, :], "edge"), (heads4[:, :], "heads4"), (block[:, :], "block"),
                                 (gam[:, :], "gam"), (wp[:, :, :], "wp"), (decay[:, :, :], "decay")):
                    small(nc.sync.dma_start(dst, a[src]))
                small(nc.sync.dma_start(bvg[:, :], a["bvg"].partition_broadcast(P)))
                in_s = small(nc.sync.dma_start(bp[:, :], a["bp"].partition_broadcast(P)))
                for r in range(4):
                    in_t = tables(nc.sync.dma_start(rot[:, r, :], a["rot"][:, r, :]))
                V(nc.vector.memset(state[:, :, :], 0.0), "state_r")

                normalise_stats(x1, sq, in_c)
                V.wait("rstd")
                for s in range(4):
                    t = slice(s * NT // 4, (s + 1) * NT // 4)
                    V(nc.vector.tensor_tensor(x1[:, t, :], x1[:, t, :], rstd[:, t].unsqueeze(2).broadcast_to([P, NT // 4, D]),
                                              ALU.mult), "x1")
                V.wait("x1", in_s, in_t)
                G.wait("x1", in_s)
                for s in range(4):
                    t = slice(s * NT // 4, (s + 1) * NT // 4)
                    G(nc.gpsimd.tensor_tensor(bx[:, t, :], x1[:, t, :], bp[:, :].unsqueeze(1).broadcast_to([P, NT // 4, D]),
                                              ALU.add), "x1_bp")
                M.wait(in_s, in_t)
                S.wait(in_s)
                by_batch = lambda v: v.rearrange("p (b c) d -> p b c d", b=B)
                over_b = lambda v: v.unsqueeze(1).broadcast_to([P, B, C])

                def turn_x(c_, u):
                    V.wait("x_turned")
                    V(nc.vector.tensor_copy(xs[u][:, :, :].unsqueeze(2), by_batch(x1[:, :, :])[:, :, ds(c_, 1), :]), "xs_r")
                    M.wait("xs_r", "xt_r", "k2t")
                    for b in range(B):
                        tr(p_turn[:, b * P:(b + 1) * P], xs[u][:, b, :], "x_turned")
                    S.wait("x_turned", f"vg_made{u}", "k_made")
                    S(nc.scalar.activation(xt_[u][:, :], p_turn[:, 0:B * P], ACT.Identity), "xt_r")

                def project_qk(c_, u):
                    M.wait("xt_r", "rot_q", "rot_k")
                    for j, (bnk, nm) in enumerate(((p_q, "q_made"), (p_q, "q_made"), (p_k, "k_made"), (p_k, "k_made"))):
                        mm(bnk[:, (j % 2) * B * C:(j % 2 + 1) * B * C], wqk[:, j * D:(j + 1) * D], xt_[u][:, :], name=nm)

                def rotate(c_, u):
                    for j, (bnk, dst, nm, far) in enumerate(((p_q, qr, "q", q2), (p_k, kr, "k", k2))):
                        V.wait(f"{nm}_made", f"{nm}_summed")
                        for r, part in enumerate((ra[j], rb[j])):
                            V(nc.vector.scalar_tensor_tensor(part[:, :, :], view(bnk, B, C, r * B * C), bqk[:, 2 * j + r:2 * j + r + 1],
                                                             rot[:, 2 * j + r, ds(c_ * C, C)].unsqueeze(1).broadcast_to([P, B, C]),
                                                             ALU.add, ALU.mult), f"rot_{nm}")
                        G.wait(f"rot_{nm}", "scores", "qx", "k2_turned", "from_state")
                        G(nc.gpsimd.tensor_tensor(dst[u][:, :, :], ra[j][:, :, :], rb[j][:, :, :], ALU.add), f"{nm}_summed")
                        G.wait(f"{nm}_summed")
                        G(nc.gpsimd.tensor_tensor(far[u][:, :, :], dst[u][:, :, :], over_b(edge[:, j, :]), ALU.mult), f"{nm}2_{u}")

                def spread_q(u):
                    V.wait("q_summed", "scores")
                    V(nc.vector.tensor_tensor(qx[u][:, :, :, :], qr[u][:, :, :].unsqueeze(2).broadcast_to([P, B, 4, C]),
                                              heads4[:, :].unsqueeze(1).unsqueeze(3).broadcast_to([P, B, 4, C]), ALU.mult), "qx")
                    name(f"qx{u}", "qx")

                def project_vg(b, u):
                    M.wait("vg", "gyt")
                    mm(p_vg[:, :], xt_[u][:, b * P:(b + 1) * P], wvg[:, :], name=f"vg_made{u}")
                    V.wait(f"vg_made{u}", f"kv{u}", f"within{u}", f"gt{u}")
                    V(nc.vector.tensor_tensor(vg[u][:, b, :], p_vg[:, :], bvg[:, :], ALU.add), "vg")
                    name(f"vg{u}", "vg")

                def gates(u):
                    S.wait(f"vg{u}", f"gy{u}")
                    S(nc.scalar.activation(gt[u][:, :, :], vg[u][:, :, EV:2 * EV], ACT.Silu), f"gt{u}")

                def scores(b, u):
                    for s in range(2):
                        M.wait(f"qx{u}", "k_summed", f"decayed{s}")
                        mm(p_s[s][:, :], kr[u][s * 64:(s + 1) * 64, b, :], qx[u][s * 64:(s + 1) * 64, b, :, :].rearrange("p m c -> p (m c)"),
                           name="scores")
                        V.wait("scores", f"within_b{b}")
                        V(nc.vector.tensor_tensor(sm[b][:, 4 * s:4 * s + 4, :], view(p_s[s], 4, C), decay[:, 4 * s:4 * s + 4, :],
                                                  ALU.mult), f"decayed{s}")
                    name(f"sm{b}", "decayed1")

                def outputs(b, u):
                    M.wait(f"q2_{u}", "state_r", "og", f"sm{b}", f"vg{u}")
                    mm(p_out[:, b * EV:(b + 1) * EV], q2[u][:, b, :], state[:, b, :], stop=False, name="from_state")
                    for h in range(NH):
                        mm(p_out[:, b * EV + h * DV:b * EV + (h + 1) * DV], sm[b][:, h, :], vg[u][:, b, h * DV:(h + 1) * DV],
                           start=False, stop=h == NH - 1, name=f"within{u}")
                    name(f"within_b{b}", f"within{u}")

                def take_out(u):
                    S.wait(f"within{u}", f"gy{u}")
                    S(nc.scalar.activation(og[u][:, :, :].rearrange("p g v -> p (g v)"), p_out[:, :], ACT.Identity), "og")
                    name(f"og{u}", "og")

                def turn_k(u):
                    M.wait(f"k2_{u}", "xt_r", "k2t")
                    for b in range(B):
                        tr(p_turn[:, 256 + b * P:256 + (b + 1) * P], k2[u][:, b, :], "k2_turned")
                    S.wait("k2_turned", f"kv{u}")
                    S(nc.scalar.activation(k2t[u][:, :, :], view(p_turn, B, P, 256), ACT.Identity), "k2t")

                def update_state(u):
                    M.wait("k2t", f"vg{u}", "kv_in", "out_r")
                    for b in range(B):
                        mm(p_kv[:, b * EV:(b + 1) * EV], k2t[u][:, b, :], vg[u][:, b, 0:EV], name=f"kv{u}")
                    V.wait(f"kv{u}", "state_r")
                    V(nc.vector.tensor_tensor(inflow_[:, :, :], view(p_kv, B, EV), block[:, :].unsqueeze(1).broadcast_to([P, B, EV]),
                                              ALU.mult), "kv_in")
                    V.wait("kv_in", "from_state")
                    V(nc.vector.scalar_tensor_tensor(state[:, :, :], state[:, :, :], gam[:, 0:1], inflow_[:, :, :],
                                                     ALU.mult, ALU.add), "state_r")

                over_v = lambda v: v[:, :].unsqueeze(2).broadcast_to([P, B * NH, DV])
                def centre(u):
                    V.wait(f"og{u}")
                    V.wait(V(nc.vector.tensor_reduce(mu[:, :], og[u][:, :, :], AX.X, ALU.add)))
                    V.wait(V(nc.vector.tensor_scalar(mu[:, :], mu[:, :], 1.0 / DV, None, ALU.mult)))
                    V(nc.vector.tensor_tensor(og[u][:, :, :], og[u][:, :, :], over_v(mu), ALU.subtract), f"centred{u}")
                    S.wait(f"centred{u}", "rs_sum")
                    S(nc.scalar.activation(og2[:, :, :], og[u][:, :, :], ACT.Square), "og2")

                def spread_of(u):
                    V.wait("og2", "rs")
                    V(nc.vector.tensor_reduce(rs[:, :], og2[:, :, :], AX.X, ALU.add), "rs_sum")
                    S.wait("rs_sum")
                    S(nc.scalar.activation(rs[:, :], rs[:, :], ACT.Sqrt, bias=eps[:, 0:1], scale=1.0 / DV), "rs_root")

                def normed(u):
                    V.wait("rs_root")
                    V(nc.vector.reciprocal(rs[:, :], rs[:, :]), "rs")
                    V.wait("rs")
                    V(nc.vector.tensor_tensor(og[u][:, :, :], og[u][:, :, :], over_v(rs), ALU.mult), f"normed{u}")
                    G.wait(f"normed{u}", f"gt{u}", "gy_turned")
                    G(nc.gpsimd.tensor_tensor(gy[:, :], og[u][:, :, :].rearrange("p g v -> p (g v)"), gt[u][:, :, :].rearrange("p b v -> p (b v)"),
                                              ALU.mult), f"gy{u}")

                def turn_y(u):
                    M.wait(f"gy{u}", "vg", "gyt")
                    for j in range(4):
                        tr(p_vg[:, j * P:(j + 1) * P], gy[:, j * P:(j + 1) * P], "gy_turned")
                    S.wait("gy_turned", "out_made")
                    S(nc.scalar.activation(gyt[:, :], p_vg[:, :], ACT.Identity), "gyt")

                def project_out(c_, u):
                    M.wait("gyt", "kv_in", "out_r")
                    for b in range(B):
                        for j in range(2):
                            mm(p_kv[:, b * P:(b + 1) * P], gyt[:, (2 * b + j) * P:(2 * b + j + 1) * P], wp[:, j, :],
                               start=j == 0, stop=j == 1, name="out_made")
                    V.wait("out_made", "x1_bp")
                    res = by_batch(bx[:, :, :])[:, :, ds(c_, 1), :]
                    V(nc.vector.tensor_tensor(res, res, view(p_kv, B, P).unsqueeze(2), ALU.add), "out_r")

                def turn_of(c_, u, before_=True, after=True):
                    w_ = u ^ 1
                    scores(0, u)
                    if after:
                        turn_x(c_ + 1, w_)
                    if before_:
                        centre(w_)
                    scores(1, u)
                    if after:
                        project_qk(c_ + 1, w_)
                        rotate(c_ + 1, w_)
                    outputs(0, u)
                    if before_:
                        spread_of(w_)
                    turn_k(u)
                    if after:
                        project_vg(0, w_)
                    if before_:
                        normed(w_)
                    outputs(1, u)
                    take_out(u)
                    if after:
                        project_vg(1, w_)
                        gates(w_)
                        spread_q(w_)
                    update_state(u)
                    if before_:
                        turn_y(w_)
                        project_out(c_ - 1, w_)

                turn_x(0, 0)
                project_qk(0, 0)
                rotate(0, 0)
                project_vg(0, 0)
                project_vg(1, 0)
                gates(0)
                spread_q(0)
                turn_of(0, 0, before_=False)
                turn_of(1, 1)
                with c.loop(TB // 2 - 2) as ci:
                    turn_of(ci * 2 + 2, 0)
                    turn_of(ci * 2 + 3, 1)
                turn_of(TB - 2, 0)
                turn_of(TB - 1, 1, after=False)
                centre(1)
                spread_of(1)
                normed(1)
                turn_y(1)
                project_out(TB - 1, 1)
                barrier()

        layer0_mamba()
        experts(True, 0)
        layer1_retention()
        experts(False, 1)
        final()
        return c.per, c.later


def constants():
    k = {"ident": np.eye(P, dtype=np.float32), "mirror": np.eye(P, dtype=np.float32)[::-1]}
    k["keep"] = np.broadcast_to(np.array([c % (NCH // B) > 0 for c in range(NCH)] + [f[0] for f in FACTORS], np.float32), (P, NCH + len(FACTORS)))
    k["sel"] = (np.arange(96)[:, None] % 32 == np.arange(32)).astype(mybir.dt.np(BF16))
    k["before"] = np.triu(np.ones((P, P), np.float32), 1).astype(mybir.dt.np(BF16))
    k["every"] = np.ones((P, P), mybir.dt.np(BF16))
    run = np.ones((NE, NT), np.float32)
    run[:, 0] = 0.0
    row = np.concatenate([NE - np.arange(NE), run.reshape(-1), P * np.arange(NT), np.ones(NE), np.arange(ST + 3)])
    f32 = np.float32
    pos = np.arange(T, dtype=f32)
    scale = ((np.arange(0, D, 2, dtype=f32) + f32(0.4 * D)) / f32(1.4 * D))[:, None] ** (pos[None, :] / f32(512.0))
    angle = (f32(1.0) / f32(10000.0) ** (np.arange(D // 2, dtype=f32) / f32(D // 2)))[:, None] * pos[None, :]
    sin, cos, sign = np.sin(angle), np.cos(angle), np.tile(np.array([[-1], [1]], f32), (D // 2, 1))
    pairs = lambda v: np.repeat(v, 2, axis=0)
    gamma = 1.0 - np.exp(np.linspace(np.log(1 / 32), np.log(1 / 512), NH))
    log = np.log(gamma.astype(f32).astype(np.float64))
    decays = lambda n: np.exp(log[:, None] * n)
    norm = 1.0 / np.sqrt(np.cumsum(decays(np.arange(T)), axis=1)) * DK ** -0.5
    by_head = lambda v: np.repeat(v, DK, axis=0)
    k["rot"] = np.stack([pairs(cos * scale) * by_head(norm), pairs(sin * scale) * sign * by_head(norm),
                         pairs(cos / scale), pairs(sin / scale) * sign], 1).astype(f32)
    k["edge"] = np.stack([by_head(decays(np.arange(P) + 1)), by_head(decays(P - 1 - np.arange(P)))], 1).astype(f32)
    gap = np.arange(P)[None, :] - np.arange(P)[:, None]
    k["decay"] = (np.exp(log[None, :, None] * np.maximum(gap, 0)[:, None, :]) * (gap >= 0)[:, None, :]).astype(f32)
    k["heads4"] = (np.arange(P)[:, None] // DK % 4 == np.arange(4)).astype(f32)
    k["block"] = (np.arange(P)[:, None] // DK == np.arange(EV)[None, :] // DV).astype(f32)
    k["gam"] = by_head(decays(np.array([P]))).astype(f32)
    k["rc"] = np.broadcast_to(row.astype(np.float32), (P, RC_N))
    return k


def layout(x):
    x = {key: np.asarray(v) for key, v in x.items()}
    r = {"x": x["L0_attn_x"].reshape(NT, P, D).transpose(1, 0, 2)}
    r["lnp"] = np.stack([x["L0_attn_ln_g"], x["L0_attn_ln_b"]], 1)
    halves = lambda v: v.reshape(HF, P, -1).transpose(1, 0, 2).reshape(P, -1)
    in_u, conv, packed = [], [], []
    for d in "fb":
        g = lambda name: x[f"L0_attn_{d}_{name}"]
        in_u.append(g("in_w")[:DI].T)
        conv.append(np.broadcast_to(g("conv_w").T.reshape(TAPS * DI), (P, TAPS * DI)))
        bc = g("xproj_w")[RK:].T
        packed.append(np.concatenate([
            g("in_w")[DI:].T, halves(g("xproj_w")[:RK].T), halves(np.concatenate([bc, bc, bc], 1)),
            np.concatenate([g("dt_w").T, g("dt_w").T]), halves(g("out_w").T), halves(g("conv_b")),
            halves(g("dt_b")), halves(g("D")), halves(g("Alog"))], 1))
    r["in_u"], r["conv_w"], r["mamba_w"] = (np.stack(v, 1) for v in (in_u, conv, packed))
    rows = lambda v: v.reshape(*v.shape[:-2], FK, P, D).swapaxes(-3, -2).reshape(*v.shape[:-2], P, FK * D)
    f = lambda name: x["L0_ffn_" + name]
    r["rw0"] = f("router_w")
    r["shared_w"] = np.concatenate([f("shared_up_w"), f("shared_gate_w"), rows(f("shared_down_w"))], 1)
    r["l0_w"] = np.concatenate([f("up_w"), f("gate_w"), rows(f("down_w"))], 2).swapaxes(0, 1)
    f = lambda name: x["L1_attn_" + name]
    w_q, w_k, w_v = np.split(f("w_qkv"), (D, 2 * D), axis=1)
    b_q, b_k, b_v = np.split(f("b_qkv"), (D, 2 * D))
    pair = np.arange(D) ^ 1
    r["wqk"] = np.concatenate([w_q, w_q[:, pair], w_k, w_k[:, pair]], 1)
    r["bqk"] = np.stack([b_q, b_q[pair], b_k, b_k[pair]], 1)
    r["wvg"], r["bvg"] = np.concatenate([w_v, f("w_g")], 1), np.concatenate([b_v, f("b_g")])
    r["wp"], r["bp"] = f("w_p").reshape(2, P, D).swapaxes(0, 1), f("b_p")
    f = lambda name: x["L1_ffn_" + name]
    r["rw1"], r["br"], r["b2"] = f("Wr").T, f("br"), f("b2")
    r["l1_w"] = np.concatenate([f("W1").swapaxes(1, 2), rows(f("W2").swapaxes(1, 2))], 2).swapaxes(0, 1)
    r["b1"] = f("b1").reshape(NE, FK, P).transpose(2, 0, 1).reshape(P, NE * FK)
    return r


def kernel(**inputs):
    import concourse.bacc as bacc
    from concourse.bass_utils import run_bass_kernel_spmd

    arrays = {name: np.ascontiguousarray(v) for name, v in {**constants(), **layout(inputs)}.items()}
    known = ({}, {})
    for _ in range(2):
        nc = bacc.Bacc("TRN2", target_bir_lowering=False, num_devices=1)
        aps = {name: nc.dram_tensor("in_" + name, v.shape, mybir.dt.from_np(v.dtype), kind="ExternalInput").ap()
               for name, v in arrays.items()}
        out = nc.dram_tensor("out", (P, NT, D), F32, kind="ExternalOutput").ap()
        known = build(nc, known, aps, out)
    r = run_bass_kernel_spmd(nc, [{"in_" + name: v for name, v in arrays.items()}], core_ids=[0])
    return r.results[0]["out"].transpose(1, 0, 2).reshape(B, T, D)
```

```python
import concourse.bass as bass
from concourse import mybir
from contextlib import ExitStack, contextmanager
import numpy as np

F32, BF16, U32, I32 = mybir.dt.float32, mybir.dt.bfloat16, mybir.dt.uint32, mybir.dt.int32
ALU, ACT, AX = mybir.AluOpType, mybir.ActivationFunctionType, mybir.AxisListType
ds = bass.ds

P = 128
B, T, D = 2, 2048, 128
NT = B * T // P
TB = T // P
DI, NS, RK, TAPS = 256, 16, 64, 4
CH = 512
NCH = B * T // CH
HF = DI // P
FF, NE = 512, 8
FK = FF // P
ST = NT + NE
NH, DK, DV = 8, 16, 32
EV = NH * DV
EPS = 1e-5
SPREAD = 0.5186097621917725
FACTORS = ((0.5234627723693848, 0.29748213291168213), (-0.04265656694769859, 0.8761158585548401),
           (-0.7388817667961121, 0.7267470359802246), (-1.2040492296218872, 0.11629842966794968))

W_U = 0
W_Z = W_U + TAPS * DI
W_X = W_Z + DI
W_DT = W_X + HF * P
W_O = W_DT + DI
W_CB = W_O + HF * D
W_DB = W_CB + HF
W_D = W_DB + HF
W_A = W_D + HF
W_N = W_A + HF * NS

RC_REV = 0
RC_RUN = RC_REV + NE
RC_MULT = RC_RUN + NE * NT
RC_ONE = RC_MULT + NT
RC_J = RC_ONE + NE
RC_N = RC_J + ST + 3


class Mark:
    def __init__(self, lane, at, loops):
        self.lane, self.at, self.loops = lane, at, loops


class Counts:
    START = 1 << 13

    def __init__(self, nc, known):
        self.nc, self.known, self.per, self.later = nc, known, {}, {}
        self.lanes, self.loops, self.n_loops, self.scopes = [], [], 0, [(None, {})]

    @contextmanager
    def loop(self, n):
        key = self.n_loops
        self.n_loops += 1
        before = [(l, l.at) for l in self.lanes]
        for l in self.lanes:
            l.waited = {}
        with self.nc.Fori(0, n, 1) as i:
            self.loops.append((key, i, n))
            self.scopes.append((key, {}))
            yield i
            self.loops.pop()
            _, names = self.scopes.pop()
        self.later.update({(key, name): mark for name, mark in names.items()})
        self.scopes[-1][1].update(names)
        for l, at in before:
            self.per[key, l.name] = l.at - at
            l.at = at + n * (l.at - at)
            l.waited = {}

    def named(self, name):
        found = []
        for key, names in reversed(self.scopes):
            if name in names:
                return found + [(names[name], None)]
            if (key, name) in self.known[1]:
                found.append((self.known[1][key, name], key))
        return found

    def at_iteration(self, name, i):
        mark = self.scopes[-1][1][name]
        (key, _), = mark.loops
        return Mark(mark.lane, mark.at + i * self.known[0].get((key, mark.lane.name), 0), [])

    def value(self, mark, back):
        per = self.known[0]
        active = {key: i for key, i, _ in self.loops}
        value, terms = mark.at, []
        for key, n in mark.loops:
            m = per.get((key, mark.lane.name), 0)
            if key in active:
                terms += [(active[key], m)] if m else []
            else:
                value += (n - 1) * m
        if back is not None:
            value -= per.get((back, mark.lane.name), 0)
        return value, terms


class Lane:
    def __init__(self, c, name, engine, sem, step=1, start=Counts.START):
        self.c, self.name, self.e, self.sem, self.step = c, name, engine, sem, step
        self.at = self.start = start
        self.waited = {}
        c.lanes.append(self)

    def __call__(self, ins, name=None):
        ins.then_inc(self.sem, self.step)
        self.at += self.step
        m = Mark(self, self.at, [(k, n) for k, _, n in self.c.loops])
        if name:
            self.c.scopes[-1][1][name] = m
        return m

    def wait(self, *marks):
        for m in marks:
            for mark, back in (self.c.named(m) if isinstance(m, str) else [(m, None)]):
                value, terms = self.c.value(mark, back)
                key = (mark.lane.name, tuple(per for _, per in terms))
                if self.waited.get(key, -1) >= value:
                    continue
                self.waited[key] = value
                for i, per in terms:
                    value = value + i * per
                self.e.wait_ge(next(l.sem for l in self.c.lanes if l.name == mark.lane.name), value)


def build(nc, known, a, out):
    c = Counts(nc, known)
    ctx = ExitStack()

    def lane(name, engine, step=1, start=Counts.START):
        l = Lane(c, name, engine, ctx.enter_context(nc.semaphore("s_" + name)), step, start)
        if start:
            engine.sem_inc(l.sem, start)
        return l

    with ctx:
        V = lane("vector", nc.vector)
        S = lane("scalar", nc.scalar)
        G = lane("gpsimd", nc.gpsimd)
        M = lane("tensor", nc.tensor)
        L = {k: lane("load_" + k, nc.sync, 16) for k in ("pads", "mamba", "const")}
        L["out"] = lane("store_out", nc.sync, 16)
        SY = Lane(c, "sync", nc.sync, None)

        def name(new, old):
            c.scopes[-1][1][new] = c.scopes[-1][1][old]

        def barrier():
            now = [Mark(l, l.at, []) for l in c.lanes if l.at > l.start]
            for w in (V, S, G, M, SY):
                w.wait(*now)

        used = {}

        def unused(name):
            used[name] = used.get(name, 0) + 1
            return name if used[name] == 1 else f"{name}_{used[name]}"

        def sb(scope, name, shape, dt=F32):
            return scope.enter_context(nc.sbuf_tensor(unused(name), shape, dt))

        def bank(scope, name, n=1):
            return scope.enter_context(nc.psum_tensor(unused(name), [P, n * 512], F32))

        def flat(t):
            return t.rearrange("p a c -> p (a c)")

        def view(t, n, w, off=0):
            return t[:, off:off + n * w].rearrange("p (n w) -> p n w", n=n)

        def mm(out, lhsT, rhs, start=True, stop=True, name=None):
            i = nc.tensor.matmul(out, lhsT, rhs, start=start, stop=stop)
            return M(i, name)

        def tr(out, in_, name=None):
            i = nc.tensor.transpose(out, in_, ident[:, :])
            return M(i, name)

        bx = sb(ctx, "residual", [P, NT, D])
        ident = sb(ctx, "ident", [P, P])
        mirror = sb(ctx, "mirror", [P, P])
        number = sb(ctx, "number", [P, NT])
        eps = sb(ctx, "eps", [P, 1])
        stats = sb(ctx, "stats", [P, NT, 6])
        moments = sb(ctx, "moments", [P, NT, 2])
        rstd = sb(ctx, "rstd", [P, NT])
        shift = sb(ctx, "shift", [P, NT])
        xsorted = [nc.dram_tensor(f"xsorted{layer}", (ST * P, D + 1), F32, kind="Internal").ap() for layer in range(2)]
        ytoken = nc.dram_tensor("ytoken", ((NT + ST) * P, D), F32, kind="Internal").ap()

        in_x = []
        for k in range(4):
            n = NT // 4
            in_x.append(lane(f"load_x{k}", nc.sync, 16)(nc.sync.dma_start(bx[:, k * n:(k + 1) * n, :], a["x"][:, k * n:(k + 1) * n, :])))
        L["const"](nc.sync.dma_start(ident[:, :], a["ident"]))
        L["const"](nc.sync.dma_start(number[:, :], a["number"]))
        in_c = L["const"](nc.sync.dma_start(mirror[:, :], a["mirror"]))
        h_eps = V(nc.vector.memset(eps[:, :], EPS))

        def measure(tiles):
            for t in tiles:
                V(nc.vector.bn_stats(stats[:, t, :], bx[:, t, :]), "stats")
            V.wait("stats")
            combine_stats(tiles)

        def combine_stats(tiles):
            for t in tiles:
                V(nc.vector.bn_aggr(moments[:, t, :], stats[:, t, :]), "measured")

        def deviations(tiles=range(NT)):
            t = slice(tiles[0], tiles[-1] + 1)
            S.wait("measured", h_eps)
            V.wait(S(nc.scalar.activation(rstd[:, t], moments[:, t, 1], ACT.Sqrt, bias=eps[:, 0:1])))
            V(nc.vector.reciprocal(rstd[:, t], rstd[:, t]), "rstd")

        def normalise(tiles=range(NT), on="VSVSVSVG"):
            deviations(tiles)
            V.wait("rstd")
            t = slice(tiles[0], tiles[-1] + 1)
            V(nc.vector.scalar_tensor_tensor(shift[:, t], moments[:, t, 0], -1.0, rstd[:, t], ALU.mult, ALU.mult), "shift")
            S.wait("shift")
            if "G" in on:
                G.wait("rstd")
            for t in tiles:
                which = on[t % len(on)]
                if which == "S":
                    S(nc.scalar.activation(xn[:, t, 0:D], bx[:, t, :], ACT.Identity, bias=shift[:, t:t + 1], scale=rstd[:, t:t + 1]),
                      "x1_s")
                else:
                    lane_, e = (G, nc.gpsimd) if which == "G" else (V, nc.vector)
                    lane_(e.tensor_scalar(xn[:, t, 0:D], bx[:, t, :], moments[:, t, 0:1], rstd[:, t:t + 1], ALU.subtract, ALU.mult),
                          "x1_g" if which == "G" else "x1_v")

        def layer0_mamba():
            with ExitStack() as k:
                xt = sb(k, "xt", [P, 2 * NCH + 2, TAPS - 1 + CH])
                om = sb(k, "om", [P, 2 * (NCH + 1), CH])
                wd = [sb(k, f"w{i}", [P, W_N]) for i in range(2)]
                lnp = sb(k, "lnp", [P, 2])
                keep = sb(k, "keep", [P, NCH + len(FACTORS)])
                sel = sb(k, "sel", [P, 2 * NS], BF16)
                pre = sb(k, "pre", [P, 4, CH])
                uz = [sb(k, f"uz{i}", [P, 4, CH]) for i in range(2)]
                with ExitStack() as k0:
                    xs = sb(k0, "xs", [P, 4, D])
                    pt = [bank(k0, f"pt{u}") for u in range(4)]
                    L["mamba"](nc.sync.dma_start(lnp[:, :], a["lnp"]))
                    L["mamba"](nc.sync.dma_start(keep[:, :], a["keep"]))
                    in_w = L["mamba"](nc.sync.dma_start(sel[0:96, :], a["sel"]))
                    in_w2 = []
                    for i, w in enumerate(wd):
                        conv, load = (pre, uz[0])[i], lane(f"load_w{i}", nc.sync, 16)
                        load(nc.sync.dma_start(conv[:, 0:2, :], a["conv_w"][:, i, :]))
                        load(nc.sync.dma_start(conv[:, 2, 0:DI], a["in_u"][:, i, :]))
                        in_w2.append(load(nc.sync.dma_start(w[:, W_Z:W_N], a["mamba_w"][:, i, :])))
                    for rows in xsorted:
                        L["pads"](nc.sync.dma_start(rows, a["pads"]), "padded")
                    for s in range(4):
                        V.wait(in_x[s])
                        measure(range(s * NT // 4, (s + 1) * NT // 4))
                    deviations()
                    G(nc.gpsimd.memset(xt[:, 2 * NCH:2 * NCH + 2, :], 0.0), "xt_end")
                    M.wait(in_c)
                    S.wait(in_w)
                    V.wait("rstd")
                    with c.loop(TB // 4) as ci:
                        for kt in range(4):
                            for u in range(B):
                                tile = ci * 4 + (u * TB + kt)
                                v = kt % 2 * B + u
                                V.wait(f"mirrored{v}")
                                V(nc.vector.tensor_scalar(xs[:, v, :], flat(bx[:, ds(tile, 1), :]), flat(moments[:, ds(tile, 1), 0:1]),
                                                          rstd[:, ds(tile, 1)], ALU.subtract, ALU.mult), f"xs{v}")
                                M.wait(f"xs{v}", f"xt{v}")
                                nc.tensor.matmul(pt[v][:, 0:P], xs[:, v, :], ident[:, :], start=True, stop=True)
                                mm(pt[v][:, P:2 * P], xs[:, v, :], mirror[:, :], name=f"mirrored{v}")
                                S.wait(f"mirrored{v}")
                                col = TAPS - 1 + kt * P
                                S(nc.scalar.activation(flat(xt[:, ds(ci + u * 4, 1), col:col + P]), pt[v][:, 0:P],
                                                       ACT.Identity, bias=lnp[:, 1:2], scale=lnp[:, 0:1]))
                                col = TAPS - 1 + (3 - kt) * P
                                S(nc.scalar.activation(flat(xt[:, ds((NCH + u * 4 + 3) - ci, 1), col:col + P]), pt[v][:, P:2 * P],
                                                       ACT.Identity, bias=lnp[:, 1:2], scale=lnp[:, 0:1]), f"xt{v}")
                    V.wait("xt0", "xt1", "xt2", "xt3", "xt_end")
                    V.wait(V(nc.vector.tensor_copy(xt[:, 1:2 * NCH + 1, 0:3], xt[:, 0:2 * NCH, CH:CH + 3])))
                    V(nc.vector.memset(xt[:, 0:2 * NCH + 1:4, 0:3], 0.0))
                    for i, w in enumerate(wd):
                        conv = (pre, uz[0])[i]
                        V.wait(in_w2[i])
                        V(nc.vector.tensor_tensor(view(w, TAPS, DI), conv[:, 0:2, :].rearrange("p a (t d) -> p (a t) d", d=DI),
                                                  conv[:, 2, 0:DI].unsqueeze(1).broadcast_to([P, TAPS, DI]), ALU.mult))
                        S.wait(in_w2[i])
                        V.wait(S(nc.scalar.activation(w[:, W_A:W_N], w[:, W_A:W_N], ACT.Exp)))
                        V(nc.vector.tensor_scalar(w[:, W_A:W_N], w[:, W_A:W_N], -1.0, None, ALU.mult), "w")
                    barrier()

                dtr, rest = pre[P - RK:P, 3, :], pre[:, 2, :]
                mid = sb(k, "mid", [P, CH], BF16)
                bc = [sb(k, f"bc{i}", [P, CH], BF16) for i in range(2)]
                ab = sb(k, "ab", [P, HF, CH])
                rx = sb(k, "rx", [P, HF, CH])
                dt = [sb(k, f"dt{i}", [P, HF, CH]) for i in range(2)]
                dtu = [sb(k, f"dtu{i}", [P, HF, CH]) for i in range(2)]
                db = [sb(k, f"db{i}", [P, HF, CH]) for i in range(3)]
                yz, sq0, sq1, hh4 = [bx[:, s * 8:s * 8 + 8, :].rearrange("p (h a) d -> p h (a d)", h=HF) for s in range(4)]
                sq = (sq0, sq1)
                hh = [sb(k, f"hh{i}", [P, HF, CH]) for i in range(4)] + [hh4]
                hc = [sb(k, f"hc{i}", [P, HF, CH]) for i in range(3)]
                cs = [sb(k, f"cs{i}", [P, CH]) for i in range(3)]
                st = sb(k, "st", [P, 2, NS, HF])
                py = bank(k, "py", 2)
                pb = [bank(k, f"pb{i}") for i in range(2)]
                pc = [bank(k, f"pc{i}") for i in range(2)]
                pq = [bank(k, f"pq{i}") for i in range(2)]

                def prep(i, slot, next_slot, before=[], only_u=False):
                    def project(j, col, taps=(TAPS - 1,), last=True):
                        M.wait("w", f"pq{j % 2}_empty")
                        at, w = (next_slot, wd[i ^ 1]) if j < HF else (slot, wd[i])
                        for t in taps:
                            m = nc.tensor.matmul(pq[j % 2][:, :], w[:, col:col + P] if j >= HF else w[:, col + t * DI:col + t * DI + P],
                                                 flat(xt[:, ds(at, 1), t:t + CH]), start=t == taps[0] and (j >= HF or t == 0),
                                                 stop=t == TAPS - 1)
                        M(m, f"pq{j % 2}")

                    def keep_pre(j):
                        S.wait(f"pq{j % 2}", "w", "uz0", "uz1", "low", "mid", "dt_in1")
                        bias = wd[i ^ 1][:, W_CB + j:W_CB + j + 1] if j < HF else 0.0
                        S(nc.scalar.activation(pre[:, j, :], pq[j % 2][:, :], ACT.Identity, bias=bias), f"pre{j}")
                        name(f"pq{j % 2}_empty", f"pre{j}")

                    def silu():
                        S.wait("pre0", "pre1", "pre3", f"gated{i}", f"dtu{i}")
                        S(nc.scalar.activation(uz[i][:, :, :], pre[:, :, :], ACT.Silu), f"uz{i}")

                    def x_project():
                        M.wait(f"uz{i}", "pq0_empty")
                        for h in range(HF):
                            mm(pq[0][:, :], wd[i][:, W_X + h * P:W_X + (h + 1) * P], uz[i][:, h, :],
                               start=h == 0, stop=h == HF - 1, name="pq0")

                    def keep_rank():
                        S.wait("pq0", "dt_in1")
                        S(nc.scalar.activation(dtr, pq[0][P - RK:P, :], ACT.Identity), "dtr")
                        name("pq0_empty", "dtr")

                    def high_part():
                        S.wait("pq0", f"c_read{i}", f"b_read{i}", "low")
                        S(nc.scalar.activation(bc[i][0:64, :], pq[0][0:64, :], ACT.Identity), "high")

                    def rest_of_high():
                        V.wait("high", "low_mid")
                        V(nc.vector.tensor_tensor(rest[0:64, :], pq[0][0:64, :], bc[i][0:64, :], ALU.subtract), "b_c_read")

                    def mid_part():
                        S.wait("b_c_read", "low")
                        S(nc.scalar.activation(mid[0:64, :], rest[0:64, :], ACT.Identity), "mid")

                    def low_part():
                        V.wait("mid")
                        V(nc.vector.tensor_tensor(bc[i][64:96, :], rest[32:64, :], mid[32:64, :], ALU.subtract), f"low{i}")
                        name("low", f"low{i}")
                        S.wait("mid")
                        S(nc.scalar.activation(bc[i][32:64, :], mid[32:64, :], ACT.Identity), f"bc{i}")
                        name("low_mid", f"bc{i}")

                    def dt_in(h):
                        M.wait("dtr", f"pq{1 - h}_empty", "b_c_read")
                        mm(pq[1 - h][:, :], wd[i][P - RK:P, W_DT + h * P:W_DT + (h + 1) * P], dtr, name=f"dt_in{h}")

                    def relu_abs(h):
                        bias = wd[i][:, W_DB + h:W_DB + h + 1]
                        S.wait(f"dt_in{h}", "softplus", "factor")
                        S(nc.scalar.activation(rx[:, h, :], pq[1 - h][:, :], ACT.Relu, bias=bias), "rx")
                        S(nc.scalar.activation(ab[:, h, :], pq[1 - h][:, :], ACT.Abs, bias=bias), "abs")
                        name(f"pq{1 - h}_empty", "abs")

                    def exponent():
                        S.wait("abs")
                        S(nc.scalar.activation(ab[:, :, :], ab[:, :, :], ACT.Exp, scale=-1.0), "e")

                    def square(f):
                        S.wait("e", f"factor{f % 2}")
                        S(nc.scalar.activation(sq[f % 2][:, :, :], ab[:, :, :], ACT.Square, scale=SPREAD,
                                               bias=keep[:, NCH + f:NCH + f + 1]), f"square{f % 2}")

                    def factor(f):
                        V.wait(f"square{f % 2}", "factor", f"da{i}")
                        V(nc.vector.scalar_tensor_tensor(dt[i][:, :, :], sq[f % 2][:, :, :], FACTORS[f][1],
                                                         ab[:, :, :] if f == 0 else dt[i][:, :, :], ALU.add, ALU.mult), "factor")
                        name(f"factor{f % 2}", "factor")

                    def finish():
                        V.wait("factor", "rx")
                        V(nc.vector.tensor_tensor(dt[i][:, :, :], rx[:, :, :], dt[i][:, :, :], ALU.add), f"dt{i}")
                        name("softplus", f"dt{i}")
                        G.wait(f"dt{i}", f"uz{i}", f"dtu_read{i}")
                        G(nc.gpsimd.tensor_tensor(dtu[i][:, :, :], dt[i][:, :, :], uz[i][:, 0:HF, :], ALU.mult), f"dtu{i}")

                    def of(stage, *args):
                        return lambda: stage(*args)

                    next_u = [[]] * 11 + [
                        [of(project, 0, W_U, (0, 1))], [of(project, 0, W_U, (2, 3))],
                        [of(keep_pre, 0), of(project, 1, W_U + P, (0, 1))], [of(project, 1, W_U + P, (2, 3))],
                        [of(keep_pre, 1)]]
                    if only_u:
                        return next_u
                    rest_ = [[of(project, 2, W_Z)],
                            [of(keep_pre, 2), of(project, 3, W_Z + P)],
                            [of(keep_pre, 3)],
                            [silu, x_project],
                            [keep_rank, high_part, of(dt_in, 0)],
                            [of(relu_abs, 0), rest_of_high],
                            [of(dt_in, 1), mid_part],
                            [of(relu_abs, 1), exponent, of(square, 0), low_part],
                            [of(square, 1), of(factor, 0)] + before[0:1],
                            [of(square, 2), of(factor, 1)] + before[1:2],
                            [of(square, 3), of(factor, 2)] + before[2:3],
                            [of(factor, 3)], [finish]] + [[]] * 3
                    return [x + y for x, y in zip(rest_, next_u)]

                def gate(j):
                    V.wait("summed", "projected", "w")
                    for h in range(HF):
                        V(nc.vector.scalar_tensor_tensor(yz[:, h, :], uz[j][:, h, :], wd[j][:, W_D + h:W_D + h + 1],
                                                         py[:, h * CH:(h + 1) * CH], ALU.mult, ALU.add), "py_empty")
                    G.wait("py_empty")
                    G(nc.gpsimd.tensor_tensor(yz[:, :, :], yz[:, :, :], uz[j][:, HF:2 * HF, :], ALU.mult), f"gated{j}")

                def out_project(j, slot):
                    def tiles(of):
                        M.wait(f"gated{j}", "pq0_empty")
                        for kt in of:
                            for h in range(HF):
                                mm(pq[0][:, kt * P:(kt + 1) * P], yz[:, h, kt * P:(kt + 1) * P], wd[j][:, W_O + h * D:W_O + (h + 1) * D],
                                   start=h == 0, stop=h == HF - 1, name="projected")

                    def store():
                        S.wait("projected")
                        S(nc.scalar.activation(flat(om[:, ds(slot, 1), :]), pq[0][:, :], ACT.Identity), "pq0_empty")
                    return [lambda: tiles((0, 1)), lambda: tiles((2, 3)), store]

                def add_up(n, b):
                    M.wait(f"hc{b}", "py_empty")
                    for h in range(HF):
                        mm(py[:, h * CH:(h + 1) * CH], ident[:, :], hc[b][:, h, :], start=n == 0, stop=n == NS - 1, name=f"summed{b}")
                    if n == NS - 1:
                        name("summed", f"summed{b}")

                def spread_b(n, i):
                    M.wait(f"bc{i}", f"low{i}", f"b_used{n % 2}")
                    mm(pb[n % 2][:, :], sel[0:96, n:n + 1].broadcast_to([96, P]), bc[i][0:96, :], name=f"b{n % 2}")
                    name(f"b_read{i}", f"b{n % 2}")

                def spread_c(n, i):
                    M.wait(f"bc{i}", f"low{i}", f"c_copied{n % 2}")
                    mm(pc[n % 2][:, :], sel[0:96, NS + n:NS + n + 1].broadcast_to([96, P]), bc[i][0:96, :], name=f"c_read{i}")
                    name(f"c{n % 2}", f"c_read{i}")

                def inflow(n, i):
                    b = n % 2
                    m = (i * NS + n) % 3
                    V.wait(f"b{b}", f"dtu{i}", f"scans{m}")
                    V(nc.vector.tensor_tensor(db[m][:, :, :], dtu[i][:, :, :], pb[b][:, :].unsqueeze(1).broadcast_to([P, HF, CH]),
                                              ALU.mult), f"db{m}")
                    name(f"dtu_read{i}", f"db{m}")
                    name(f"b_used{b}", f"db{m}")

                def decays(n, i):
                    r = (i * NS + n) % 5
                    S.wait(f"dt{i}", "w", f"state{r}")
                    for h in range(HF):
                        S(nc.scalar.activation(hh[r][:, h, :], dt[i][:, h, :], ACT.Exp,
                                               scale=wd[i][:, W_A + h * NS + n:W_A + h * NS + n + 1]), f"da{i}")
                        name(f"a{r}{h}", f"da{i}")

                def copy_c(n, i):
                    r = (i * NS + n) % 3
                    S.wait(f"c{n % 2}", f"hc{r}")
                    S(nc.scalar.activation(cs[r][:, :], pc[n % 2][:, :], ACT.Identity), "cs")
                    name(f"cs{r}", "cs")
                    name(f"c_copied{n % 2}", "cs")

                def scan_step(n, i, meanwhile):
                    r, m = (i * NS + n) % 5, (i * NS + n) % 3
                    ahead = lambda k: ((n + k) % NS, i if n + k < NS else i ^ 1)
                    decays(*ahead(1))
                    copy_c(*ahead(1))
                    inflow(*ahead(1))
                    spread_c(*ahead(2))
                    spread_b(*ahead(2))
                    V.wait(f"db{m}", f"st{i}")
                    for h in range(HF):
                        V.wait(f"a{r}{h}")
                        V(nc.vector.tensor_tensor_scan(hh[r][:, h, :], hh[r][:, h, :], db[m][:, h, :], st[:, i, n, h:h + 1],
                                                       ALU.mult, ALU.add), f"scan{r}")
                    name(f"scans{m}", f"scan{r}")
                    if n == 2:
                        gate(i ^ 1)
                    if n == 3:
                        add_up(0, (i * NS) % 3)
                    if n != 2:
                        add_up((n - 2) % NS, (i * NS + n - 2) % (2 * NS) % 3)
                    G.wait(f"scan{r}", f"cs{m}", f"summed{m}")
                    G(nc.gpsimd.tensor_tensor(hc[m][:, :, :], hh[r][:, :, :], cs[m][:, :].unsqueeze(1).broadcast_to([P, HF, CH]),
                                              ALU.mult), f"hc{m}")
                    G(nc.gpsimd.tensor_copy(st[:, i, n, :], hh[r][:, :, CH - 1]), f"state{r}")
                    name(f"kept{i}", f"state{r}")
                    for work in meanwhile:
                        work()

                V(nc.vector.memset(uz[1][:, :, :], 0.0), "uz1")
                V(nc.vector.memset(st[:, :, :, :], 0.0), "st")
                V.wait("uz1", "st")
                M.wait("w")
                S.wait("w")
                for works in prep(1, 0, 0, only_u=True) + prep(0, 0, NCH):
                    for work in works:
                        work()
                for step in (2 * NS - 2, 2 * NS - 1):
                    b = step % 3
                    V(nc.vector.memset(hc[b][:, :, :], 0.0), f"hc{b}")
                add_up(0, (2 * NS - 2) % 3)
                spread_b(0, 0)
                spread_c(0, 0)
                decays(0, 0)
                copy_c(0, 0)
                inflow(0, 0)
                spread_b(1, 0)
                spread_c(1, 0)
                with c.loop(NCH) as q:
                    first = prep(1, q + NCH, q + 1, out_project(1, q + (NCH + 1)))
                    second = prep(0, q + 1, q + (NCH + 1), out_project(0, q + 1))
                    for i, steps in enumerate((first, second)):
                        V.wait(f"kept{i}")
                        V(nc.vector.tensor_scalar(st[:, i, :, :], st[:, i, :, :], keep[:, ds(q, 1)], None, ALU.mult), f"st{i}")
                        for n in range(NS):
                            scan_step(n, i, steps[n])
                add_up(NS - 2, (2 * NS - 2) % 3)
                add_up(NS - 1, (2 * NS - 1) % 3)
                gate(1)
                for work in out_project(1, 2 * NCH + 1):
                    work()

                barrier()
                again = [lane(f"load_x_again{s}", nc.sync, 16)(nc.sync.dma_start(bx[:, s * 8:s * 8 + 8, :], a["x"][:, s * 8:s * 8 + 8, :]))
                         for s in range(4)]
                for g in (2, 3, 0, 1, 6, 7, 4, 5):
                    bnk = (pb[0], pb[1], pc[0], pq[0])[g % 4]
                    M.wait(f"turned{g % 4}")
                    mm(bnk[:, :], mirror[:, :], om[:, NCH + 2 + g, :], name="turned")
                    t = (g // 4) * TB + (3 - g % 4) * 4
                    V.wait(again[t // 8])
                    V.wait(V(nc.vector.scalar_tensor_tensor(bx[:, t:t + 4, :], bx[:, t:t + 4, :], 2.0,
                                                            view(om[:, 1 + t // 4, :], 4, D), ALU.mult, ALU.add)), "turned")
                    for kt in range(4):
                        V(nc.vector.tensor_tensor(bx[:, t + 3 - kt, :], bx[:, t + 3 - kt, :], bnk[:, kt * P:(kt + 1) * P], ALU.add),
                          f"turned{g % 4}")
                    V.wait(f"turned{g % 4}")
                    measure(range(t, t + 4))
                barrier()

        def experts(glu, layer, load_more):
            with ExitStack() as k:
                small, shared, weights, sorted_x = [lane(f"load{layer}_{s}", nc.sync, 16)
                                                    for s in ("small", "shared", "weights", "sorted_x")]
                scatter = lane(f"scatter{layer}", nc.gpsimd, 16, 0)
                return_y = lane(f"return{layer}_y", nc.gpsimd, 16, 0)
                load_y = [lane(f"load{layer}_y{s}", nc.sync, 16) for s in range(4)]
                q = (2 if glu else 1) * FF
                xsort = sb(k, "xsort", [P, ST + 3, D + 1])
                ysort = sb(k, "ysort", [P, ST, D])
                back = ysort[:, 0:NT, :]
                wx = sb(k, "wx", [P, NE, q + FF])
                x1 = xn[:, :, 0:D]
                rc = sb(k, "rc", [P, RC_N])
                before = sb(k, "before", [P, P], BF16)
                every = sb(k, "every", [P, P], BF16)
                rw = sb(k, "rw", [P, NE])
                lg = sb(k, "lg", [P, NT, NE])
                hot = sb(k, "hot", [P, NT, NE])
                hot_b = sb(k, "hot_b", [P, NT, NE], BF16)
                work_ = sb(k, "work", [P, NT, NE])
                incl = sb(k, "incl", [P, NE, NT])
                tot = sb(k, "tot", [P, NE, NT])
                top = sb(k, "top", [P, NT])
                factor2 = sb(k, "factor2", [P, NT])
                tiles_of = sb(k, "tiles_of", [P, NE])
                ends = sb(k, "ends", [P, NE])
                cmp_ = sb(k, "cmp", [P, ST + 3, NE])
                exf = sb(k, "exf", [P, ST + 3])
                expert = sb(k, "expert", [P, ST + 3], I32)
                pos = sb(k, "pos", [P, NT], U32)
                token = sb(k, "token", [P, ST], U32)
                xs4 = [sb(k, f"xs4{u}", [P, 4, D]) for u in range(4)]
                xt4 = [sb(k, f"xt4{u}", [P, 4 * P]) for u in range(4)]
                sg = xt4[2:4]
                hid = [flat(x[:, :, :]) for x in xs4[2:4]]
                ht = [sb(k, f"ht{u}", [P, FF]) for u in range(2)]
                pbk = [bank(k, f"bank{u}") for u in range(8)]
                pt, pl, pu, pg, pw = pbk[0:2], pbk[2], pbk[3:5], pbk[5:7], pbk[7]
                p_tr, p_lg = pt + pu, pg + [pl, pw]
                if glu:
                    xall = flat(ysort[:, 0:NT, :])
                    ws = sb(k, "ws", [P, 3 * FF])
                    ht4 = [sb(k, f"ht4{u}", [P, 4 * P]) for u in range(2)]
                else:
                    brb = sb(k, "brb", [P, NE])
                    b1 = sb(k, "b1", [P, NE * FK])
                    b2 = sb(k, "b2", [P, NE, D])

                small(nc.sync.dma_start(rw[:, :], a[f"rw{layer}"]))
                small(nc.sync.dma_start(before[:, :], a["before"]))
                small(nc.sync.dma_start(every[:, :], a["every"]))
                if not glu:
                    small(nc.sync.dma_start(brb[:, :], a["br"].partition_broadcast(P)))
                    small(nc.sync.dma_start(b1[:, :], a["b1"]))
                    small(nc.sync.dma_start(b2[:, :, :], a["b2"].partition_broadcast(P)))
                in_r = small(nc.sync.dma_start(rc[:, :], a["rc"]))
                if glu:
                    in_s = shared(nc.sync.dma_start(ws[:, :], a["shared_w"]))
                    no_expert = V(nc.vector.memset(wx[:, NE - 1:NE, :], 0.0))
                else:
                    no_expert = in_r
                last = NE - 1 if glu else NE
                weights(nc.sync.dma_start(wx[:, 0:4, :], a[f"l{layer}_w"][:, 0:4, :]))
                in_e = weights(nc.sync.dma_start(wx[:, 4:last, :], a[f"l{layer}_w"][:, 4:last, :]))
                loaded = load_more()
                V(nc.vector.memset(xsort[:, ST:ST + 3, :], 0.0), "xsort_end")

                def transpose_x(g, u):
                    V.wait("x1_v", "x1_s", "x1_g", f"xs4_read{u}")
                    V(nc.vector.tensor_copy(xs4[u][:, :, :], x1[:, ds(g * 4, 4), :]), f"xs4{u}")
                    M.wait(f"xs4{u}", f"xt4{u}")
                    for kt in range(4):
                        tr(p_tr[u][:, kt * P:(kt + 1) * P], xs4[u][:, kt, :], f"xs4_read{u}")
                    S.wait(f"xs4_read{u}", f"logits{u}", *(["xall"] if glu else []))
                    S(nc.scalar.activation(xt4[u][:, :], p_tr[u][:, :], ACT.Identity), f"xt4{u}")

                def keep_x(g, u):
                    if glu:
                        S.wait(f"xt4{u}")
                        S(nc.scalar.activation(xall[:, ds(g * (4 * P), 4 * P)], xt4[u][:, :], ACT.Identity), "xall")

                def logits(g, u):
                    M.wait(f"xt4{u}", f"lg{u}", in_r)
                    for kt in range(4):
                        mm(p_lg[u][:, kt * NE:(kt + 1) * NE], xt4[u][:, kt * P:(kt + 1) * P], rw[:, :], name=f"logits{u}")
                    V.wait(f"logits{u}")
                    if glu:
                        V(nc.vector.tensor_copy(lg[:, ds(g * 4, 4), :], view(p_lg[u], 4, NE)), f"lg{u}")
                    else:
                        V(nc.vector.tensor_tensor(lg[:, ds(g * 4, 4), :], view(p_lg[u], 4, NE),
                                                  brb[:, :].unsqueeze(1).broadcast_to([P, 4, NE]), ALU.add), f"lg{u}")

                M.wait(in_c)
                with c.loop(NT // 16) as gi:
                    for stage in (transpose_x, keep_x, logits):
                        for u in range(4):
                            stage(gi * 4 + u, u)

                def step(ins, name=None):
                    V.wait(V(ins, name))
                over_e = lambda v: v.unsqueeze(2).broadcast_to([P, NT, NE])
                V.wait("lg0", "lg1", "lg2", "lg3", in_r)
                step(nc.vector.tensor_reduce(top[:, :], lg[:, :, :], AX.X, ALU.max))
                step(nc.vector.tensor_tensor(lg[:, :, :], lg[:, :, :], over_e(top[:, :]), ALU.subtract), "shifted")
                if glu:
                    S.wait("shifted")
                    S(nc.scalar.activation(work_[:, :, :], lg[:, :, :], ACT.Exp), "exps")
                step(nc.vector.tensor_scalar(hot[:, :, :], lg[:, :, :], 0.0, None, ALU.is_ge))
                step(nc.vector.tensor_tensor(hot[:, :, :], hot[:, :, :], rc[:, RC_REV:RC_REV + NE].unsqueeze(1).broadcast_to([P, NT, NE]),
                                             ALU.mult))
                step(nc.vector.tensor_reduce(top[:, :], hot[:, :, :], AX.X, ALU.max))
                step(nc.vector.tensor_tensor(hot[:, :, :], hot[:, :, :], over_e(top[:, :]), ALU.is_equal))
                step(nc.vector.tensor_copy(hot_b[:, :, :], hot[:, :, :]), "hot_b")
                M.wait("hot_b", "xt41")
                mm(pl[:, 0:NT * NE], before[:, :], flat(hot_b[:, :, :]))
                mm(pt[1][:, 0:NT * NE], every[:, :], flat(hot_b[:, :, :]), name="ranks")
                if glu:
                    V.wait("exps")
                    step(nc.vector.tensor_reduce(factor2[:, :], work_[:, :, :], AX.X, ALU.add))
                    step(nc.vector.reciprocal(factor2[:, :], factor2[:, :]))
                    step(nc.vector.tensor_scalar(factor2[:, :], factor2[:, :], 2.0, None, ALU.mult), "factor2")
                V.wait("ranks")
                step(nc.vector.tensor_copy(tot[:, :, :], view(pt[1], NT, NE).rearrange("p t e -> p e t")))
                step(nc.vector.tensor_tensor_scan(flat(incl[:, :, :]), rc[:, RC_RUN:RC_RUN + NE * NT], flat(tot[:, :, :]), 0.0,
                                                  ALU.mult, ALU.add))
                step(nc.vector.tensor_tensor(tot[:, :, :], incl[:, :, :], tot[:, :, :], ALU.subtract))
                exceeds = flat(work_[:, :, :]).rearrange("p (e m) -> p e m", e=NE)
                step(nc.vector.tensor_tensor(exceeds,
                                             incl[:, :, NT - 1:NT].broadcast_to([P, NE, NT]),
                                             rc[:, RC_MULT:RC_MULT + NT].unsqueeze(1).broadcast_to([P, NE, NT]), ALU.is_gt))
                step(nc.vector.tensor_reduce(tiles_of[:, :], exceeds, AX.X, ALU.add))
                step(nc.vector.tensor_tensor_scan(ends[:, :], rc[:, RC_ONE:RC_ONE + NE], tiles_of[:, :], 0.0, ALU.mult, ALU.add))
                step(nc.vector.tensor_tensor(tiles_of[:, :], ends[:, :], tiles_of[:, :], ALU.subtract))
                step(nc.vector.scalar_tensor_tensor(tot[:, :, :], tiles_of[:, :].unsqueeze(2).broadcast_to([P, NE, NT]), float(P),
                                                    tot[:, :, :], ALU.mult, ALU.add))
                step(nc.vector.tensor_tensor(work_[:, :, :], view(pl, NT, NE), tot[:, :, :].rearrange("p e t -> p t e"), ALU.add))
                step(nc.vector.tensor_tensor(work_[:, :, :], work_[:, :, :], hot[:, :, :], ALU.mult))
                step(nc.vector.tensor_reduce(top[:, :], work_[:, :, :], AX.X, ALU.add))
                step(nc.vector.tensor_copy(pos[:, :], top[:, :]), "pos")
                step(nc.vector.tensor_tensor(cmp_[:, :, :], rc[:, RC_J:RC_J + ST + 3].unsqueeze(2).broadcast_to([P, ST + 3, NE]),
                                             ends[:, :].unsqueeze(1).broadcast_to([P, ST + 3, NE]), ALU.is_ge))
                step(nc.vector.tensor_reduce(exf[:, :], cmp_[:, :, :], AX.X, ALU.add))
                step(nc.vector.tensor_scalar(exf[:, :], exf[:, :], float(NE - 1), None, ALU.min))
                step(nc.vector.tensor_copy(expert[:, :], exf[:, :]), "expert")

                G.wait("pos", "x1_v", "x1_s", "x1_g", "padded")
                for t in range(NT):
                    sent = scatter(nc.gpsimd.indirect_dma_start(
                        out=xsorted[layer], out_offset=bass.IndirectOffsetOnAxis(ap=pos[:, t:t + 1], axis=0),
                        in_=xn[:, t, :], in_offset=None))
                SY.wait(sent)
                for s in range(4):
                    t = slice(s * ST // 4, (s + 1) * ST // 4)
                    in_xs = sorted_x(nc.sync.dma_start(xsort[:, t, :], xsorted[layer].rearrange("(t p) d -> p t d", p=P)[:, t, :]))

                if glu:
                    M.wait(in_s, "xall", "lg0", "lg1", "lg2", "lg3")
                    def hidden(g, f):
                        u = f % 2
                        M.wait(f"ht4{u}")
                        mm(pu[u][:, :], ws[:, f * P:(f + 1) * P], xall[:, ds(g * (4 * P), 4 * P)])
                        mm(pg[u][:, :], ws[:, FF + f * P:FF + (f + 1) * P], xall[:, ds(g * (4 * P), 4 * P)], name=f"ug{u}")
                        S.wait(f"ug{u}", f"ht4{u}")
                        S(nc.scalar.activation(sg[u][:, :], pg[u][:, :], ACT.Silu), f"sg{u}")
                        V.wait(f"sg{u}", f"down{u}")
                        V(nc.vector.tensor_tensor(ht4[u][:, :], pu[u][:, :], sg[u][:, :], ALU.mult), f"ht4{u}")

                    def down(f):
                        u = f % 2
                        M.wait(f"ht4{u}", "yt_read")
                        mm(pw[:, :], ws[:, 2 * FF + f * P:2 * FF + (f + 1) * P], ht4[u][:, :], start=f == 0, stop=f == FK - 1,
                           name=f"down{u}")
                        if f == FK - 1:
                            S.wait(f"down{u}", "yt4_read")
                            S(nc.scalar.activation(ht[0][:, :], pw[:, :], ACT.Identity), "yt_read")

                    def finish(g):
                        M.wait("yt_read", "added")
                        for kt in range(4):
                            tr(pt[0][:, kt * P:(kt + 1) * P], ht[0][:, kt * P:(kt + 1) * P], "yt4_read")
                        V.wait("yt4_read")
                        V(nc.vector.tensor_tensor(bx[:, ds(g * 4, 4), :], x1[:, ds(g * 4, 4), :], view(pt[0], 4, P), ALU.add), "added")

                    def four_tiles(g, first=False):
                        hidden(g, 0)
                        if not first:
                            down(FK - 1)
                        hidden(g, 1)
                        if not first:
                            finish(g - 1)
                        down(0)
                        for f in range(2, FK):
                            hidden(g, f)
                            down(f - 1)

                    four_tiles(0, first=True)
                    with c.loop(NT // 4 - 1) as g:
                        four_tiles(g + 1)
                    down(FK - 1)
                    finish(NT // 4 - 1)
                    V.wait("added")
                    S.wait("added")

                def copy_xs(j, u):
                    V.wait(f"xs_read{u}", "xsort_end", in_xs)
                    V(nc.vector.tensor_copy(xs4[u][:, 0, :], flat(xsort[:, ds(j, 1), 0:D])), f"xs{u}")

                def turn_xs(u):
                    M.wait(f"xs{u}", f"xt{u}")
                    tr(pt[u][:, 0:P], xs4[u][:, 0, :], f"xs_read{u}")
                    S.wait(f"xs_read{u}", f"ug{u}")
                    S(nc.scalar.activation(xt4[u][:, 0:P], pt[u][:, 0:P], ACT.Identity), f"xt{u}")

                e_pe = [nc.tensor.alloc_register(unused(f"expert_pe{r}")) for r in range(4)]
                e_v = [nc.vector.alloc_register(unused(f"expert_v{r}")) for r in range(3)]

                def held(engine, reg):
                    return engine.snap(reg, min_val=0, max_val=NE - 1)

                def load_pe(j):
                    nc.tensor.reg_load(e_pe, expert[0:1, ds(j, 4)])

                def load_v(j):
                    if not glu:
                        nc.vector.reg_load(e_v, expert[0:1, ds(j, 3)])

                def products_in(u, e):
                    M.wait(f"xt{u}", f"hid{u}")
                    if glu:
                        mm(pu[u][:, :], xt4[u][:, 0:P], flat(wx[:, ds(e, 1), 0:FF]))
                        mm(pg[u][:, :], xt4[u][:, 0:P], flat(wx[:, ds(e, 1), FF:2 * FF]), name=f"ug{u}")
                        S.wait(f"ug{u}", f"hid{u}")
                        S(nc.scalar.activation(sg[u][:, :], pg[u][:, :], ACT.Silu), f"sg{u}")
                    else:
                        mm(pu[u][:, :], xt4[u][:, 0:P], flat(wx[:, ds(e, 1), 0:FF]), name=f"ug{u}")
                        S.wait(f"ug{u}", f"hid_read{u}")
                        S(nc.scalar.activation(hid[u][:, :], pu[u][:, :], ACT.Identity), f"hid{u}")

                def gate_hidden(u):
                    if glu:
                        V.wait(f"sg{u}", f"hid_read{u}")
                        V(nc.vector.tensor_tensor(hid[u][:, :], pu[u][:, :], sg[u][:, :], ALU.mult), f"hid{u}")

                def turn_hidden(u, bias_of):
                    M.wait(f"hid{u}", "ht")
                    for f in range(FK):
                        tr(pl[:, f * P:(f + 1) * P], hid[u][:, f * P:(f + 1) * P], f"hid_read{u}")
                    V.wait(f"hid_read{u}", f"y{u}")
                    if glu:
                        V(nc.vector.tensor_copy(ht[u][:, :], pl[:, :]), "ht")
                    else:
                        e = held(nc.vector, bias_of)
                        for f in range(FK):
                            V(nc.vector.tensor_scalar(ht[u][:, f * P:(f + 1) * P], pl[:, f * P:(f + 1) * P],
                                                      b1[:, ds(e * FK + f, 1)], 0.0, ALU.add, ALU.max), "ht")
                    name(f"ht{u}", "ht")

                def products_out(j, u, e, bias_of):
                    M.wait(f"ht{u}", f"ysort{u ^ 1}")
                    for f in range(FK):
                        mm(pw[:, 0:P], ht[u][:, f * P:(f + 1) * P], flat(wx[:, ds(e, 1), q + f * P:q + (f + 1) * P]),
                           start=f == 0, stop=f == FK - 1, name=f"y{u}")
                    if glu:
                        S.wait(f"y{u}")
                        S(nc.scalar.activation(flat(ysort[:, ds(j, 1), :]), pw[:, 0:P], ACT.Identity), f"ysort{u}")
                    else:
                        e = held(nc.vector, bias_of)
                        V.wait(f"y{u}")
                        V(nc.vector.tensor_tensor(flat(ysort[:, ds(j, 1), :]), pw[:, 0:P], flat(b2[:, ds(e, 1), :]),
                                                  ALU.add), f"ysort{u}")

                M.wait(in_e, no_expert, "expert")
                V.wait(in_e, "expert", in_xs)
                V(nc.vector.tensor_copy(token[:, :], xsort[:, 0:ST, D]), "token")
                load_pe(0)
                load_v(0)
                for j in range(2):
                    copy_xs(j, j)
                    turn_xs(j)
                    products_in(j, held(nc.tensor, e_pe[j]))
                    gate_hidden(j)
                for j in (2, 3):
                    copy_xs(j, j - 2)
                    turn_xs(j - 2)
                turn_hidden(0, e_v[0])
                with c.loop(ST // 2 - 1) as ji:
                    first = ji * 2
                    products_in(0, held(nc.tensor, e_pe[2]))
                    copy_xs(first + 4, 0)
                    turn_hidden(1, e_v[1])
                    gate_hidden(0)
                    products_out(first, 0, held(nc.tensor, e_pe[0]), e_v[0])
                    name("in_loop0", "ysort0")
                    turn_xs(0)
                    products_in(1, held(nc.tensor, e_pe[3]))
                    last_pe = held(nc.tensor, e_pe[1])
                    load_pe(first + 2)
                    copy_xs(first + 5, 1)
                    turn_hidden(0, e_v[2])
                    gate_hidden(1)
                    last_v = None if glu else held(nc.vector, e_v[1])
                    load_v(first + 2)
                    products_out(first + 1, 1, last_pe, last_v)
                    name("in_loop1", "ysort1")
                    turn_xs(1)
                products_out(ST - 2, 0, held(nc.tensor, e_pe[0]), e_v[0])
                turn_hidden(1, e_v[1])
                products_out(ST - 1, 1, held(nc.tensor, e_pe[1]), e_v[1])
                G.wait("token")
                for j in range(ST):
                    mark = c.at_iteration(f"in_loop{j % 2}", j // 2) if j < ST - 2 else f"ysort{j % 2}"
                    G.wait(mark)
                    sent = return_y(nc.gpsimd.indirect_dma_start(
                        out=ytoken, out_offset=bass.IndirectOffsetOnAxis(ap=token[:, j:j + 1], axis=0),
                        in_=ysort[:, j, :], in_offset=None))

                SY.wait(sent)
                per = NT // 4
                got = [load_y[s](nc.sync.dma_start(back[:, s * per:(s + 1) * per, :],
                                                   ytoken.rearrange("(t p) d -> p t d", p=P)[:, s * per:(s + 1) * per, :]))
                       for s in range(4)]
                for s in range(4):
                    t = slice(s * per, (s + 1) * per)
                    V.wait(got[s])
                    if glu:
                        for one in range(s * per, (s + 1) * per):
                            V(nc.vector.scalar_tensor_tensor(bx[:, one, :], back[:, one, :], factor2[:, one:one + 1], bx[:, one, :],
                                                             ALU.mult, ALU.add), "bx")
                    else:
                        V(nc.vector.tensor_tensor(bx[:, t, :], x1[:, t, :], back[:, t, :], ALU.add), "bx")
                    V.wait("bx")
                    mine = range(s * per, (s + 1) * per)
                    measure(mine)
                    normalise(mine, "S")
                    if not glu:
                        SY.wait("x1_s")
                        L["out"](nc.sync.dma_start(out[:, t, :], x1[:, t, :]))
                if not glu:
                    SY.wait(Mark(L["out"], L["out"].at, []))
                barrier()
                return loaded

        def layer1_retention(rot, held_, in_t):
            x1 = xn[:, :, 0:D]
            with ExitStack() as k:
                small = lane("load_ret_small", nc.sync, 16)
                wqk, wvg, wp, bqk, bvg, bp = held_
                C = P
                stats2 = sb(k, "stats2", [P, B, 6])
                res2 = sb(k, "res2", [P, B, D])
                decay = sb(k, "decay", [P, NH, C])
                edge = sb(k, "edge", [P, 2, C])
                heads4 = sb(k, "heads4", [P, 4])
                block = sb(k, "block", [P, EV])
                gam = sb(k, "gam", [P, 1])
                state = sb(k, "state", [P, B, EV])
                inflow_ = sb(k, "kv_in", [P, B, EV])
                two = lambda n, shape: [sb(k, f"{n}{u}", shape) for u in range(2)]
                xs, xt_ = two("xs_r", [P, B, D]), two("xt_r", [P, B * P])
                ra, rb = two("ra", [P, B, C]), two("rb", [P, B, C])
                qr, kr = two("qr", [P, B, C]), two("kr", [P, B, C])
                q2, k2 = two("q2_", [P, B, C]), two("k2_", [P, B, C])
                k2t = two("k2t", [P, B, C])
                qx = two("qx", [P, B, 4, C])
                vg = two("vg", [P, B, 2 * EV])
                gt = two("gt", [P, B, EV])
                sm = two("sm", [P, NH, C])
                og = two("og", [P, B * NH, DV])
                og2 = sb(k, "og2", [P, B * NH, DV])
                mu = sb(k, "mu", [P, B * NH])
                rs = sb(k, "rs", [P, B * NH])
                gy = sb(k, "gy", [P, B * EV])
                gyt = sb(k, "gyt", [P, B * EV])
                p_turn, p_q, p_k, p_vg, p_s0, p_s1, p_out, p_kv = [bank(k, f"pr{u}") for u in range(8)]
                p_s = (p_s0, p_s1)

                for dst, src in ((edge[:, :, :], "edge"), (heads4[:, :], "heads4"), (block[:, :], "block"), (gam[:, :], "gam"),
                                 (decay[:, :, :], "decay")):
                    in_s = small(nc.sync.dma_start(dst, a[src]))
                V(nc.vector.memset(state[:, :, :], 0.0), "state_r")

                V.wait("x1_v", "x1_s", "x1_g", in_t)
                G.wait("x1_v", "x1_s", "x1_g", in_t)
                for s in range(4):
                    t = slice(s * NT // 4, (s + 1) * NT // 4)
                    G(nc.gpsimd.tensor_tensor(bx[:, t, :], x1[:, t, :], bp[:, :].unsqueeze(1).broadcast_to([P, NT // 4, D]),
                                              ALU.add), "x1_bp")
                G.wait(in_s)
                M.wait(in_t)
                V.wait(in_s)
                by_batch = lambda v: v.rearrange("p (b c) d -> p b c d", b=B)
                over_b = lambda v: v.unsqueeze(1).broadcast_to([P, B, C])

                def copy_x(c_, u):
                    V.wait(f"x_turned{u}")
                    V(nc.vector.tensor_copy(xs[u][:, :, :].unsqueeze(2), by_batch(x1[:, :, :])[:, :, ds(c_, 1), :]), f"xs_r{u}")

                def turn_x(u):
                    M.wait(f"xs_r{u}", "xt_r", "k2t")
                    for b in range(B):
                        tr(p_turn[:, b * P:(b + 1) * P], xs[u][:, b, :], f"x_turned{u}")
                    S.wait(f"x_turned{u}", f"vg_made{u}", "k_made")
                    S(nc.scalar.activation(xt_[u][:, :], p_turn[:, 0:B * P], ACT.Identity), "xt_r")

                def project_qk(c_, u):
                    M.wait("xt_r", "rot_q", "rot_k")
                    for j, (bnk, nm) in enumerate(((p_q, "q_made"), (p_q, "q_made"), (p_k, "k_made"), (p_k, "k_made"))):
                        mm(bnk[:, (j % 2) * B * C:(j % 2 + 1) * B * C], wqk[:, j * D:(j + 1) * D], xt_[u][:, :], name=nm)

                def rotate(c_, u):
                    for j, (bnk, dst, nm, far) in enumerate(((p_q, qr, "q", q2), (p_k, kr, "k", k2))):
                        V.wait(f"{nm}_made", f"{nm}_summed")
                        for r, part in enumerate((ra[j], rb[j])):
                            V(nc.vector.scalar_tensor_tensor(part[:, :, :], view(bnk, B, C, r * B * C), bqk[:, 2 * j + r:2 * j + r + 1],
                                                             rot[:, 2 * j + r, ds(c_ * C, C)].unsqueeze(1).broadcast_to([P, B, C]),
                                                             ALU.add, ALU.mult), f"rot_{nm}")
                        G.wait(f"rot_{nm}", "scores", "qx", "k2_turned", "from_state")
                        G(nc.gpsimd.tensor_tensor(dst[u][:, :, :], ra[j][:, :, :], rb[j][:, :, :], ALU.add), f"{nm}_summed")
                        G.wait(f"{nm}_summed")
                        if nm == "q":
                            G(nc.gpsimd.tensor_tensor(qx[u][:, :, :, :], qr[u][:, :, :].unsqueeze(2).broadcast_to([P, B, 4, C]),
                                                      heads4[:, :].unsqueeze(1).unsqueeze(3).broadcast_to([P, B, 4, C]), ALU.mult), "qx")
                            name(f"qx{u}", "qx")
                        G(nc.gpsimd.tensor_tensor(far[u][:, :, :], dst[u][:, :, :], over_b(edge[:, j, :]), ALU.mult), f"{nm}2_{u}")

                def project_vg(b, u):
                    M.wait("vg", "gyt")
                    mm(p_vg[:, :], xt_[u][:, b * P:(b + 1) * P], wvg[:, :], name=f"vg_made{u}")
                    V.wait(f"vg_made{u}", f"kv{u}", f"within{u}", f"gt{u}")
                    V(nc.vector.tensor_tensor(vg[u][:, b, :], p_vg[:, :], bvg[:, :], ALU.add), "vg")
                    name(f"vg{u}", "vg")

                def gates(u):
                    S.wait(f"vg{u}", f"gy{u}")
                    S(nc.scalar.activation(gt[u][:, :, :], vg[u][:, :, EV:2 * EV], ACT.Silu), f"gt{u}")

                def scores(b, u):
                    for s in range(2):
                        M.wait(f"qx{u}", "k_summed", f"decayed{s}")
                        half = slice(s * 64, (s + 1) * 64)
                        mm(p_s[s][:, :], kr[u][half, b, :], flat(qx[u][half, b, :, :]), name="scores")
                        V.wait("scores", f"within_b{b}")
                        V(nc.vector.tensor_tensor(sm[b][:, 4 * s:4 * s + 4, :], view(p_s[s], 4, C), decay[:, 4 * s:4 * s + 4, :],
                                                  ALU.mult), f"decayed{s}")
                    name(f"sm{b}", "decayed1")

                def outputs(b, u):
                    M.wait(f"q2_{u}", "state_r", "og", f"sm{b}", f"vg{u}")
                    mm(p_out[:, b * EV:(b + 1) * EV], q2[u][:, b, :], state[:, b, :], stop=False, name="from_state")
                    for h in range(NH):
                        mm(p_out[:, b * EV + h * DV:b * EV + (h + 1) * DV], sm[b][:, h, :], vg[u][:, b, h * DV:(h + 1) * DV],
                           start=False, stop=h == NH - 1, name=f"within{u}")
                    name(f"within_b{b}", f"within{u}")

                def take_out(u):
                    S.wait(f"within{u}", f"gy{u}")
                    S(nc.scalar.activation(og[u][:, :, :].rearrange("p g v -> p (g v)"), p_out[:, :], ACT.Identity), "og")
                    name(f"og{u}", "og")

                def turn_k(u):
                    M.wait(f"k2_{u}", "xt_r", "k2t")
                    for b in range(B):
                        tr(p_turn[:, 256 + b * P:256 + (b + 1) * P], k2[u][:, b, :], "k2_turned")
                    S.wait("k2_turned", f"kv{u}")
                    S(nc.scalar.activation(k2t[u][:, :, :], view(p_turn, B, P, 256), ACT.Identity), "k2t")

                def update_state(u):
                    M.wait("k2t", f"vg{u}", "kv_in", "res_kept")
                    for b in range(B):
                        mm(p_kv[:, b * EV:(b + 1) * EV], k2t[u][:, b, :], vg[u][:, b, 0:EV], name=f"kv{u}")
                    V.wait(f"kv{u}", "state_r")
                    V(nc.vector.tensor_tensor(inflow_[:, :, :], view(p_kv, B, EV), block[:, :].unsqueeze(1).broadcast_to([P, B, EV]),
                                              ALU.mult), "kv_in")
                    V.wait("kv_in", "from_state")
                    V(nc.vector.scalar_tensor_tensor(state[:, :, :], state[:, :, :], gam[:, 0:1], inflow_[:, :, :],
                                                     ALU.mult, ALU.add), "state_r")

                over_v = lambda v: v[:, :].unsqueeze(2).broadcast_to([P, B * NH, DV])
                def centre(u):
                    V.wait(f"og{u}")
                    V.wait(V(nc.vector.tensor_reduce(mu[:, :], og[u][:, :, :], AX.X, ALU.add)))
                    V.wait(V(nc.vector.tensor_scalar(mu[:, :], mu[:, :], 1.0 / DV, None, ALU.mult)))
                    V(nc.vector.tensor_tensor(og[u][:, :, :], og[u][:, :, :], over_v(mu), ALU.subtract), f"centred{u}")
                    S.wait(f"centred{u}", "rs_sum")
                    S(nc.scalar.activation(og2[:, :, :], og[u][:, :, :], ACT.Square), "og2")

                def spread_of(u):
                    V.wait("og2", "rs")
                    V(nc.vector.tensor_reduce(rs[:, :], og2[:, :, :], AX.X, ALU.add), "rs_sum")
                    S.wait("rs_sum")
                    S(nc.scalar.activation(rs[:, :], rs[:, :], ACT.Sqrt, bias=eps[:, 0:1], scale=1.0 / DV), "rs_root")

                def normed(u):
                    V.wait("rs_root")
                    V(nc.vector.reciprocal(rs[:, :], rs[:, :]), "rs")
                    V.wait("rs")
                    V(nc.vector.tensor_tensor(og[u][:, :, :], og[u][:, :, :], over_v(rs), ALU.mult), f"normed{u}")
                    G.wait(f"normed{u}", f"gt{u}", "gy_turned")
                    G(nc.gpsimd.tensor_tensor(gy[:, :], flat(og[u][:, :, :]), flat(gt[u][:, :, :]), ALU.mult), f"gy{u}")

                def turn_y(u):
                    M.wait(f"gy{u}", "vg", "gyt")
                    for j in range(4):
                        tr(p_vg[:, j * P:(j + 1) * P], gy[:, j * P:(j + 1) * P], "gy_turned")
                    S.wait("gy_turned", "out_made")
                    S(nc.scalar.activation(gyt[:, :], p_vg[:, :], ACT.Identity), "gyt")

                def project_out(c_, u):
                    M.wait("gyt", "kv_in", "res_kept")
                    for b in range(B):
                        for j in range(2):
                            mm(p_kv[:, b * P:(b + 1) * P], gyt[:, (2 * b + j) * P:(2 * b + j + 1) * P], wp[:, j, :],
                               start=j == 0, stop=j == 1, name="out_made")
                    V.wait("out_made", "x1_bp", "stats_kept", "res_kept")
                    res = by_batch(bx[:, :, :])[:, :, ds(c_, 1), :]
                    V(nc.vector.tensor_tensor(res2[:, :, :].unsqueeze(2), res, view(p_kv, B, P).unsqueeze(2), ALU.add), "out_r")
                    V.wait("out_r")
                    V(nc.vector.tensor_tensor(res, res, view(p_kv, B, P).unsqueeze(2), ALU.add), "res_kept")
                    for b in range(B):
                        V(nc.vector.bn_stats(stats2[:, b, :], res2[:, b, :]), "stats2")
                    V.wait("stats2")
                    V(nc.vector.tensor_scalar(by_batch(stats[:, :, :])[:, :, ds(c_, 1), :], stats2[:, :, :].unsqueeze(2), 1.0, None,
                                              ALU.mult), "stats_kept")

                def turn_of(c_, u, norm=True, out_=True, after=True, copy=True):
                    w_ = u ^ 1
                    if after:
                        turn_x(w_)
                    scores(0, u)
                    if out_:
                        turn_y(u)
                    if after:
                        project_qk(c_ + 1, w_)
                    if out_:
                        project_out(c_ - 2, u)
                    scores(1, u)
                    if norm:
                        centre(w_)
                    if after:
                        rotate(c_ + 1, w_)
                    outputs(0, u)
                    turn_k(u)
                    if norm:
                        spread_of(w_)
                    if after:
                        project_vg(0, w_)
                    outputs(1, u)
                    if norm:
                        normed(w_)
                    take_out(u)
                    if after:
                        project_vg(1, w_)
                        gates(w_)
                    if copy:
                        copy_x(c_ + 2, u)
                    update_state(u)

                copy_x(0, 0)
                turn_x(0)
                copy_x(1, 1)
                project_qk(0, 0)
                rotate(0, 0)
                project_vg(0, 0)
                project_vg(1, 0)
                gates(0)
                turn_of(0, 0, norm=False, out_=False)
                turn_of(1, 1, out_=False)
                with c.loop(TB // 2 - 2) as ci:
                    turn_of(ci * 2 + 2, 0)
                    turn_of(ci * 2 + 3, 1)
                turn_of(TB - 2, 0, copy=False)
                turn_of(TB - 1, 1, after=False, copy=False)
                turn_y(0)
                project_out(TB - 2, 0)
                centre(1)
                spread_of(1)
                normed(1)
                turn_y(1)
                project_out(TB - 1, 1)
                V.wait("stats_kept")
                combine_stats(range(NT))
                barrier()

        layer0_mamba()
        with ExitStack() as k:
            xn = sb(k, "xn", [P, NT, D + 1])
            V.wait(in_c)
            V(nc.vector.tensor_copy(xn[:, :, D], number[:, :]), "x1_v")
            normalise()
            with ExitStack() as k_rot:
                rot = sb(k_rot, "rot", [P, 4, T])
                tables = lane("load_tables", nc.sync, 16)

                shapes = {"wqk": [P, 4 * D], "wvg": [P, 2 * EV], "wp": [P, 2, D], "bqk": [P, 4], "bvg": [P, 2 * EV], "bp": [P, D]}
                held_ = [sb(k_rot, n, shape) for n, shape in shapes.items()]

                def load_tables():
                    for (n, shape), t in zip(shapes.items(), held_):
                        dst = t[:, :, :] if len(shape) == 3 else t[:, :]
                        tables(nc.sync.dma_start(dst, a[n].partition_broadcast(P) if n in ("bvg", "bp") else a[n]))
                    return [tables(nc.sync.dma_start(rot[:, r, :], a["rot"][:, r, :])) for r in range(4)][-1]

                in_t = experts(True, 0, load_tables)
                layer1_retention(rot, held_, in_t)
            normalise()
            experts(False, 1, lambda: None)
        return c.per, c.later


def constants():
    k = {"ident": np.eye(P, dtype=np.float32), "mirror": np.eye(P, dtype=np.float32)[::-1]}
    keep = np.array([c % (NCH // B) > 0 for c in range(NCH)] + [f[0] for f in FACTORS], np.float32)
    k["keep"] = np.broadcast_to(keep, (P, len(keep)))
    k["number"] = (np.arange(NT)[None, :] * P + np.arange(P)[:, None]).astype(np.float32)
    k["pads"] = np.zeros((ST * P, D + 1), np.float32)
    k["pads"][:, D] = NT * P + np.arange(ST * P)
    k["sel"] = (np.arange(96)[:, None] % 32 == np.arange(32)).astype(mybir.dt.np(BF16))
    k["before"] = np.triu(np.ones((P, P), np.float32), 1).astype(mybir.dt.np(BF16))
    k["every"] = np.ones((P, P), mybir.dt.np(BF16))
    run = np.ones((NE, NT), np.float32)
    run[:, 0] = 0.0
    row = np.concatenate([NE - np.arange(NE), run.reshape(-1), P * np.arange(NT), np.ones(NE), np.arange(ST + 3)])
    f32 = np.float32
    pos = np.arange(T, dtype=f32)
    scale = ((np.arange(0, D, 2, dtype=f32) + f32(0.4 * D)) / f32(1.4 * D))[:, None] ** (pos[None, :] / f32(512.0))
    angle = (f32(1.0) / f32(10000.0) ** (np.arange(D // 2, dtype=f32) / f32(D // 2)))[:, None] * pos[None, :]
    sin, cos, sign = np.sin(angle), np.cos(angle), np.tile(np.array([[-1], [1]], f32), (D // 2, 1))
    pairs = lambda v: np.repeat(v, 2, axis=0)
    gamma = 1.0 - np.exp(np.linspace(np.log(1 / 32), np.log(1 / 512), NH))
    log = np.log(gamma.astype(f32).astype(np.float64))
    decays = lambda n: np.exp(log[:, None] * n)
    norm = 1.0 / np.sqrt(np.cumsum(decays(np.arange(T)), axis=1)) * DK ** -0.5
    by_head = lambda v: np.repeat(v, DK, axis=0)
    k["rot"] = np.stack([pairs(cos * scale) * by_head(norm), pairs(sin * scale) * sign * by_head(norm),
                         pairs(cos / scale), pairs(sin / scale) * sign], 1).astype(f32)
    k["edge"] = np.stack([by_head(decays(np.arange(P) + 1)), by_head(decays(P - 1 - np.arange(P)))], 1).astype(f32)
    gap = np.arange(P)[None, :] - np.arange(P)[:, None]
    k["decay"] = (np.exp(log[None, :, None] * np.maximum(gap, 0)[:, None, :]) * (gap >= 0)[:, None, :]).astype(f32)
    k["heads4"] = (np.arange(P)[:, None] // DK % 4 == np.arange(4)).astype(f32)
    k["block"] = (np.arange(P)[:, None] // DK == np.arange(EV)[None, :] // DV).astype(f32)
    k["gam"] = by_head(decays(np.array([P]))).astype(f32)
    k["rc"] = np.broadcast_to(row.astype(np.float32), (P, RC_N))
    return k


def layout(x):
    x = {key: np.asarray(v) for key, v in x.items()}
    r = {"x": x["L0_attn_x"].reshape(NT, P, D).transpose(1, 0, 2)}
    r["lnp"] = np.stack([x["L0_attn_ln_g"], x["L0_attn_ln_b"]], 1)
    halves = lambda v: v.reshape(HF, P, -1).transpose(1, 0, 2).reshape(P, -1)
    in_u, conv, packed = [], [], []
    for d in "fb":
        g = lambda name: x[f"L0_attn_{d}_{name}"]
        in_u.append(g("in_w")[:DI].T)
        conv.append(np.broadcast_to(g("conv_w").T.reshape(TAPS * DI), (P, TAPS * DI)))
        bc = g("xproj_w")[RK:].T
        packed.append(np.concatenate([
            g("in_w")[DI:].T, halves(np.concatenate([bc, bc, g("xproj_w")[:RK].T], 1)),
            np.concatenate([g("dt_w").T, g("dt_w").T]), halves(g("out_w").T), halves(g("conv_b")),
            halves(g("dt_b")), halves(g("D")), halves(g("Alog"))], 1))
    r["in_u"], r["conv_w"], r["mamba_w"] = (np.stack(v, 1) for v in (in_u, conv, packed))
    rows = lambda v: v.reshape(*v.shape[:-2], FK, P, D).swapaxes(-3, -2).reshape(*v.shape[:-2], P, FK * D)
    f = lambda name: x["L0_ffn_" + name]
    r["rw0"] = f("router_w")
    r["shared_w"] = np.concatenate([f("shared_up_w"), f("shared_gate_w"), rows(f("shared_down_w"))], 1)
    r["l0_w"] = np.concatenate([f("up_w"), f("gate_w"), rows(f("down_w"))], 2).swapaxes(0, 1)
    f = lambda name: x["L1_attn_" + name]
    w_q, w_k, w_v = np.split(f("w_qkv"), (D, 2 * D), axis=1)
    b_q, b_k, b_v = np.split(f("b_qkv"), (D, 2 * D))
    pair = np.arange(D) ^ 1
    r["wqk"] = np.concatenate([w_q, w_q[:, pair], w_k, w_k[:, pair]], 1)
    r["bqk"] = np.stack([b_q, b_q[pair], b_k, b_k[pair]], 1)
    r["wvg"], r["bvg"] = np.concatenate([w_v, f("w_g")], 1), np.concatenate([b_v, f("b_g")])
    r["wp"], r["bp"] = f("w_p").reshape(2, P, D).swapaxes(0, 1), f("b_p")
    f = lambda name: x["L1_ffn_" + name]
    r["rw1"], r["br"], r["b2"] = f("Wr").T, f("br"), f("b2")
    r["l1_w"] = np.concatenate([f("W1").swapaxes(1, 2), rows(f("W2").swapaxes(1, 2))], 2).swapaxes(0, 1)
    r["b1"] = f("b1").reshape(NE, FK, P).transpose(2, 0, 1).reshape(P, NE * FK)
    return r


def kernel(**inputs):
    import concourse.bacc as bacc
    from concourse.bass_utils import run_bass_kernel_spmd

    arrays = {name: np.ascontiguousarray(v) for name, v in {**constants(), **layout(inputs)}.items()}
    known = ({}, {})
    for _ in range(2):
        nc = bacc.Bacc("TRN2", target_bir_lowering=False, num_devices=1)
        aps = {name: nc.dram_tensor("in_" + name, v.shape, mybir.dt.from_np(v.dtype), kind="ExternalInput").ap()
               for name, v in arrays.items()}
        out = nc.dram_tensor("out", (P, NT, D), F32, kind="ExternalOutput").ap()
        known = build(nc, known, aps, out)
    r = run_bass_kernel_spmd(nc, [{"in_" + name: v for name, v in arrays.items()}], core_ids=[0])
    return r.results[0]["out"].transpose(1, 0, 2).reshape(B, T, D)
```
